# Optimizing a Trainium2 kernel written in Bass

```python
import numpy as np
import jax
import jax.numpy as jnp

def _softmax(x, axis=-1):
    return jax.nn.softmax(x, axis=axis)

def _gelu(x):
    return jax.nn.gelu(x, approximate=True)

def _silu(x):
    return jax.nn.silu(x)

def _sigmoid(x):
    return jax.nn.sigmoid(x)

def _layernorm(x, axis=-1, eps=1e-05):
    m = jnp.mean(x, axis=axis, keepdims=True)
    v = jnp.var(x, axis=axis, keepdims=True)
    return (x - m) / jnp.sqrt(v + eps)

def _scatter_add(tgt, idx, src, axis=0):
    return tgt.at[idx].add(src)

def _segment_sum(src, seg, n):
    return jax.ops.segment_sum(src, seg, n)
kernel_name = 'mk_decoder_preln_d2_seqx_r8_5e5c4a'

def setup_inputs(seed: int=0):
    np.random.seed(seed)
    _w = jnp.asarray

    def _rec_inputs():
        import jax
        import jax.numpy as jnp
        _rk = jax.random.key(seed)
        x = -7.109e-05 + 0.9999 * jax.random.normal(jax.random.fold_in(_rk, 1), (4, 256, 256), jnp.float32)
        _lenS = 256 - jax.random.randint(jax.random.fold_in(_rk, 7), (4,), 0, max(1, 256 // 4) + 1, jnp.int32)
        _lenS2 = 256 - jax.random.randint(jax.random.fold_in(_rk, 8), (4,), 0, max(1, 256 // 4) + 1, jnp.int32)
        _ctx_512P = jax.random.normal(jax.random.fold_in(_rk, 11), (4, 16, 64), jnp.float32)
        _ctx_512c = jax.random.dirichlet(jax.random.fold_in(_rk, 511), 0.3 * jnp.ones((16,), jnp.float32), (4, 256))
        _ctx_512t = jnp.einsum('bsk,bkd->bsd', _ctx_512c, _ctx_512P)
        _ctx_512t = _ctx_512t * jax.lax.rsqrt(jnp.mean(jnp.square(_ctx_512t)) + 1e-12) * 0.953939
        ctx_512 = 2.81802e-05 + 1.00001 * (_ctx_512t + 0.3 * jax.random.normal(jax.random.fold_in(_rk, 611), (4, 256, 64), jnp.float32))
        return (x, ctx_512)
    x, ctx_512 = _rec_inputs()

    def _L0_attn_setup():
        import jax, jax.numpy as jnp
        import numpy as np
        NH = 16
        D = 128
        C = 64
        EPS = 1e-12

        def _l2norm(x):
            n = jnp.linalg.norm(x, axis=-1, keepdims=True)
            return x / jnp.maximum(n, EPS)
        key = jax.random.key(seed)
        ks = jax.random.split(key, 12)
        B, L, H = (4, 512, 256)
        std = 0.02
        f32 = jnp.float32
        inp = {'hidden_states': jax.random.normal(ks[0], (B, L, H), f32), 'q_w': jax.random.normal(ks[1], (NH * D, H), f32) * std, 'q_b': jnp.zeros((NH * D,), f32), 'k_w': jax.random.normal(ks[2], (NH * D, H), f32) * std, 'k_b': jnp.zeros((NH * D,), f32), 'v_w': jax.random.normal(ks[3], (NH * D, H), f32) * std, 'v_b': jnp.zeros((NH * D,), f32), 'a_w': jax.random.normal(ks[4], (NH, H), f32) * std, 'a_b': jnp.zeros((NH,), f32), 'b_w': jax.random.normal(ks[5], (NH, H), f32) * std, 'b_b': jnp.zeros((NH,), f32), 'og_w': jax.random.normal(ks[6], (NH * D, H), f32) * std, 'o_w': jax.random.normal(ks[7], (H, NH * D), f32) * std, 'o_b': jnp.zeros((H,), f32)}
        return inp
    _L0_attn_all = _L0_attn_setup()
    _L0_attn_in = {k: v for k, v in _L0_attn_all.items() if k in ('q_w', 'q_b', 'k_w', 'k_b', 'v_w', 'v_b', 'a_w', 'a_b', 'b_w', 'b_b', 'og_w', 'o_w', 'o_b')}
    del _L0_attn_all

    def _L0_xattn_setup():
        import jax, jax.numpy as jnp
        import numpy as np
        EPS = 1e-06
        IMAGE_DIMS = 256
        key = jax.random.key(seed)
        k1, k2, k3 = jax.random.split(key, 3)
        B, I, J, D = (16, 256, 256, 64)
        p = jax.random.normal(k1, (B, I, J), dtype=jnp.float32)
        k_v = jax.random.normal(k2, (B, J, D), dtype=jnp.float32)
        W_k = jax.random.normal(k3, (D, D), dtype=jnp.float32) * (1.0 / np.sqrt(D))
        b_k = jnp.zeros((D,), dtype=jnp.float32)
        ln_gamma = jnp.ones((J,), dtype=jnp.float32)
        ln_beta = jnp.zeros((J,), dtype=jnp.float32)
        return {'p': p, 'k_v': k_v, 'W_k': W_k, 'b_k': b_k, 'ln_gamma': ln_gamma, 'ln_beta': ln_beta}
    _L0_xattn_all = _L0_xattn_setup()
    _L0_xattn_in = {k: v for k, v in _L0_xattn_all.items() if k in ('W_k', 'b_k', 'ln_gamma', 'ln_beta')}
    del _L0_xattn_all

    def _L0_ffn_setup():
        import jax, jax.numpy as jnp
        import numpy as np
        B, S, D, K, R = (4, 256, 256, 8, 64)
        key = jax.random.key(seed)
        ks = jax.random.split(key, 7)
        x = jax.random.normal(ks[0], (B, S, D), dtype=jnp.float32)
        U = jax.random.normal(ks[1], (K, D, R), dtype=jnp.float32) * 0.02
        V = jax.random.normal(ks[2], (K, R, D), dtype=jnp.float32) * 0.02
        W1 = jax.random.normal(ks[3], (D, D), dtype=jnp.float32) * 0.02
        b1 = jnp.zeros((D,), dtype=jnp.float32)
        W2 = jax.random.normal(ks[4], (D, K), dtype=jnp.float32) * 0.02
        b2 = jnp.zeros((K,), dtype=jnp.float32)
        return {'x': x, 'U': U, 'V': V, 'W1': W1, 'b1': b1, 'W2': W2, 'b2': b2}
    _L0_ffn_all = _L0_ffn_setup()
    _L0_ffn_in = {k: v for k, v in _L0_ffn_all.items() if k in ('U', 'V', 'W1', 'b1', 'W2', 'b2')}
    del _L0_ffn_all

    def _L1_attn_setup():
        import jax, jax.numpy as jnp
        import numpy as np
        B, S, D, H = (2, 256, 256, 16)
        HD = D // H
        key = jax.random.key(seed)
        ks = jax.random.split(key, 5)
        scale = 0.02
        return {'hidden_states': jax.random.normal(ks[0], (B, S, D), dtype=jnp.float32), 'Wqkv_w': jax.random.normal(ks[1], (3 * D, D), dtype=jnp.float32) * scale, 'Wqkv_b': jax.random.normal(ks[2], (3 * D,), dtype=jnp.float32) * scale, 'out_w': jax.random.normal(ks[3], (D, D), dtype=jnp.float32) * scale, 'out_b': jax.random.normal(ks[4], (D,), dtype=jnp.float32) * scale}
    _L1_attn_all = _L1_attn_setup()
    _L1_attn_in = {k: v for k, v in _L1_attn_all.items() if k in ('Wqkv_w', 'Wqkv_b', 'out_w', 'out_b')}
    del _L1_attn_all

    def _L1_xattn_setup():
        import jax, jax.numpy as jnp
        import numpy as np
        B, S, L = (2, 128, 128)
        DIM_Q, H, K, D_C, D_CQ, R = (256, 16, 128, 64, 192, 64)

        def _rope_tables(length, dim):
            inv = 1.0 / 10000.0 ** (jnp.arange(0, dim, 2, dtype=jnp.float32) / dim)
            f = jnp.arange(length, dtype=jnp.float32)[:, None] * inv[None, :]
            sin = jnp.repeat(jnp.sin(f), 2, axis=-1)
            cos = jnp.repeat(jnp.cos(f), 2, axis=-1)
            return (sin, cos)

        def _rotate_half(x):
            half = x.shape[-1] // 2
            return jnp.concatenate([-x[..., half:], x[..., :half]], axis=-1)

        def _apply_rope(x, sin, cos):
            return x * cos + _rotate_half(x) * sin
        key = jax.random.key(seed)
        ks = jax.random.split(key, 8)
        return {'hidden_q': jax.random.normal(ks[0], (B, S, DIM_Q), jnp.float32), 'kv_c': jax.random.normal(ks[1], (B, L, D_C), jnp.float32), 'Wq': jax.random.normal(ks[2], (H * K, DIM_Q), jnp.float32) / np.sqrt(DIM_Q).astype(np.float32), 'w_kc_q': jax.random.normal(ks[3], (H, K, D_CQ), jnp.float32) / np.sqrt(K).astype(np.float32), 'w_kc_kv': jax.random.normal(ks[4], (H, K, D_C), jnp.float32) / np.sqrt(K).astype(np.float32), 'W_qr': jax.random.normal(ks[5], (H, D_CQ, R), jnp.float32) / np.float32(np.sqrt(D_CQ) * np.sqrt(R)), 'W_kr': jax.random.normal(ks[6], (H, D_C, R), jnp.float32) / np.sqrt(D_C).astype(np.float32), 'Wo': jax.random.normal(ks[7], (DIM_Q, H * K), jnp.float32) / np.sqrt(H * K).astype(np.float32)}
    _L1_xattn_all = _L1_xattn_setup()
    _L1_xattn_in = {k: v for k, v in _L1_xattn_all.items() if k in ('Wq', 'w_kc_q', 'w_kc_kv', 'W_qr', 'W_kr', 'Wo')}
    del _L1_xattn_all

    def _L1_ffn_setup():
        import jax, jax.numpy as jnp
        import numpy as np
        H = 256
        E = 8
        TOPK = 2
        I_MOE = 128
        I_SH = 512

        def _silu_and_mul(gu):
            g, u = jnp.split(gu, 2, axis=-1)
            return jax.nn.silu(g) * u
        key = jax.random.key(seed)
        ks = jax.random.split(key, 6)
        s = lambda *sh: 1.0 / np.sqrt(sh[-2])
        hidden_states = jax.random.normal(ks[0], (2, 128, H), dtype=jnp.float32)
        w_gate = jax.random.normal(ks[1], (H, E), dtype=jnp.float32) * (1.0 / np.sqrt(H))
        w_gate_up = jax.random.normal(ks[2], (E, H, 2 * I_MOE), dtype=jnp.float32) * (1.0 / np.sqrt(H))
        w_down = jax.random.normal(ks[3], (E, I_MOE, H), dtype=jnp.float32) * (1.0 / np.sqrt(I_MOE))
        w_sh_gate_up = jax.random.normal(ks[4], (H, 2 * I_SH), dtype=jnp.float32) * (1.0 / np.sqrt(H))
        w_sh_down = jax.random.normal(ks[5], (I_SH, H), dtype=jnp.float32) * (1.0 / np.sqrt(I_SH))
        return {'hidden_states': hidden_states, 'w_gate': w_gate, 'w_gate_up': w_gate_up, 'w_down': w_down, 'w_sh_gate_up': w_sh_gate_up, 'w_sh_down': w_sh_down}
    _L1_ffn_all = _L1_ffn_setup()
    _L1_ffn_in = {k: v for k, v in _L1_ffn_all.items() if k in ('w_gate', 'w_gate_up', 'w_down', 'w_sh_gate_up', 'w_sh_down')}
    del _L1_ffn_all
    return {'x': x, 'ctx_512': ctx_512, 'L0_attn_q_w': _L0_attn_in['q_w'], 'L0_attn_q_b': _L0_attn_in['q_b'], 'L0_attn_k_w': _L0_attn_in['k_w'], 'L0_attn_k_b': _L0_attn_in['k_b'], 'L0_attn_v_w': _L0_attn_in['v_w'], 'L0_attn_v_b': _L0_attn_in['v_b'], 'L0_attn_a_w': _L0_attn_in['a_w'], 'L0_attn_a_b': _L0_attn_in['a_b'], 'L0_attn_b_w': _L0_attn_in['b_w'], 'L0_attn_b_b': _L0_attn_in['b_b'], 'L0_attn_og_w': _L0_attn_in['og_w'], 'L0_attn_o_w': _L0_attn_in['o_w'], 'L0_attn_o_b': _L0_attn_in['o_b'], 'L0_xattn_W_k': _L0_xattn_in['W_k'], 'L0_xattn_b_k': _L0_xattn_in['b_k'], 'L0_xattn_ln_gamma': _L0_xattn_in['ln_gamma'], 'L0_xattn_ln_beta': _L0_xattn_in['ln_beta'], 'L0_ffn_U': _L0_ffn_in['U'], 'L0_ffn_V': _L0_ffn_in['V'], 'L0_ffn_W1': _L0_ffn_in['W1'], 'L0_ffn_b1': _L0_ffn_in['b1'], 'L0_ffn_W2': _L0_ffn_in['W2'], 'L0_ffn_b2': _L0_ffn_in['b2'], 'L1_attn_Wqkv_w': _L1_attn_in['Wqkv_w'], 'L1_attn_Wqkv_b': _L1_attn_in['Wqkv_b'], 'L1_attn_out_w': _L1_attn_in['out_w'], 'L1_attn_out_b': _L1_attn_in['out_b'], 'L1_xattn_Wq': _L1_xattn_in['Wq'], 'L1_xattn_w_kc_q': _L1_xattn_in['w_kc_q'], 'L1_xattn_w_kc_kv': _L1_xattn_in['w_kc_kv'], 'L1_xattn_W_qr': _L1_xattn_in['W_qr'], 'L1_xattn_W_kr': _L1_xattn_in['W_kr'], 'L1_xattn_Wo': _L1_xattn_in['Wo'], 'L1_ffn_w_gate': _L1_ffn_in['w_gate'], 'L1_ffn_w_gate_up': _L1_ffn_in['w_gate_up'], 'L1_ffn_w_down': _L1_ffn_in['w_down'], 'L1_ffn_w_sh_gate_up': _L1_ffn_in['w_sh_gate_up'], 'L1_ffn_w_sh_down': _L1_ffn_in['w_sh_down']}

def reference(x, ctx_512, L0_attn_q_w, L0_attn_q_b, L0_attn_k_w, L0_attn_k_b, L0_attn_v_w, L0_attn_v_b, L0_attn_a_w, L0_attn_a_b, L0_attn_b_w, L0_attn_b_b, L0_attn_og_w, L0_attn_o_w, L0_attn_o_b, L0_xattn_W_k, L0_xattn_b_k, L0_xattn_ln_gamma, L0_xattn_ln_beta, L0_ffn_U, L0_ffn_V, L0_ffn_W1, L0_ffn_b1, L0_ffn_W2, L0_ffn_b2, L1_attn_Wqkv_w, L1_attn_Wqkv_b, L1_attn_out_w, L1_attn_out_b, L1_xattn_Wq, L1_xattn_w_kc_q, L1_xattn_w_kc_kv, L1_xattn_W_qr, L1_xattn_W_kr, L1_xattn_Wo, L1_ffn_w_gate, L1_ffn_w_gate_up, L1_ffn_w_down, L1_ffn_w_sh_gate_up, L1_ffn_w_sh_down):
    import jax
    import jax.numpy as jnp

    def _L0_attn_ref(hidden_states, q_w, q_b, k_w, k_b, v_w, v_b, a_w, a_b, b_w, b_b, og_w, o_w, o_b):
        import jax, jax.numpy as jnp
        import numpy as np
        NH = 16
        D = 128
        C = 64
        EPS = 1e-12

        def _l2norm(x):
            n = jnp.linalg.norm(x, axis=-1, keepdims=True)
            return x / jnp.maximum(n, EPS)
        B, L, H = hidden_states.shape
        nh, d, c = (NH, D, C)
        hs = hidden_states
        q = (hs @ q_w.T + q_b).reshape(B, L, nh, d)
        k = (hs @ k_w.T + k_b).reshape(B, L, nh, d)
        v = (hs @ v_w.T + v_b).reshape(B, L, nh, d)
        beta = jax.nn.softplus(hs @ b_w.T + b_b)
        scale = float(d) ** 0.5
        qn = _l2norm(q / scale)
        kn = _l2norm(k / scale)
        gv = beta[..., None] * v
        nchunks = L // c

        def to_chunks(x):
            return x.reshape(B, nchunks, c, nh, d).transpose(0, 1, 3, 2, 4)
        qc, kc, gvc = (to_chunks(qn), to_chunks(kn), to_chunks(gv))
        attn = jnp.einsum('bnhid,bnhjd->bnhij', qc, kc)
        pos = jnp.arange(c, dtype=jnp.float32)
        dist = jnp.clip(pos[None, :] - pos[:, None], 0.0, None)
        decay = jnp.exp(-0.1 * dist)
        causal = pos[None, :] <= pos[:, None]
        mask = jnp.where(causal, decay, 0.0)
        out = jnp.einsum('bnhij,bnhjd->bnhid', attn * mask, gvc)
        out = out.transpose(0, 1, 3, 2, 4).reshape(B, L, nh * d)
        gate = jax.nn.silu(hs @ og_w.T)
        out = out * gate
        return out @ o_w.T + o_b

    def _L0_xattn_ref(p, k_v, W_k, b_k, ln_gamma, ln_beta):
        import jax, jax.numpy as jnp
        import numpy as np
        EPS = 1e-06
        IMAGE_DIMS = 256
        kv = k_v @ W_k.T + b_k
        out = jnp.einsum('bij,bjd->bid', p, kv)
        scale = IMAGE_DIMS ** (-0.5)
        sim = jnp.einsum('bid,bjd->bij', out, kv) * scale
        mu = jnp.mean(sim, axis=-1, keepdims=True)
        var = jnp.var(sim, axis=-1, keepdims=True)
        sim = (sim - mu) * jax.lax.rsqrt(var + EPS) * ln_gamma + ln_beta
        attn = jax.nn.softmax(sim, axis=-1)
        return attn

    def _L0_ffn_ref(x, U, V, W1, b1, W2, b2):
        import jax, jax.numpy as jnp
        import numpy as np
        B, S, D, K, R = (4, 256, 256, 8, 64)
        h = jax.nn.relu(jnp.einsum('bsd,de->bse', x, W1) + b1)
        alpha = jax.nn.softmax(jnp.einsum('bse,ek->bsk', h, W2) + b2, axis=-1)
        vx = jnp.einsum('krd,bsd->bskr', V, x)
        uvx = jnp.einsum('kdr,bskr->bskd', U, vx)
        out = jnp.einsum('bsk,bskd->bsd', alpha, uvx)
        return out

    def _L1_attn_ref(hidden_states, Wqkv_w, Wqkv_b, out_w, out_b):
        import jax, jax.numpy as jnp
        import numpy as np
        B, S, D, H = (2, 256, 256, 16)
        HD = D // H
        b, s, d = hidden_states.shape
        qkv = hidden_states @ Wqkv_w.T + Wqkv_b
        qkv = qkv.reshape(b, s, 3, H, HD)
        q, k, v = (qkv[:, :, 0], qkv[:, :, 1], qkv[:, :, 2])
        softmax_scale = 1.0 / np.float32(np.sqrt(HD))
        scores = jnp.einsum('bthd,bshd->bhts', q, k) * softmax_scale
        attn = jax.nn.softmax(scores, axis=-1)
        ctx = jnp.einsum('bhts,bshd->bthd', attn, v)
        ctx = ctx.reshape(b, s, d)
        return ctx @ out_w.T + out_b

    def _L1_xattn_ref(hidden_q, kv_c, Wq, w_kc_q, w_kc_kv, W_qr, W_kr, Wo):
        import jax, jax.numpy as jnp
        import numpy as np
        B, S, L = (2, 128, 128)
        DIM_Q, H, K, D_C, D_CQ, R = (256, 16, 128, 64, 192, 64)

        def _rope_tables(length, dim):
            inv = 1.0 / 10000.0 ** (jnp.arange(0, dim, 2, dtype=jnp.float32) / dim)
            f = jnp.arange(length, dtype=jnp.float32)[:, None] * inv[None, :]
            sin = jnp.repeat(jnp.sin(f), 2, axis=-1)
            cos = jnp.repeat(jnp.cos(f), 2, axis=-1)
            return (sin, cos)

        def _rotate_half(x):
            half = x.shape[-1] // 2
            return jnp.concatenate([-x[..., half:], x[..., :half]], axis=-1)

        def _apply_rope(x, sin, cos):
            return x * cos + _rotate_half(x) * sin
        Bv, Sv, _ = hidden_q.shape
        _, Lv, _ = kv_c.shape
        q_hk = (hidden_q @ Wq.T).reshape(Bv, Sv, H, K)
        q_big = jnp.einsum('bshk,hkq->bshq', q_hk, w_kc_q)
        sin_q, cos_q = _rope_tables(Sv, D_CQ)
        q_big = _apply_rope(q_big, sin_q[None, :, None, :], cos_q[None, :, None, :])
        sin_k, cos_k = _rope_tables(Lv, D_C)
        kv_r = _apply_rope(kv_c, sin_k[None], cos_k[None])
        q_r = jnp.einsum('bshq,hqr->bhsr', q_big, W_qr)
        k_r = jnp.einsum('bld,hdr->bhlr', kv_r, W_kr)
        scores = jnp.einsum('bhsr,bhlr->bhsl', q_r, k_r)
        attn = jax.nn.softmax(scores, axis=-1)
        ctx_c = jnp.einsum('bhsl,bld->bhsd', attn, kv_r)
        ctx_lat = jnp.einsum('bhsd,hkd->bhsk', ctx_c, w_kc_kv)
        ctx = ctx_lat.transpose(0, 2, 1, 3).reshape(Bv, Sv, H * K)
        return ctx @ Wo.T

    def _L1_ffn_ref(hidden_states, w_gate, w_gate_up, w_down, w_sh_gate_up, w_sh_down):
        import jax, jax.numpy as jnp
        import numpy as np
        H = 256
        E = 8
        TOPK = 2
        I_MOE = 128
        I_SH = 512

        def _silu_and_mul(gu):
            g, u = jnp.split(gu, 2, axis=-1)
            return jax.nn.silu(g) * u
        orig_shape = hidden_states.shape
        x = hidden_states.reshape(-1, orig_shape[-1])
        router_logits = x @ w_gate
        probs = jax.nn.softmax(router_logits, axis=-1)
        topk_w, topk_ids = jax.lax.top_k(probs, TOPK)
        topk_w = topk_w / jnp.sum(topk_w, axis=-1, keepdims=True)
        combine = jnp.sum(topk_w[..., None] * jax.nn.one_hot(topk_ids, E, dtype=x.dtype), axis=1)
        gu = jnp.einsum('th,ehf->etf', x, w_gate_up)
        act = _silu_and_mul(gu)
        eo = jnp.einsum('eti,eih->eth', act, w_down)
        routed = jnp.einsum('te,eth->th', combine, eo)
        shared = _silu_and_mul(x @ w_sh_gate_up) @ w_sh_down
        return (routed + shared).reshape(orig_shape)
    x = x + _L0_attn_ref(_layernorm(x, axis=-1), L0_attn_q_w, L0_attn_q_b, L0_attn_k_w, L0_attn_k_b, L0_attn_v_w, L0_attn_v_b, L0_attn_a_w, L0_attn_a_b, L0_attn_b_w, L0_attn_b_b, L0_attn_og_w, L0_attn_o_w, L0_attn_o_b)
    x = x + _L0_xattn_ref(_layernorm(x, axis=-1), ctx_512, L0_xattn_W_k, L0_xattn_b_k, L0_xattn_ln_gamma, L0_xattn_ln_beta)
    x = x + _L0_ffn_ref(_layernorm(x, axis=-1), L0_ffn_U, L0_ffn_V, L0_ffn_W1, L0_ffn_b1, L0_ffn_W2, L0_ffn_b2)
    x = x + _L1_attn_ref(_layernorm(x, axis=-1), L1_attn_Wqkv_w, L1_attn_Wqkv_b, L1_attn_out_w, L1_attn_out_b)
    x = x + _L1_xattn_ref(_layernorm(x, axis=-1), ctx_512, L1_xattn_Wq, L1_xattn_w_kc_q, L1_xattn_w_kc_kv, L1_xattn_W_qr, L1_xattn_W_kr, L1_xattn_Wo)
    x = x + _L1_ffn_ref(_layernorm(x, axis=-1), L1_ffn_w_gate, L1_ffn_w_gate_up, L1_ffn_w_down, L1_ffn_w_sh_gate_up, L1_ffn_w_sh_down)
    return x

_drawn_inputs = setup_inputs


def setup_inputs(seed=0):
    import zlib

    import numpy as np

    out = dict(_drawn_inputs(seed))
    spreads = {'L0_attn_q_b': (0.0, 0.282),
     'L0_attn_k_b': (0.0, 0.282),
     'L0_attn_v_b': (0.0, 0.1),
     'L0_attn_a_b': (0.0, 0.1),
     'L0_attn_b_b': (0.0, 2.0),
     'L0_attn_o_b': (0.0, 0.1),
     'L0_xattn_b_k': (0.0, 2.0),
     'L0_xattn_ln_gamma': (1.0, 0.6),
     'L0_xattn_ln_beta': (0.0, 2.0),
     'L0_ffn_b1': (0.0, 0.676),
     'L0_ffn_b2': (0.0, 2.0)}
    factors = {'L0_attn_b_w': 4.298,
     'L0_xattn_W_k': 3.185,
     'L0_ffn_W1': 8.0,
     'L0_ffn_W2': 8.0,
     'L1_attn_Wqkv_b': 3.027}
    for name, (base, spread) in spreads.items():
        noise = np.random.default_rng([zlib.crc32(name.encode()), seed]).standard_normal(out[name].shape)
        drawn = base * np.exp(spread * noise) if base else spread * noise
        out[name] = jnp.asarray(drawn.astype(out[name].dtype))
    for name, factor in factors.items():
        out[name] = (out[name] * factor).astype(out[name].dtype)
    return out
```

```python
from contextlib import ExitStack, contextmanager

import concourse.bass as bass
from concourse import mybir

F32 = mybir.dt.float32
ALU = mybir.AluOpType
ACT = mybir.ActivationFunctionType
AX_X = mybir.AxisListType.X
ds = bass.ds

P = 128
B, S, D = 4, 256, 256
T = B * S
NT = T // P
KT = D // P
TB = S // P
LN_EPS = 1e-5

H0, D0, CHUNK = 16, 128, 64
NORM_FLOOR = (1e-12 ** 2) * D0

XC = 64
X0_EPS = 1e-6
X0_SCALE = 256 ** -0.5

FK, FR = 8, 64
FM = FK * FR // P

H1, D1 = 16, 16
V1 = D1 + 1

H2, K2, Q2, R2 = 16, 128, 192, 64
QH = Q2 // 2
C2 = XC + 1

E6, I6, SH6 = 8, 128, 512
SF = SH6 // P


class Chain:

    def __init__(self, eng, sem):
        self.eng, self.sem, self.n, self.loop = eng, sem, 0, None

    def value(self):
        if self.loop is None:
            return self.n
        i, first, start, per = self.loop
        return (i - first) * per + self.n

    def __call__(self, ins):
        ins.then_inc(self.sem, 1)
        self.n += 1
        self.eng.wait_ge(self.sem, self.value())

    @contextmanager
    def over(self, i, first, last, per):
        start = self.n
        self.loop = (i, first, start, per)
        yield
        assert self.n == start + per, (self.n - start, per)
        self.n = start + per * (last - first)
        self.loop = None


def lay_out(np, g):
    def tiles(w):
        return w.reshape(-1, P, w.shape[1]).transpose(1, 0, 2)

    heads = np.stack([g[f"L0_attn_{n}_w"].reshape(H0, D0, KT, P).transpose(0, 3, 2, 1)
                      for n in ("q", "k", "v", "og")], axis=3)
    return {
        "x": g["x"],
        "w_head": np.concatenate([heads.reshape(H0, P, KT * 4 * D0), g["L0_attn_q_b"].reshape(H0, D0, 1),
                                  g["L0_attn_k_b"].reshape(H0, D0, 1)], axis=2),
        "o_w": g["L0_attn_o_w"].reshape(D, H0, D0).transpose(2, 1, 0),
        "vb": g["L0_attn_v_b"],
        "b_w": tiles(g["L0_attn_b_w"].T),
        "bb": g["L0_attn_b_b"],
        "ob": g["L0_attn_o_b"],
        "ctx": g["ctx_512"].reshape(NT, P, XC).transpose(1, 0, 2),
        "ctxT": g["ctx_512"].reshape(T, XC).T,
        "wk_T": g["L0_xattn_W_k"].T,
        "bk": g["L0_xattn_b_k"].reshape(XC, 1),
        "gam": g["L0_xattn_ln_gamma"],
        "bet": g["L0_xattn_ln_beta"],
        "f_w1": tiles(g["L0_ffn_W1"]),
        "f_b1": g["L0_ffn_b1"].reshape(KT, P).T,
        "f_w2": tiles(g["L0_ffn_W2"]),
        "f_b2": g["L0_ffn_b2"],
        "f_v": tiles(g["L0_ffn_V"].reshape(FK * FR, D).T),
        "f_u": tiles(g["L0_ffn_U"].transpose(0, 2, 1).reshape(FK * FR, D)),
        "a_w": tiles(g["L1_attn_Wqkv_w"].T),
        "a_b": g["L1_attn_Wqkv_b"].reshape(6, P).T,
        "a_ow": tiles(g["L1_attn_out_w"].T),
        "aob": g["L1_attn_out_b"],
        "w5": np.concatenate([g["L1_xattn_Wq"].reshape(H2, K2, KT, P).transpose(0, 3, 2, 1).reshape(H2, P, KT * K2),
                              g["L1_xattn_w_kc_q"]], axis=2),
        "qr_T": g["L1_xattn_W_qr"].transpose(2, 0, 1),
        "kr_T": g["L1_xattn_W_kr"].transpose(2, 0, 1),
        "kc_kv": g["L1_xattn_w_kc_kv"].transpose(1, 0, 2),
        "wo_T": g["L1_xattn_Wo"].reshape(D, H2, K2).transpose(2, 1, 0),
        "e_gate": tiles(g["L1_ffn_w_gate"]),
        "e_gu": g["L1_ffn_w_gate_up"].reshape(E6, KT, P, 2 * I6).transpose(2, 1, 0, 3),
        "e_sgu": tiles(g["L1_ffn_w_sh_gate_up"]),
        "e_dn": g["L1_ffn_w_down"].transpose(1, 0, 2),
        "e_sdn": tiles(g["L1_ffn_w_sh_down"]),
    }


def constants(np):
    i = np.arange(P)
    same = (i[:, None] // CHUNK == i[None, :] // CHUNK) & (i[:, None] <= i[None, :])
    def tables(length, dim):
        inv = np.float32(1.0) / np.float32(10000.0) ** (np.arange(0, dim, 2, dtype=np.float32) / np.float32(dim))
        f = np.arange(length, dtype=np.float32)[:, None] * inv[None, :]
        return np.repeat(np.sin(f), 2, axis=-1), np.repeat(np.cos(f), 2, axis=-1)

    sin_k, cos_k = tables(S, XC)
    sin_k[:, 0:XC // 2] *= -1
    sin_q, cos_q = tables(S, Q2)
    rows = np.arange(P) % 32 // 16
    pick = (np.arange(P)[None, None, :] // FR + 2 * np.arange(FM)[None, :, None] == np.arange(FK)[:, None, None])
    return {
        "cos_k": cos_k.reshape(TB, P, XC).transpose(1, 0, 2),
        "sin_k": sin_k.reshape(TB, P, XC).transpose(1, 0, 2),
        "cos_q": cos_q.T.reshape(2, QH, S).transpose(1, 0, 2),
        "sin_q": sin_q.T.reshape(2, QH, S).transpose(1, 0, 2),
        "f_sel": pick.astype(np.float32),
        "a_par": np.stack([rows == 0, rows == 1], axis=1).astype(np.float32),
        "e_rev": np.arange(E6, 0, -1).astype(np.float32),
        "ident": np.eye(P, dtype=np.float32),
        "mask": (0.5 * same).astype(np.float32),
    }


def decoder(nc, a, out):
    ctx = ExitStack()
    with ctx:
        def sb(name, shape, dt=F32):
            return ctx.enter_context(nc.sbuf_tensor(name, shape, dt))

        def sem(name):
            return ctx.enter_context(nc.semaphore(name))

        bank = [ctx.enter_context(nc.psum_tensor(f"bank{n}", [P, 512], F32)) for n in range(8)]

        X = sb("X", [P, NT, D])
        HN = sb("HN", [P, NT, D])
        HT = sb("HT", [P, KT, T])
        ident = sb("ident", [P, P])
        ones = sb("ones", [P, 1])
        ln_stat = sb("ln_stat", [P, NT, 6])
        ln_mv = sb("ln_mv", [P, NT, 2])
        ln_var = sb("ln_var", [P, NT])
        ln_r = sb("ln_r", [P, NT])
        ln_t = sb("ln_t", [P, NT])
        ln_rstd = sb("ln_rstd", [P, NT])
        ln_none = sb("ln_none", [P, 1])
        half = sb("half", [P, 2 * NT])
        big = sb("big", [P, 16384])
        work = sb("work", [P, 9216])

        w_slot = sb("w_slot", [P, 2, KT * 4 * D0 + 2])
        o_w = sb("o_w", [P, H0, D])
        vb_row = sb("vb_row", [P, H0 * D0])
        b_w = sb("b_w", [P, KT, H0])
        bb_row = sb("bb_row", [P, H0])
        ob_row = sb("ob_row", [P, D])
        mask = sb("mask", [P, P])
        beta = sb("beta", [P, NT, H0])
        bt = work[:, 4 * T:4 * T + 6 * NT * H0].rearrange("p (n c) -> p n c", n=6)
        norm = sb("norm", [P, 4, 2 * NT])
        w_head = w_slot[:, :, 0:KT * 4 * D0].rearrange("p j (k c) -> p j k c", k=KT)
        qk_bias = w_slot[:, :, KT * 4 * D0:]
        outT = big[:, :].rearrange("p (h t) -> p h t", h=H0)
        qT = work[:, 0:T]
        kT = work[:, T:2 * T]
        q2 = work[:, 2 * T:3 * T]
        k2 = work[:, 3 * T:4 * T]
        attn = work[:, 4 * T:5 * T].rearrange("p (t i) -> p t i", t=NT)
        v_tok = work[:, 5 * T:6 * T].rearrange("p (t d) -> p t d", t=NT)
        gate = work[:, 6 * T:7 * T].rearrange("p (t d) -> p t d", t=NT)
        gated = work[:, 7 * T:8 * T].rearrange("p (t d) -> p t d", t=NT)
        tanh_g = work[:, 8 * T:8 * T + 512].rearrange("p (n t d) -> p n t d", n=2, t=2)
        QK = bank[0:2]
        VG = [b[:, :].rearrange("p (t c) -> p t c", t=2) for b in bank[2:4]]
        SC = [b[:, :].rearrange("p (t i) -> p t i", t=4) for b in bank[4:6]]
        OV = [b[:, :].rearrange("p (t d) -> p t d", t=4) for b in bank[6:8]]
        sumsq = bank[2][:, 0:2 * NT]
        PRB = bank[4][:, 0:NT * H0]


        ctx_tok = work[:, 3 * T:3 * T + NT * XC].rearrange("p (t c) -> p t c", t=NT)
        ctxT = work[0:XC, 2 * T:3 * T]
        wk_T = sb("wk_T", [XC, XC])
        bk_col = sb("bk_col", [XC, 1])
        bk_row = sb("bk_row", [P, XC])
        kvT = sb("kvT", [XC, T])
        kv = sb("kv", [P, NT, XC])
        cos_k = work[:, 0:2 * XC].rearrange("p (t c) -> p t c", t=TB)
        sin_k = work[:, 2 * XC:4 * XC].rearrange("p (t c) -> p t c", t=TB)
        rot_k = work[:, 4 * XC:4 * XC + NT * XC].rearrange("p (t c) -> p t c", t=NT)
        lat2 = work[:, T:2 * T].rearrange("p (t c) -> p t c", t=NT)
        lat = sb("lat", [P, NT, C2])
        latT = sb("latT", [P, T])

        gam_row = sb("gam_row", [P, S])
        bet_row = sb("bet_row", [P, S])
        x_sim = work[:, 0:1024].rearrange("p (n t j) -> p n t j", n=2, t=TB)
        x_e = work[:, 1024:2048].rearrange("p (n t j) -> p n t j", n=2, t=TB)
        x_oT = work[0:XC, 2048:2560].rearrange("p (n i) -> p n i", n=2)
        x_stat = sb("x_stat", [P, TB, 6])
        x_mv = sb("x_mv", [P, TB, 2])
        x_v = sb("x_v", [P, 4, TB])
        x_nm = sb("x_nm", [P, 2, TB])
        x_sum = sb("x_sum", [P, 2, TB])
        x_rc = sb("x_rc", [P, TB])
        XO = bank[2:4]
        XS = [b[:, :].rearrange("p (t j) -> p t j", t=TB) for b in bank[4:6]]

        f_w1 = sb("f_w1", [P, KT, D])
        f_b1 = sb("f_b1", [P, KT])
        f_w2 = sb("f_w2", [P, KT, FK])
        f_b2 = sb("f_b2", [P, FK])
        f_wvu = sb("f_wvu", [P, 2048])
        f_v = f_wvu[:, 0:1024].rearrange("p (k c) -> p k c", k=KT)
        f_u = f_wvu[:, 1024:2048].rearrange("p (m d) -> p m d", m=FM)
        f_sel = sb("f_sel", [FK, FM, P])
        f_h = work[:, 2560:3072].rearrange("p (m t) -> p m t", m=KT)
        f_vx = work[:, 3072:4096].rearrange("p (m t) -> p m t", m=FM)
        f_ax = work[:, 4096:5120].rearrange("p (m t) -> p m t", m=FM)
        f_aT = work[0:FK, 5120:5376]
        f_al = sb("f_al", [P, 4, TB, FK])
        f_st = sb("f_st", [P, 3, TB])
        FH = bank[0][:, :].rearrange("p (m t) -> p m t", m=KT)
        FL = bank[1][:, 0:TB * FK].rearrange("p (t k) -> p t k", t=TB)
        FT = bank[1][0:FK, 0:S]
        FA = [b[:, :].rearrange("p (m t) -> p m t", m=2) for b in bank[2:4]]
        FX = [b[:, :].rearrange("p (m t) -> p m t", m=2) for b in bank[4:6]]
        FO = bank[6][:, :].rearrange("p (t d) -> p t d", t=TB)

        wo_T = o_w[:, :, :]
        kc_kv = big[:, 8192:8192 + H2 * XC].rearrange("p (h c) -> p h c", h=H2)
        qr_T = big[0:R2, 9216:9216 + H2 * Q2].rearrange("p (h q) -> p h q", h=H2)
        kr_T = big[0:R2, 12288:12288 + H2 * XC].rearrange("p (h c) -> p h c", h=H2)
        Gw = sb("Gw", [QH, 2, H2, XC])
        Mw = f_wvu[:, :].rearrange("p (m d) -> p m d", m=H2 // 2)

        a_w = sb("a_w", [P, KT, 3 * D])
        a_b = sb("a_b", [P, 6])
        a_bs = sb("a_bs", [P, 6])
        a_par = sb("a_par", [P, 2])
        a_ow = sb("a_ow", [P, KT, D])
        aob_row = sb("aob_row", [P, D])
        a_q = work[:, 0:512].rearrange("p (m t) -> p m t", m=KT)
        a_k = work[:, 512:1536].rearrange("p (o m t) -> p o m t", o=2, m=KT)
        a_vT = work[:, 1536:2048].rearrange("p (m t) -> p m t", m=KT)
        a_v = work[:, 2048:2048 + TB * H1 * V1].rearrange("p (t h c) -> p t h c", t=TB, h=H1)
        a_p = work[:, 2600:3624].rearrange("p (n t s) -> p n t s", n=2, t=TB)
        a_pT = work[:, 3624:4648].rearrange("p (n c t) -> p n c t", n=2, c=4)
        a_cn = work[:, 4648:5160].rearrange("p (t c) -> p t c", t=TB)
        a_cT = work[:, 5376:5888].rearrange("p (c t) -> p c t", c=4)
        a_nm = sb("a_nm", [P, 2, TB])
        a_rc = sb("a_rc", [P, TB, H1])
        AS = [b[:, :].rearrange("p (t s) -> p t s", t=TB) for b in bank[2:4]]
        AT = [b[:, :].rearrange("p (c t) -> p c t", c=4) for b in bank[4:6]]
        AV = [b[:, 0:H1 * V1].rearrange("p (h c) -> p h c", h=H1) for b in bank[6:8]]
        AB = [b[:, :].rearrange("p (m t) -> p m t", m=KT) for b in bank[0:2]]

        w5 = w_slot
        cos_q = vb_row[0:QH, 1024:1536].rearrange("p (o s) -> p o s", o=2)
        sin_q = vb_row[0:QH, 1536:2048].rearrange("p (o s) -> p o s", o=2)
        l_q = work[:, 0:1024]
        l_rot = work[0:QH, 1024:3072].rearrange("p (o t) -> p o t", o=2)
        l_pr = work[0:QH, 3072:5120].rearrange("p (n t) -> p n t", n=4)
        l_u = work[:, 5120:6144].rearrange("p (t c) -> p t c", t=NT)
        l_uT = work[:, 6144:7168]
        l_p = work[:, 7168:7680].rearrange("p (t l) -> p t l", t=TB)
        l_pT = work[:, 7680:8192].rearrange("p (c t) -> p c t", c=4)
        l_cT = work[:, 0:2048].rearrange("p (n m t) -> p n m t", n=2, m=8)
        l_cn = big[:, 8192:16384].rearrange("p (t c) -> p t c", t=NT)
        l_nm = sb("l_nm", [P, 2, TB])
        l_rc = sb("l_rc", [P, TB])
        LR = bank[2:4]
        LU = bank[4][:, :].rearrange("p (t c) -> p t c", t=NT)
        LS = bank[5][:, :].rearrange("p (t l) -> p t l", t=TB)
        LT = bank[6][:, :].rearrange("p (c t) -> p c t", c=4)
        LV = bank[7][:, 0:TB * C2].rearrange("p (t c) -> p t c", t=TB)

        e_gate = sb("e_gate", [P, KT, E6])
        e_rev = sb("e_rev", [P, E6])
        e_gu = big[:, 0:4096].rearrange("p (k e f) -> p k e f", k=KT, e=E6)
        e_sgu = big[:, 4096:6144].rearrange("p (k f) -> p k f", k=KT)
        e_dn = big[:, 6144:8192].rearrange("p (e d) -> p e d", e=E6)
        e_sdn = vb_row[:, 0:1024].rearrange("p (f d) -> p f d", f=SF)
        e_r = work[:, 4096:4096 + 6 * NT * E6].rearrange("p (n t e) -> p n t e", n=6, t=NT)
        e_s = sb("e_s", [P, 6, NT])
        e_comb = sb("e_comb", [P, NT, E6])
        e_th = work[:, 2048:2560].rearrange("p (n t) -> p n t", n=2)
        e_sg = work[:, 2560:3072].rearrange("p (n t) -> p n t", n=2)
        e_act = work[:, 3072:3584].rearrange("p (n t) -> p n t", n=2)
        EG = [b[:, :].rearrange("p (g t) -> p g t", g=2) for b in bank[0:2]]
        EY = [b[:, :].rearrange("p (t d) -> p t d", t=TB) for b in bank[2:4]]
        ES = bank[4:6]
        EL = bank[6][:, 0:NT * E6].rearrange("p (t e) -> p t e", t=NT)

        ld_x = [sem(f"ld_x{b}") for b in range(B)]
        ld_c = sem("ld_c")
        ld_1 = sem("ld_1")
        ld_w = [sem(f"ld_w{j}") for j in range(2)]
        ld_o = sem("ld_o")
        dve = sem("dve")
        act_own = sem("act_own")
        pool_own = sem("pool_own")
        consts = sem("consts")
        ln_ve = sem("ln_ve")
        ln_pw = sem("ln_pw")
        ln_h = sem("ln_h")
        ln_tr = sem("ln_tr")
        ln_ht = sem("ln_ht")
        x_bias = sem("x_bias")
        bt_mm = sem("bt_mm")
        bt_abs = sem("bt_abs")
        bt_exp = sem("bt_exp")
        bt_w = sem("bt_w")
        bt_ln = sem("bt_ln")
        qk_mm = sem("qk_mm")
        qk_read = sem("qk_read")
        vg_mm = sem("vg_mm")
        tanh_done = sem("tanh_done")
        vg_read = sem("vg_read")
        ss_mm = sem("ss_mm")
        ss_read = sem("ss_read")
        ss_pow = sem("ss_pow")
        sc_mm = sem("sc_mm")
        masked = sem("masked")
        pv_mm = sem("pv_mm")
        gated_ok = sem("gated_ok")
        tr_mm = sem("tr_mm")
        outT_ok = sem("outT_ok")
        o_mm = sem("o_mm")
        o_read = sem("o_read")
        ld_cx = sem("ld_cx")
        ld_2 = sem("ld_2")
        ld_3 = sem("ld_3")
        ld_4 = sem("ld_4")
        ld_p = sem("ld_p")
        ld_t = sem("ld_t")
        ld_6 = sem("ld_6")
        ld_7 = sem("ld_7")
        kvt_mm = sem("kvt_mm")
        kvt_ok = sem("kvt_ok")
        kvn_mm = sem("kvn_mm")
        kvn_ok = sem("kvn_ok")
        lat_ok = sem("lat_ok")
        lat_mm = sem("lat_mm")
        latT_ok = sem("latT_ok")
        xo_mm = sem("xo_mm")
        xo_ok = sem("xo_ok")
        xs_mm = sem("xs_mm")
        xs_ve = sem("xs_ve")
        xs_pw = sem("xs_pw")
        xs_nm = sem("xs_nm")
        xs_exp = sem("xs_exp")
        xs_free = sem("xs_free")
        fh_mm = sem("fh_mm")
        fh_ok = sem("fh_ok")
        fx_mm = sem("fx_mm")
        fx_ok = sem("fx_ok")
        fl_mm = sem("fl_mm")
        fl_ex = sem("fl_ex")
        fl_al = sem("fl_al")
        fl_e = sem("fl_e")
        fa_tr = sem("fa_tr")
        fa_T = sem("fa_T")
        fa_mm = sem("fa_mm")
        fa_ok = sem("fa_ok")
        fo_mm = sem("fo_mm")
        fo_read = sem("fo_read")
        gw_mm = sem("gw_mm")
        gw_ok = sem("gw_ok")
        mw_mm = sem("mw_mm")
        mw_ok = sem("mw_ok")
        a_mm = sem("a_mm")
        a_ok = sem("a_ok")
        av_tr = sem("av_tr")
        av_ok = sem("av_ok")
        as_mm = sem("as_mm")
        as_nm = sem("as_nm")
        as_exp = sem("as_exp")
        at_mm = sem("at_mm")
        at_ev = sem("at_ev")
        at_od = sem("at_od")
        av_mm = sem("av_mm")
        cn_ok = sem("cn_ok")
        cn_tr = sem("cn_tr")
        cn_T = sem("cn_T")
        ao_mm = sem("ao_mm")
        ao_read = sem("ao_read")
        l_q_mm = sem("l_q_mm")
        l_q_ok = sem("l_q_ok")
        lb_mm = sem("lb_mm")
        lb_rot = sem("lb_rot")
        lb_add = sem("lb_add")
        lu_mm = sem("lu_mm")
        lu_ok = sem("lu_ok")
        lut_mm = sem("lut_mm")
        lut_ok = sem("lut_ok")
        ls_mm = sem("ls_mm")
        ls_nm = sem("ls_nm")
        ls_exp = sem("ls_exp")
        lt_mm = sem("lt_mm")
        lt_ok = sem("lt_ok")
        lv_mm = sem("lv_mm")
        lc_ok = sem("lc_ok")
        lf_tr = sem("lf_tr")
        lf_T = sem("lf_T")
        lf_mm = sem("lf_mm")
        lf_read = sem("lf_read")
        er_mm = sem("er_mm")
        er_sub = sem("er_sub")
        er_exp = sem("er_exp")
        eg_mm = sem("eg_mm")
        eg_th = sem("eg_th")
        eg_ok = sem("eg_ok")
        ey_mm = sem("ey_mm")
        ey_ok = sem("ey_ok")
        es_mm = sem("es_mm")
        x_done = sem("x_done")
        ld_w5 = [sem(f"ld_w5{j}") for j in range(2)]
        s_out = sem("s_out")

        block = ctx.enter_context(nc.Block())

        xv = a["x"].rearrange("b (t p) d -> p (b t) d", p=P)
        ov = out.rearrange("b (t p) d -> p (b t) d", p=P)

        @block.sync
        def _(sp):
            for b in range(B):
                sp.dma_start(X[:, TB * b:TB * b + TB, :], xv[:, TB * b:TB * b + TB, :]).then_inc(ld_x[b], 16)
                if b == 0:
                    sp.dma_start(ident[:, :], a["ident"]).then_inc(ld_c, 16)
            for dst, src in ((ctxT, "ctxT"), (wk_T[:, :], "wk_T"), (bk_col[:, :], "bk"), (ctx_tok, "ctx"),
                             (cos_k, "cos_k"), (sin_k, "sin_k")):
                sp.dma_start(dst, a[src]).then_inc(ld_cx, 16)
            sp.dma_start(bk_row[:, :], a["bk"].rearrange("c o -> (c o)").partition_broadcast(P)).then_inc(ld_cx, 16)
            for dst, src in ((b_w, "b_w"), (mask, "mask")):
                sp.dma_start(dst[:], a[src]).then_inc(ld_1, 16)
            for dst, src in ((bb_row, "bb"), (vb_row, "vb"), (ob_row, "ob")):
                sp.dma_start(dst[:, :], a[src].partition_broadcast(P)).then_inc(ld_1, 16)
            for j in range(2):
                sp.dma_start(w_slot[:, j], a["w_head"][j]).then_inc(ld_w[j], 16)
            sp.dma_start(o_w[:], a["o_w"]).then_inc(ld_o, 16)
            with nc.sync.Fori(1, H0 // 2) as i:
                for j in range(2):
                    sp.wait_ge(vg_mm, 8 * i - 4 + 4 * j)
                    sp.wait_ge(qk_read, 8 * i - 4 + 4 * j)
                    sp.dma_start(w_slot[:, j], a["w_head"][2 * i + j]).then_inc(ld_w[j], 16)
            for dst, src in ((gam_row, "gam"), (bet_row, "bet")):
                sp.dma_start(dst[:, :], a[src].partition_broadcast(P)).then_inc(ld_2, 16)
            for dst, src in ((f_w1, "f_w1"), (f_b1, "f_b1"), (f_w2, "f_w2"), (f_v, "f_v"), (f_u, "f_u"), (f_sel, "f_sel")):
                sp.dma_start(dst[:] if dst is not f_v and dst is not f_u else dst, a[src]).then_inc(ld_3, 16)
            sp.dma_start(f_b2[:, :], a["f_b2"].partition_broadcast(P)).then_inc(ld_3, 16)
            for dst, src in ((a_w, "a_w"), (a_b, "a_b"), (a_par, "a_par"), (a_ow, "a_ow"), (e_gate, "e_gate")):
                sp.dma_start(dst[:], a[src]).then_inc(ld_4, 16)
            for dst, src in ((aob_row, "aob"), (e_rev, "e_rev")):
                sp.dma_start(dst[:, :], a[src].partition_broadcast(P)).then_inc(ld_4, 16)
            sp.wait_ge(o_mm, NT)
            for dst, src in ((wo_T, "wo_T"), (kc_kv, "kc_kv"), (qr_T, "qr_T"), (kr_T, "kr_T")):
                sp.dma_start(dst, a[src]).then_inc(ld_p, 16)
            for dst, src in ((cos_q, "cos_q"), (sin_q, "sin_q")):
                sp.dma_start(dst, a[src]).then_inc(ld_t, 16)
            for j in range(2):
                sp.dma_start(w5[:, j, 0:448], a["w5"][j]).then_inc(ld_w5[j], 16)
            for dst, src in ((e_gu, "e_gu"), (e_sgu, "e_sgu"), (e_dn, "e_dn"), (e_sdn, "e_sdn")):
                sp.dma_start(dst, a[src]).then_inc(ld_6, 16)
            with nc.sync.Fori(1, H2 // 2) as p:
                for j in range(2):
                    sp.wait_ge(lb_mm, 4 * p - 2 + 2 * j)
                    sp.dma_start(w5[:, j, 0:448], a["w5"][2 * p + j]).then_inc(ld_w5[j], 16)
            for b in range(B):
                sp.wait_ge(x_done, b + 1)
                sp.dma_start(ov[:, TB * b:TB * b + TB, :], X[:, TB * b:TB * b + TB, :]).then_inc(s_out, 16)
            sp.wait_ge(s_out, 16 * B)

        @block.gpsimd
        def _(pool):
            nc.gpsimd.memset(ones[:, :], 1.0)
            nc.gpsimd.memset(half[:, :], -0.5).then_inc(consts, 1)
            pool.wait_ge(consts, 1)

            def ln_power(s, b, place=None):
                at = TB * b if place is None else place
                pool.wait_ge(ln_ve, B * s + b + 1)
                nc.gpsimd.tensor_tensor(ln_r[:, at:at + TB], ln_var[:, at:at + TB], half[:, 0:TB],
                                        ALU.pow).then_inc(ln_pw, 1)

            nc.gpsimd.memset(lat[:, :, XC:C2], 1.0).then_inc(consts, 1)
            for b in range(B):
                ln_power(0, b)
            pool.wait_ge(ln_h, B)
            pool.wait_ge(ld_1, 16 * 5)
            nc.gpsimd.tensor_tensor(X[:, :, :], X[:, :, :], ob_row[:, :].unsqueeze(1).broadcast_to([P, NT, D]),
                                    ALU.add).then_inc(x_bias, 1)

            def norm_power(h):
                pool.wait_ge(ss_read, h + 1)
                nc.gpsimd.tensor_tensor(norm[:, 1, :], norm[:, 0, :], half[:, :], ALU.pow).then_inc(ss_pow, 1)

            norm_power(0)
            with nc.gpsimd.Fori(1, H0) as h:
                norm_power(h)
            for b in range(B):
                ln_power(1, b)

            for b in range(B + 1):
                if b < B:
                    pool.wait_ge(xs_ve, b + 1)
                    nc.gpsimd.tensor_tensor(x_v[:, 1, :], x_v[:, 0, :], half[:, 0:TB], ALU.pow).then_inc(xs_pw, 1)
                if b:
                    ln_power(2, b - 1)
            for b in range(B):
                ln_power(3, b)
            pool.wait_ge(fo_read, B)
            nc.gpsimd.memset(a_v[:, :, :, D1:V1], 1.0).then_inc(consts, 1)
            pool.wait_ge(ln_h, 4 * B)
            pool.wait_ge(ld_4, 16 * 7)
            nc.gpsimd.tensor_tensor(X[:, :, :], X[:, :, :], aob_row[:, :].unsqueeze(1).broadcast_to([P, NT, D]),
                                    ALU.add).then_inc(x_bias, 1)
            with nc.gpsimd.Fori(0, B) as b:
                ln_power(4, b, 0)
            def rotate_sum(r, c, after):
                if after:
                    pool.wait_ge(lu_mm, r - 1)
                pool.wait_ge(lb_rot, r + 1)
                cols = slice(512 * c, 512 * c + 512)
                nc.gpsimd.tensor_tensor(l_rot[:, 0, cols], l_pr[:, 0, :], l_pr[:, 1, :], ALU.subtract)
                nc.gpsimd.tensor_tensor(l_rot[:, 1, cols], l_pr[:, 2, :], l_pr[:, 3, :], ALU.add).then_inc(lb_add, 1)

            for r in range(4):
                rotate_sum(r, r % 2, r >= 2)
            with nc.gpsimd.Fori(1, H2 // 2) as p:
                for r in range(4):
                    rotate_sum(4 * p + r, r % 2, True)
            for b in range(B):
                ln_power(5, b)

        @block.vector
        def _(v):
            link = Chain(v, dve)

            def ln_rows(s, b, place=None):
                at = TB * b if place is None else place
                two = slice(at, at + TB)
                for i in range(TB):
                    ins = nc.vector.bn_stats(ln_stat[:, at + i, :], X[:, ds(TB * b + i, 1), :].rearrange("p o c -> p (o c)"))
                link(ins)
                if place is not None:
                    nc.vector.memset(ln_none[:, :], 0.0)
                for i in range(TB):
                    ins = nc.vector.bn_aggr(ln_mv[:, at + i, :], ln_stat[:, at + i, :])
                link(ins)
                nc.vector.tensor_scalar(ln_var[:, two], ln_mv[:, two, 1], LN_EPS, None, ALU.add).then_inc(ln_ve, 1)
                v.wait_ge(ln_pw, B * s + b + 1)
                link(nc.vector.scalar_tensor_tensor(out=ln_t[:, two], in0=ln_r[:, two], scalar=-0.5, in1=ln_r[:, two],
                                                    op0=ALU.mult, op1=ALU.mult))
                link(nc.vector.tensor_tensor(ln_t[:, two], ln_t[:, two], ln_var[:, two], ALU.mult))
                link(nc.vector.scalar_tensor_tensor(out=ln_rstd[:, two], in0=ln_t[:, two], scalar=1.5, in1=ln_r[:, two],
                                                    op0=ALU.add, op1=ALU.mult))
                for i in range(TB):
                    ins = nc.vector.tensor_scalar(HN[:, at + i:at + i + 1, :], X[:, ds(TB * b + i, 1), :],
                                                  ln_mv[:, at + i, 0:1], ln_rstd[:, at + i:at + i + 1],
                                                  ALU.subtract, ALU.mult)
                ins.then_inc(ln_h, 1)

            for b in range(B):
                v.wait_ge(ld_x[b], 16)
                ln_rows(0, b)

            v.wait_ge(ld_cx, 16 * 7)
            hf = XC // 2
            for b in range(B):
                two = slice(TB * b, TB * b + TB)
                nc.vector.tensor_tensor(rot_k[:, two, 0:hf], ctx_tok[:, two, hf:XC], sin_k[:, :, 0:hf], ALU.mult)
                nc.vector.tensor_tensor(rot_k[:, two, hf:XC], ctx_tok[:, two, 0:hf], sin_k[:, :, hf:XC], ALU.mult)
                ins = nc.vector.tensor_tensor(lat[:, two, 0:XC], ctx_tok[:, two, :], cos_k, ALU.mult)
            link(ins)
            link(nc.vector.tensor_tensor(lat[:, :, 0:XC], lat[:, :, 0:XC], rot_k, ALU.add))
            for j in range(2):
                ins = nc.vector.tensor_copy(lat2[:, :, j * XC:j * XC + XC], lat[:, :, 0:XC])
            ins.then_inc(lat_ok, 1)
            v.wait_ge(kvn_mm, 1)
            nc.vector.tensor_tensor(kv[:, :, :], bank[3][:, :].rearrange("p (t c) -> p t c", t=NT),
                                    bk_row[:, :].unsqueeze(1).broadcast_to([P, NT, XC]), ALU.add).then_inc(kvn_ok, 1)

            z, m, u, w, lw, c = [bt[:, n, :] for n in range(6)]
            v.wait_ge(bt_mm, 1)
            v.wait_ge(ld_1, 16 * 5)
            link(nc.vector.tensor_tensor(z.rearrange("p (t h) -> p t h", t=NT), PRB.rearrange("p (t h) -> p t h", t=NT),
                                         bb_row[:, :].unsqueeze(1).broadcast_to([P, NT, H0]), ALU.add))
            link(nc.vector.tensor_scalar(m, z, -1.0, None, ALU.mult))
            nc.vector.tensor_tensor(c, z, m, ALU.max).then_inc(bt_abs, 1)
            v.wait_ge(bt_abs, 1)
            v.wait_ge(bt_exp, 1)
            nc.vector.tensor_scalar(w, u, 1.0, None, ALU.add).then_inc(bt_w, 1)
            v.wait_ge(bt_w, 1)
            link(nc.vector.tensor_scalar(c, w, -1.0, None, ALU.add))
            link(nc.vector.tensor_tensor(c, u, c, ALU.subtract))
            link(nc.vector.reciprocal(m, w))
            link(nc.vector.tensor_tensor(c, c, m, ALU.mult))
            link(nc.vector.tensor_scalar(m, z, 0.0, None, ALU.max))
            link(nc.vector.tensor_tensor(c, c, m, ALU.add))
            v.wait_ge(bt_ln, 1)
            link(nc.vector.tensor_tensor(beta[:, :, :].rearrange("p t h -> p (t h)"), c, lw, ALU.add))

            def scale_of(g):
                v.wait_ge(ss_mm, g + 1)
                nc.vector.tensor_scalar(norm[:, 0, :], sumsq, NORM_FLOOR, None, ALU.max).then_inc(ss_read, 1)
                v.wait_ge(ss_pow, g + 1)
                link(nc.vector.scalar_tensor_tensor(out=norm[:, 2, :], in0=norm[:, 1, :], scalar=-0.5,
                                                    in1=norm[:, 1, :], op0=ALU.mult, op1=ALU.mult))
                link(nc.vector.tensor_tensor(norm[:, 2, :], norm[:, 2, :], norm[:, 0, :], ALU.mult))
                link(nc.vector.scalar_tensor_tensor(out=norm[:, 3, :], in0=norm[:, 2, :], scalar=1.5,
                                                    in1=norm[:, 1, :], op0=ALU.add, op1=ALU.mult))
                link(nc.vector.tensor_tensor(norm[:, 3, NT:2 * NT], norm[:, 3, NT:2 * NT],
                                             beta[:, :, ds(g, 1)].rearrange("p t o -> p (t o)"), ALU.mult))

            def mask_scores(g, after):
                if after:
                    v.wait_ge(pv_mm, 2 * g)
                for n in range(2):
                    v.wait_ge(sc_mm, 2 * g + n + 1)
                    for t in range(4 * n, 4 * n + 4):
                        ins = nc.vector.scalar_tensor_tensor(out=attn[:, t, :], in0=SC[n][:, t % 4, :],
                                                             scalar=norm[:, 3, NT + t:NT + t + 1], in1=mask[:, :],
                                                             op0=ALU.mult, op1=ALU.mult)
                    ins.then_inc(masked, 1)

            def gate_out(g, after):
                if after:
                    v.wait_ge(tr_mm, 2 * g)
                for n in range(2):
                    v.wait_ge(pv_mm, 2 * g + n + 1)
                    for t in range(4 * n, 4 * n + 4):
                        ins = nc.vector.scalar_tensor_tensor(out=gated[:, t, :], in0=OV[n][:, t % 4, :],
                                                             scalar=norm[:, 3, t:t + 1], in1=gate[:, t, :],
                                                             op0=ALU.mult, op1=ALU.mult)
                    ins.then_inc(gated_ok, 1)

            def values_gates(h, after):
                if after:
                    v.wait_ge(gated_ok, 2 * h)
                for n in range(4):
                    two = slice(2 * n, 2 * n + 2)
                    v.wait_ge(tanh_done, 4 * h + n + 1)
                    nc.vector.tensor_tensor(v_tok[:, two, :], VG[n % 2][:, :, 0:D0],
                                            vb_row[:, ds(h * D0, D0)].unsqueeze(1).broadcast_to([P, 2, D0]), ALU.add)
                    nc.vector.scalar_tensor_tensor(out=gate[:, two, :], in0=tanh_g[:, n % 2], scalar=1.0,
                                                   in1=VG[n % 2][:, :, D0:2 * D0], op0=ALU.add,
                                                   op1=ALU.mult).then_inc(vg_read, 1)

            values_gates(0, False)
            scale_of(0)
            mask_scores(0, False)
            gate_out(0, False)
            values_gates(1, True)
            with nc.vector.Fori(2, H0) as h, link.over(h, 2, H0, 4):
                scale_of(h - 1)
                mask_scores(h - 1, True)
                gate_out(h - 1, True)
                values_gates(h, True)
            scale_of(H0 - 1)
            mask_scores(H0 - 1, True)
            gate_out(H0 - 1, True)

            v.wait_ge(x_bias, 1)
            for t in range(NT):
                v.wait_ge(o_mm, t + 1)
                nc.vector.tensor_tensor(X[:, t, :], X[:, t, :], bank[t % 2][:, 0:D], ALU.add).then_inc(o_read, 1)
                if t % TB == TB - 1:
                    v.wait_ge(o_read, t + 1)
                    ln_rows(1, t // TB)

            def similarity(b):
                n = b % 2
                v.wait_ge(xs_mm, b + 1)
                for t in range(TB):
                    ins = nc.vector.bn_stats(x_stat[:, t, :], XS[n][:, t, :])
                link(ins)
                for t in range(TB):
                    ins = nc.vector.bn_aggr(x_mv[:, t, :], x_stat[:, t, :])
                link(ins)
                nc.vector.tensor_scalar(x_v[:, 0, :], x_mv[:, :, 1], X0_EPS, None, ALU.add).then_inc(xs_ve, 1)
                for t in range(TB):
                    ins = nc.vector.scalar_tensor_tensor(out=x_sim[:, n, t, :], in0=XS[n][:, t, :],
                                                         scalar=x_mv[:, t, 0:1], in1=gam_row[:, :],
                                                         op0=ALU.subtract, op1=ALU.mult)
                ins.then_inc(xs_free, 1)
                v.wait_ge(xs_pw, b + 1)
                link(nc.vector.scalar_tensor_tensor(out=x_v[:, 2, :], in0=x_v[:, 1, :], scalar=-0.5, in1=x_v[:, 1, :],
                                                    op0=ALU.mult, op1=ALU.mult))
                link(nc.vector.tensor_tensor(x_v[:, 2, :], x_v[:, 2, :], x_v[:, 0, :], ALU.mult))
                link(nc.vector.scalar_tensor_tensor(out=x_v[:, 3, :], in0=x_v[:, 2, :], scalar=1.5, in1=x_v[:, 1, :],
                                                    op0=ALU.add, op1=ALU.mult))
                for t in range(TB):
                    ins = nc.vector.scalar_tensor_tensor(out=x_sim[:, n, t, :], in0=x_sim[:, n, t, :],
                                                         scalar=x_v[:, 3, t:t + 1], in1=bet_row[:, :],
                                                         op0=ALU.mult, op1=ALU.add)
                link(ins)
                nc.vector.tensor_reduce(x_nm[:, n, :], x_sim[:, n], AX_X, ALU.max, negate=True).then_inc(xs_nm, 1)

            def attend_context(b):
                n = b % 2
                v.wait_ge(xs_exp, b + 1)
                link(nc.vector.reciprocal(x_rc[:, :], x_sum[:, n, :]))
                for t in range(TB):
                    ins = nc.vector.scalar_tensor_tensor(out=X[:, TB * b + t, :], in0=x_e[:, n, t, :],
                                                         scalar=x_rc[:, t:t + 1], in1=X[:, TB * b + t, :],
                                                         op0=ALU.mult, op1=ALU.add)
                link(ins)

            v.wait_ge(ld_2, 32)
            for b in range(B + 1):
                if b < B:
                    similarity(b)
                if b:
                    attend_context(b - 1)
                    ln_rows(2, b - 1)

            def mixture(b):
                wide = [P, TB, FK]
                lg, ex, al = f_al[:, 0], f_al[:, 1], f_al[:, 2]
                v.wait_ge(fl_mm, b + 1)
                link(nc.vector.tensor_tensor(lg, FL, f_b2[:, :].unsqueeze(1).broadcast_to(wide), ALU.add))
                link(nc.vector.tensor_reduce(f_st[:, 0, :], lg, AX_X, ALU.max))
                nc.vector.tensor_tensor(lg, lg, f_st[:, 0, :].unsqueeze(2).broadcast_to(wide), ALU.subtract).then_inc(fl_ex, 1)
                v.wait_ge(fl_e, b + 1)
                link(nc.vector.tensor_reduce(f_st[:, 1, :], ex, AX_X, ALU.add))
                link(nc.vector.reciprocal(f_st[:, 2, :], f_st[:, 1, :]))
                nc.vector.tensor_tensor(al, ex, f_st[:, 2, :].unsqueeze(2).broadcast_to(wide), ALU.mult).then_inc(fl_al, 1)

            def weigh(b):
                for n in range(2):
                    v.wait_ge(fa_mm, 2 * b + n + 1)
                    v.wait_ge(fx_ok, 2 * b + n + 1)
                    nc.vector.tensor_tensor(f_ax[:, 2 * n:2 * n + 2, :], f_vx[:, 2 * n:2 * n + 2, :], FA[n],
                                            ALU.mult).then_inc(fa_ok, 1)
                v.wait_ge(fo_mm, b + 1)
                nc.vector.tensor_tensor(X[:, TB * b:TB * b + TB, :], X[:, TB * b:TB * b + TB, :], FO, ALU.add).then_inc(fo_read, 1)
                v.wait_ge(fo_read, b + 1)

            v.wait_ge(ld_3, 16 * 7)
            for b in range(B):
                mixture(b)
                weigh(b)
                ln_rows(3, b)

            def value_rows(b):
                v.wait_ge(av_tr, b + 1)
                nc.vector.tensor_copy(a_v[:, :, :, 0:D1], bank[1][:, :].rearrange("p (t h c) -> p t h c", t=TB, h=H1)).then_inc(av_ok, 1)

            def heads(b):
                for n in range(H1 + 1):
                    if n < H1:
                        v.wait_ge(as_mm, H1 * b + n + 1)
                        nc.vector.tensor_reduce(a_nm[:, n % 2, :], AS[n % 2], AX_X, ALU.max, negate=True).then_inc(as_nm, 1)
                    if n >= 1 and (n - 1) % 2:
                        v.wait_ge(at_mm, H1 * b + n)
                        nc.vector.tensor_copy(a_pT[:, 1], AT[1]).then_inc(at_od, 1)
                v.wait_ge(av_mm, b + 1)
                for t in range(TB):
                    ins = nc.vector.reciprocal(a_rc[:, t, :], AV[t][:, :, D1])
                link(ins)
                for t in range(TB):
                    ins = nc.vector.tensor_tensor(a_cn[:, t, :].rearrange("p (h c) -> p h c", h=H1), AV[t][:, :, 0:D1],
                                                  a_rc[:, t, :].unsqueeze(2).broadcast_to([P, H1, D1]), ALU.mult)
                ins.then_inc(cn_ok, 1)

            def attend_self(b):
                v.wait_ge(ao_mm, b + 1)
                xb = X[:, ds(TB * b, TB), :]
                link(nc.vector.tensor_tensor(xb, xb, AB[0], ALU.add))
                v.sem_inc(ao_read, 1)

            v.wait_ge(ld_4, 16 * 7)
            nc.vector.tensor_scalar(a_bs[:, 0:2], a_b[:, 0:2], D1 ** -0.5, None, ALU.mult)
            nc.vector.tensor_scalar(a_bs[:, 2:4], a_b[:, 2:4], a_par[:, 0:1], None, ALU.mult)
            nc.vector.tensor_scalar(a_bs[:, 4:6], a_b[:, 2:4], a_par[:, 1:2], None, ALU.mult).then_inc(consts, 1)
            v.wait_ge(x_bias, 2)
            value_rows(0)
            heads(0)
            with nc.vector.Fori(1, B) as b, link.over(b, 1, B, 7):
                value_rows(b)
                attend_self(b - 1)
                ln_rows(4, b - 1, 0)
                heads(b)
            attend_self(B - 1)
            ln_rows(4, B - 1, 0)

            def rotate(r, after):
                v.wait_ge(lb_mm, r + 1)
                if after:
                    v.wait_ge(lb_add, r)
                for n, (src, table) in enumerate(((0, cos_q[:, 0]), (1, sin_q[:, 0]), (1, cos_q[:, 1]), (0, sin_q[:, 1]))):
                    ins = nc.vector.tensor_tensor(l_pr[:, n, :].rearrange("p (b s) -> p b s", b=2),
                                                  LR[src][0:QH, :].rearrange("p (b s) -> p b s", b=2),
                                                  table.unsqueeze(1).broadcast_to([QH, 2, S]), ALU.mult)
                ins.then_inc(lb_rot, 1)

            def row_max(u, n):
                v.wait_ge(ls_mm, u + 1)
                nc.vector.tensor_reduce(l_nm[:, n % 2, :], LS, AX_X, ALU.max, negate=True).then_inc(ls_nm, 1)

            def latent_out(g, u, n):
                v.wait_ge(lv_mm, u + 1)
                link(nc.vector.reciprocal(l_rc[:, :], LV[:, :, XC]))
                j, b = n // B, n % B
                nc.vector.tensor_tensor(l_cn[:, TB * b:TB * b + TB, ds(g * P + j * XC, XC)], LV[:, :, 0:XC],
                                        l_rc[:, :].unsqueeze(2).broadcast_to([P, TB, XC]), ALU.mult).then_inc(lc_ok, 1)
                v.wait_ge(lc_ok, u + 1)

            def pair_rows(p, make, use):
                for k in range(10):
                    if make and k in (2, 4, 6, 7):
                        r = (2, 4, 6, 7).index(k)
                        rotate(4 * p + r, use or r)
                    if use and 1 <= k <= 8:
                        row_max(8 * p - 8 + k - 1, k - 1)
                    if use and k >= 2:
                        latent_out(p - 1, 8 * p - 8 + k - 2, k - 2)

            v.wait_ge(ld_t, 32)
            pair_rows(0, True, False)
            with nc.vector.Fori(1, H2 // 2) as p, link.over(p, 1, H2 // 2, 8):
                pair_rows(p, True, True)
            pair_rows(H2 // 2, False, True)
            for t in range(NT):
                v.wait_ge(lf_mm, t + 1)
                nc.vector.tensor_tensor(X[:, t, :], X[:, t, :], bank[2 + t % 2][:, 0:D], ALU.add).then_inc(lf_read, 1)
                if t % TB == TB - 1:
                    v.wait_ge(lf_read, t + 1)
                    ln_rows(5, t // TB)

            def first_best(p, best, one, sc, mi):
                wide = [P, NT, E6]
                link(nc.vector.tensor_reduce(best, p, AX_X, ALU.max))
                link(nc.vector.tensor_tensor(sc, p, best.unsqueeze(2).broadcast_to(wide), ALU.is_equal))
                link(nc.vector.tensor_tensor(sc, sc, e_rev[:, :].unsqueeze(1).broadcast_to(wide), ALU.mult))
                link(nc.vector.tensor_reduce(mi, sc, AX_X, ALU.max))
                link(nc.vector.tensor_tensor(one, sc, mi.unsqueeze(2).broadcast_to(wide), ALU.is_equal))

            def route():
                wide = [P, NT, E6]
                lg, ex, p, one1, one2, sc = [e_r[:, n] for n in range(6)]
                mx, sm, rc, b1, b2, mi = [e_s[:, n, :] for n in range(6)]
                v.wait_ge(er_mm, 1)
                link(nc.vector.tensor_reduce(mx, EL, AX_X, ALU.max))
                nc.vector.tensor_tensor(lg, EL, mx.unsqueeze(2).broadcast_to(wide), ALU.subtract).then_inc(er_sub, 1)
                v.wait_ge(er_exp, 1)
                link(nc.vector.tensor_reduce(sm, ex, AX_X, ALU.add))
                link(nc.vector.reciprocal(rc, sm))
                link(nc.vector.tensor_tensor(p, ex, rc.unsqueeze(2).broadcast_to(wide), ALU.mult))
                first_best(p, b1, one1, sc, mi)
                link(nc.vector.scalar_tensor_tensor(out=lg.rearrange("p t e -> p (t e)"), in0=one1.rearrange("p t e -> p (t e)"),
                                                    scalar=-4.0, in1=p.rearrange("p t e -> p (t e)"), op0=ALU.mult, op1=ALU.add))
                first_best(lg, b2, one2, sc, mi)
                link(nc.vector.tensor_tensor(one1, one1, one2, ALU.add))
                link(nc.vector.tensor_tensor(sm, b1, b2, ALU.add))
                link(nc.vector.reciprocal(rc, sm))
                link(nc.vector.tensor_scalar(rc, rc, 0.5, None, ALU.mult))
                link(nc.vector.tensor_tensor(p, p, one1, ALU.mult))
                link(nc.vector.tensor_tensor(e_comb[:, :, :], p, rc.unsqueeze(2).broadcast_to(wide), ALU.mult))

            def gated_unit(b, u):
                U = (E6 + SF) * b + u
                n = u % 2
                v.wait_ge(eg_th, U + 1)
                link(nc.vector.scalar_tensor_tensor(out=e_sg[:, n, :], in0=e_th[:, n, :], scalar=1.0, in1=EG[n][:, 0, :],
                                                    op0=ALU.add, op1=ALU.mult))
                nc.vector.tensor_tensor(e_act[:, n, :], e_sg[:, n, :], EG[n][:, 1, :], ALU.mult).then_inc(eg_ok, 1)

            def add_expert(b, e, after):
                v.wait_ge(ey_mm, E6 * b + e + 1)
                if after:
                    v.wait_ge(ey_ok, E6 * b + e)
                for t in range(TB):
                    xt = X[:, ds(TB * b + t, 1), :].rearrange("p o d -> p (o d)")
                    ins = nc.vector.scalar_tensor_tensor(out=xt, in0=EY[e % 2][:, t, :],
                                                         scalar=e_comb[:, ds(TB * b + t, 1), e].rearrange("p o -> p o"), in1=xt,
                                                         op0=ALU.mult, op1=ALU.add)
                ins.then_inc(ey_ok, 1)

            def moe_batch(b, after):
                for u in range(E6 + SF):
                    gated_unit(b, u)
                    if 1 <= u <= E6:
                        add_expert(b, u - 1, after or u > 1)
                v.wait_ge(es_mm, b + 1)
                v.wait_ge(ey_ok, E6 * b + E6)
                for t in range(TB):
                    xt = X[:, ds(TB * b + t, 1), :].rearrange("p o d -> p (o d)")
                    ins = nc.vector.scalar_tensor_tensor(out=xt, in0=ES[t][:, 0:D], scalar=0.5, in1=xt,
                                                         op0=ALU.mult, op1=ALU.add)
                ins.then_inc(x_done, 1)

            route()
            moe_batch(0, False)
            with nc.vector.Fori(1, B) as b, link.over(b, 1, B, E6 + SF):
                moe_batch(b, True)

        @block.scalar
        def _(act):
            def ln_columns(s, b, src):
                act.wait_ge(ln_tr, B * s + b + 1)
                nc.scalar.copy(HT[:, :, ds(S * b, S)], src[:, :].rearrange("p (k t) -> p k t", k=KT)).then_inc(ln_ht, 1)

            act.wait_ge(ld_cx, 16 * 7)
            for n in range(2):
                act.wait_ge(kvt_mm, n + 1)
                nc.scalar.activation(kvT[:, 512 * n:512 * n + 512], bank[n][0:XC, :], ACT.Identity,
                                     bias=bk_col[:, :]).then_inc(kvt_ok, 1)
            for b in range(B):
                ln_columns(0, b, bank[6 + b % 2])
            for n in range(2):
                act.wait_ge(lat_mm, n + 1)
                nc.scalar.copy(latT[:, 512 * n:512 * n + 512], bank[4 + n][:, :]).then_inc(latT_ok, 1)
            z, m, u, w, lw, c = [bt[:, n, :] for n in range(6)]
            act.wait_ge(bt_abs, 1)
            nc.scalar.activation(u, c, ACT.Exp, scale=-1.0).then_inc(bt_exp, 1)
            act.wait_ge(bt_w, 1)
            nc.scalar.activation(lw, w, ACT.Ln).then_inc(bt_ln, 1)

            def queries_keys(h, j):
                for n, (lin, sq) in enumerate(((qT, q2), (kT, k2))):
                    bias = qk_bias[:, j, n:n + 1]
                    for c in range(2):
                        cols = slice(512 * c, 512 * c + 512)
                        act.wait_ge(qk_mm, 4 * h + 2 * n + c + 1)
                        nc.scalar.activation(lin[:, cols], QK[c][:, :], ACT.Identity, bias=bias)
                        nc.scalar.activation(sq[:, cols], QK[c][:, :], ACT.Square, bias=bias).then_inc(qk_read, 1)

            def gates(h):
                for n in range(4):
                    act.wait_ge(vg_mm, 4 * h + n + 1)
                    nc.scalar.activation(tanh_g[:, n % 2], VG[n % 2][:, :, D0:2 * D0], ACT.Tanh,
                                         scale=0.5).then_inc(tanh_done, 1)

            def head_out(g):
                for n in range(2):
                    act.wait_ge(tr_mm, 2 * g + n + 1)
                    nc.scalar.copy(outT[:, ds(g, 1), 512 * n:512 * n + 512].rearrange("p o t -> p (o t)"),
                                   OV[n][:, :, :].rearrange("p t d -> p (t d)")).then_inc(outT_ok, 1)

            act.wait_ge(ld_1, 16 * 5)
            queries_keys(0, 0)
            gates(0)
            queries_keys(1, 1)
            gates(1)
            head_out(0)
            with nc.scalar.Fori(1, H0 // 2) as i:
                for j in range(2):
                    queries_keys(2 * i + j, j)
                    gates(2 * i + j)
                    head_out(2 * i + j - 1)
            head_out(H0 - 1)
            for b in range(B):
                ln_columns(1, b, bank[6 + b % 2])

            def context_out(b):
                act.wait_ge(xo_mm, b + 1)
                nc.scalar.activation(x_oT[:, b % 2, :], XO[b % 2][0:XC, 0:S], ACT.Copy, scale=X0_SCALE).then_inc(xo_ok, 1)

            def context_exp(b):
                n = b % 2
                act.wait_ge(xs_nm, b + 1)
                for t in range(TB):
                    ins = nc.scalar.activation(x_e[:, n, t, :], x_sim[:, n, t, :], ACT.Exp, bias=x_nm[:, n, t:t + 1],
                                               accum_out=x_sum[:, n, t:t + 1])
                ins.then_inc(xs_exp, 1)

            for b in range(B + 2):
                if b < B:
                    context_out(b)
                if b >= 2:
                    ln_columns(2, b - 2, bank[6 + b % 2])
                if b < B:
                    context_exp(b)

            for b in range(B):
                act.wait_ge(fh_mm, b + 1)
                for m in range(KT):
                    ins = nc.scalar.activation(f_h[:, m, :], FH[:, m, :], ACT.Relu, bias=f_b1[:, m:m + 1])
                ins.then_inc(fh_ok, 1)
                for n in range(2):
                    act.wait_ge(fx_mm, 2 * b + n + 1)
                    nc.scalar.copy(f_vx[:, 2 * n:2 * n + 2, :], FX[n]).then_inc(fx_ok, 1)
                act.wait_ge(fl_ex, b + 1)
                nc.scalar.activation(f_al[:, 1], f_al[:, 0], ACT.Exp).then_inc(fl_e, 1)
                act.wait_ge(fa_tr, b + 1)
                nc.scalar.copy(f_aT, FT).then_inc(fa_T, 1)
                if b:
                    ln_columns(3, b - 1, bank[7])
            ln_columns(3, B - 1, bank[7])

            def project_columns(b):
                act.wait_ge(a_mm, 3 * b + 1)
                for m in range(KT):
                    ins = nc.scalar.activation(a_q[:, m, :], AB[0][:, m, :], ACT.Identity, bias=a_bs[:, m:m + 1],
                                               scale=D1 ** -0.5)
                ins.then_inc(a_ok, 1)
                act.wait_ge(a_mm, 3 * b + 2)
                for o in range(2):
                    for m in range(KT):
                        ins = nc.scalar.activation(a_k[:, o, m, :], AB[1][:, m, :], ACT.Identity,
                                                   bias=a_bs[:, 2 + 2 * o + m:3 + 2 * o + m], scale=a_par[:, o:o + 1])
                ins.then_inc(a_ok, 1)
                act.wait_ge(a_mm, 3 * b + 3)
                for m in range(KT):
                    ins = nc.scalar.activation(a_vT[:, m, :], AB[0][:, m, :], ACT.Identity, bias=a_b[:, 4 + m:5 + m])
                ins.then_inc(a_ok, 1)

            def head_exps(b):
                for n in range(H1 + 1):
                    if n < H1:
                        act.wait_ge(as_nm, H1 * b + n + 1)
                        for t in range(TB):
                            ins = nc.scalar.activation(a_p[:, n % 2, t, :], AS[n % 2][:, t, :], ACT.Exp,
                                                       bias=a_nm[:, n % 2, t:t + 1])
                        ins.then_inc(as_exp, 1)
                    if n >= 1 and (n - 1) % 2 == 0:
                        act.wait_ge(at_mm, H1 * b + n)
                        nc.scalar.copy(a_pT[:, 0], AT[0]).then_inc(at_ev, 1)

            def context_columns(b):
                act.wait_ge(cn_tr, b + 1)
                nc.scalar.copy(a_cT, AB[1]).then_inc(cn_T, 1)

            for n in range(4):
                act.wait_ge(gw_mm, n + 1)
                nc.scalar.copy(Gw[:, n // 2, 8 * (n % 2):8 * (n % 2) + 8, :], bank[n][0:QH, :].rearrange("p (h c) -> p h c", h=8)).then_inc(gw_ok, 1)
            for n in range(4):
                act.wait_ge(mw_mm, n + 1)
                nc.scalar.copy(Mw[:, 2 * n:2 * n + 2, :], bank[4 + n][:, :].rearrange("p (m d) -> p m d", m=2)).then_inc(mw_ok, 1)
            act.wait_ge(consts, 4)
            project_columns(0)
            head_exps(0)
            with nc.scalar.Fori(1, B) as b:
                project_columns(b)
                context_columns(b - 1)
                head_exps(b)
                ln_columns(4, b - 1, bank[1])
            context_columns(B - 1)
            ln_columns(4, B - 1, bank[1])

            def query_keys(p, q, c):
                act.wait_ge(l_q_mm, 4 * p + q + 1)
                nc.scalar.copy(l_q[:, 512 * c:512 * c + 512], bank[c][:, :]).then_inc(l_q_ok, 1)

            def pair_columns(p, make, use):
                for k in range(10):
                    if use and 2 <= k:
                        u = 8 * p - 8 + k - 2
                        act.wait_ge(ls_nm, u + 1)
                        for t in range(TB):
                            ins = nc.scalar.activation(l_p[:, t, :], LS[:, t, :], ACT.Exp, bias=l_nm[:, k % 2, t:t + 1])
                        ins.then_inc(ls_exp, 1)
                    if make and k in (0, 1, 3, 5):
                        q = (0, 1, 3, 5).index(k)
                        query_keys(p, q, q % 2)
                    if make and k == 7:
                        act.wait_ge(lu_mm, 4 * p + 2)
                        nc.scalar.copy(l_u[:, :, 0:XC], LU).then_inc(lu_ok, 1)
                    if use and 2 <= k:
                        act.wait_ge(lt_mm, u + 1)
                        nc.scalar.copy(l_pT, LT).then_inc(lt_ok, 1)
                if make:
                    act.wait_ge(lu_mm, 4 * p + 4)
                    nc.scalar.copy(l_u[:, :, XC:2 * XC], LU).then_inc(lu_ok, 1)
                    for c in range(2):
                        act.wait_ge(lut_mm, 2 * p + c + 1)
                        nc.scalar.copy(l_uT[:, 512 * c:512 * c + 512], bank[c][:, :]).then_inc(lut_ok, 1)

            pair_columns(0, True, False)
            with nc.scalar.Fori(1, H2 // 2) as p:
                pair_columns(p, True, True)
            pair_columns(H2 // 2, False, True)
            for t in range(NT):
                for n in range(2):
                    act.wait_ge(lf_tr, 2 * t + n + 1)
                    nc.scalar.copy(l_cT[:, t % 2, 4 * n:4 * n + 4, :], bank[n][:, :].rearrange("p (m t) -> p m t", m=4)).then_inc(lf_T, 1)
                if t >= 4 and t % 2 == 0:
                    ln_columns(5, t // 2 - 2, bank[6 + t // 2 % 2])
            ln_columns(5, 2, bank[6])
            ln_columns(5, 3, bank[7])

            def moe_tanh(b):
                for u in range(E6 + SF):
                    act.wait_ge(eg_mm, (E6 + SF) * b + u + 1)
                    nc.scalar.activation(e_th[:, u % 2, :], EG[u % 2][:, 0, :], ACT.Tanh, scale=0.5).then_inc(eg_th, 1)

            act.wait_ge(er_sub, 1)
            nc.scalar.activation(e_r[:, 1], e_r[:, 0], ACT.Exp).then_inc(er_exp, 1)
            with nc.scalar.Fori(0, B) as b:
                moe_tanh(b)

        @block.tensor
        def _(pe):
            mm = nc.tensor.matmul

            def ln_turn(s, b, dst, place=None, behind=1):
                if s or b >= 2:
                    pe.wait_ge(ln_ht, B * s + b - behind)
                pe.wait_ge(ln_h, B * s + b + 1)
                for t in range(TB):
                    for k in range(KT):
                        ins = nc.tensor.transpose(dst[:, k * S + t * P:k * S + t * P + P],
                                                  HN[:, (TB * b if place is None else place) + t, k * P:k * P + P],
                                                  ident[:, :])
                ins.then_inc(ln_tr, 1)

            pe.wait_ge(ld_cx, 16 * 7)
            for n in range(2):
                mm(bank[n][0:XC, :], wk_T[:, :], ctxT[:, 512 * n:512 * n + 512], start=True, stop=True).then_inc(kvt_mm, 1)
            for t in range(NT):
                ins = mm(bank[3][:, t * XC:t * XC + XC], ctxT[:, t * P:t * P + P], wk_T[:, :], start=True, stop=True)
            ins.then_inc(kvn_mm, 1)

            pe.wait_ge(ld_c, 16)
            for b in range(B):
                ln_turn(0, b, bank[6 + b % 2])
            pe.wait_ge(lat_ok, 1)
            for t in range(NT):
                ins = nc.tensor.transpose(bank[4 + t // 4][:, t % 4 * P:t % 4 * P + P], lat2[:, t, :], ident[:, :])
                if t % 4 == 3:
                    ins.then_inc(lat_mm, 1)
            pe.wait_ge(kvt_ok, 2)
            pe.wait_ge(kvn_ok, 1)
            pe.wait_ge(latT_ok, 2)
            pe.wait_ge(ln_ht, B)
            pe.wait_ge(ld_1, 16 * 5)
            for t in range(NT):
                for k in range(KT):
                    ins = mm(PRB[:, t * H0:t * H0 + H0], HT[:, k, t * P:t * P + P], b_w[:, k, :],
                             start=(k == 0), stop=(k == KT - 1))
            ins.then_inc(bt_mm, 1)

            def project_qk(h, j, after):
                pe.wait_ge(ld_w[j], 16 * (h // 2 + 1) if isinstance(h, int) else 16 * pair[0] + 16)
                for n in range(2):
                    for c in range(2):
                        if n or after:
                            pe.wait_ge(qk_read, 4 * h + 2 * n + c - 1)
                        for k in range(KT):
                            ins = mm(QK[c][:, :], w_head[:, j, k, n * D0:n * D0 + D0], HT[:, k, 512 * c:512 * c + 512],
                                     start=(k == 0), stop=(k == KT - 1))
                        ins.then_inc(qk_mm, 1)

            def project_vg(h, j, after):
                for n in range(4):
                    if n >= 2 or after:
                        pe.wait_ge(vg_read, 4 * h + n - 1)
                    if after and n == 0:
                        pe.wait_ge(ss_read, h)
                    for t in range(2):
                        for k in range(KT):
                            ins = mm(VG[n % 2][:, t, :], HT[:, k, (2 * n + t) * P:(2 * n + t + 1) * P],
                                     w_head[:, j, k, 2 * D0:4 * D0], start=(k == 0), stop=(k == KT - 1))
                    ins.then_inc(vg_mm, 1)

            def norms_scores(h):
                pe.wait_ge(qk_read, 4 * h + 4)
                pe.wait_ge(vg_read, 4 * h + 3)
                for n, sq in enumerate((q2, k2)):
                    for t in range(NT):
                        ins = mm(sumsq[:, n * NT + t:n * NT + t + 1], sq[:, t * P:t * P + P], ones[:, :],
                                 start=True, stop=True)
                ins.then_inc(ss_mm, 1)
                for t in range(NT):
                    ins = mm(SC[t // 4][:, t % 4, :], kT[:, t * P:t * P + P], qT[:, t * P:t * P + P],
                             start=True, stop=True)
                    if t % 4 == 3:
                        ins.then_inc(sc_mm, 1)

            def values(g, after):
                for n in range(2):
                    if after:
                        pe.wait_ge(outT_ok, 2 * g + n - 1)
                    pe.wait_ge(masked, 2 * g + n + 1)
                    for t in range(4 * n, 4 * n + 4):
                        ins = mm(OV[n][:, t % 4, :], attn[:, t, :], v_tok[:, t, :], start=True, stop=True)
                    ins.then_inc(pv_mm, 1)

            def turn_head(g):
                for n in range(2):
                    pe.wait_ge(gated_ok, 2 * g + n + 1)
                    for t in range(4 * n, 4 * n + 4):
                        ins = nc.tensor.transpose(OV[n][:, t % 4, :], gated[:, t, :], ident[:, :])
                    ins.then_inc(tr_mm, 1)

            pe.wait_ge(consts, 1)
            pe.wait_ge(bt_abs, 1)
            project_qk(0, 0, False)
            project_vg(0, 0, False)
            norms_scores(0)
            project_qk(1, 1, True)
            values(0, False)
            project_vg(1, 1, True)
            turn_head(0)
            norms_scores(1)
            with nc.tensor.Fori(1, H0 // 2) as i:
                pair = [i]
                for j in range(2):
                    h = 2 * i + j
                    project_qk(h, j, True)
                    values(h - 1, True)
                    project_vg(h, j, True)
                    turn_head(h - 1)
                    norms_scores(h)
            values(H0 - 1, True)
            turn_head(H0 - 1)

            pe.wait_ge(ld_o, 16)
            pe.wait_ge(outT_ok, 2 * H0)
            for t in range(NT):
                if t >= 2:
                    pe.wait_ge(o_read, t - 1)
                for h in range(H0):
                    ins = mm(bank[t % 2][:, 0:D], outT[:, h, t * P:t * P + P], o_w[:, h, :],
                             start=(h == 0), stop=(h == H0 - 1))
                ins.then_inc(o_mm, 1)
                if t % TB == 0 and t:
                    ln_turn(1, t // TB - 1, bank[6 + (t // TB - 1) % 2])
            ln_turn(1, B - 1, bank[7])

            def context_product(b):
                if b >= 2:
                    pe.wait_ge(xo_ok, b - 1)
                for k in range(KT):
                    ins = mm(XO[b % 2][0:XC, 0:S], kv[:, TB * b + k, :], HT[:, k, b * S:b * S + S],
                             start=(k == 0), stop=(k == KT - 1))
                ins.then_inc(xo_mm, 1)

            def context_similarity(b):
                pe.wait_ge(xo_ok, b + 1)
                if b >= 2:
                    pe.wait_ge(xs_free, b - 1)
                for t in range(TB):
                    ins = mm(XS[b % 2][:, t, :], x_oT[:, b % 2, t * P:t * P + P], kvT[:, b * S:b * S + S],
                             start=True, stop=True)
                ins.then_inc(xs_mm, 1)

            pe.wait_ge(ln_ht, 2 * B)
            for b in range(B + 2):
                if b < B:
                    context_product(b)
                    context_similarity(b)
                if b >= 2:
                    ln_turn(2, b - 2, bank[6 + b % 2])
            def ffn_front(b):
                if b:
                    pe.wait_ge(fh_ok, b)
                for m in range(KT):
                    for k in range(KT):
                        ins = mm(FH[:, m, :], f_w1[:, k, m * P:m * P + P], HT[:, k, b * S:b * S + S],
                                 start=(k == 0), stop=(k == KT - 1))
                ins.then_inc(fh_mm, 1)
                for m in range(FM):
                    if b and m % 2 == 0:
                        pe.wait_ge(fx_ok, 2 * b - 1 + m // 2)
                    for k in range(KT):
                        ins = mm(FX[m // 2][:, m % 2, :], f_v[:, k, m * P:m * P + P], HT[:, k, b * S:b * S + S],
                                 start=(k == 0), stop=(k == KT - 1))
                    if m % 2:
                        ins.then_inc(fx_mm, 1)
                pe.wait_ge(fh_ok, b + 1)
                if b:
                    pe.wait_ge(fa_T, b)
                for t in range(TB):
                    for k in range(KT):
                        ins = mm(FL[:, t, :], f_h[:, k, t * P:t * P + P], f_w2[:, k, :], start=(k == 0), stop=(k == KT - 1))
                ins.then_inc(fl_mm, 1)

            def ffn_back(b):
                pe.wait_ge(fl_al, b + 1)
                for t in range(TB):
                    ins = nc.tensor.transpose(FT[:, t * P:t * P + P], f_al[:, 2, t, :], ident[:, :])
                ins.then_inc(fa_tr, 1)
                pe.wait_ge(fa_T, b + 1)
                for m in range(FM):
                    ins = mm(FA[m // 2][:, m % 2, :], f_sel[:, m, :], f_aT, start=True, stop=True)
                    if m % 2:
                        ins.then_inc(fa_mm, 1)
                pe.wait_ge(fa_ok, 2 * b + 2)
                for t in range(TB):
                    for m in range(FM):
                        ins = mm(FO[:, t, :], f_ax[:, m, t * P:t * P + P], f_u[:, m, :], start=(m == 0), stop=(m == FM - 1))
                ins.then_inc(fo_mm, 1)

            pe.wait_ge(ln_ht, 3 * B)
            pe.wait_ge(ld_3, 16 * 7)
            for b in range(B):
                ffn_front(b)
                if b >= 1:
                    ln_turn(3, b - 1, bank[7], behind=0)
                ffn_back(b)
            ln_turn(3, B - 1, bank[7], behind=0)

            pe.wait_ge(ld_p, 16 * 4)
            pe.wait_ge(fo_read, B)
            pe.wait_ge(ln_ht, 4 * B)
            for n in range(4):
                for h in range(8 * (n % 2), 8 * (n % 2) + 8):
                    ins = mm(bank[n][0:QH, (h % 8) * XC:(h % 8 + 1) * XC], qr_T[:, h, n // 2 * QH:n // 2 * QH + QH], kr_T[:, h, :],
                             start=True, stop=True)
                ins.then_inc(gw_mm, 1)
            for n in range(4):
                for m in range(2 * n, 2 * n + 2):
                    for j in range(2):
                        ins = mm(bank[4 + n][j * XC:j * XC + XC, (m % 2) * D:(m % 2) * D + D], kc_kv[:, 2 * m + j, :], wo_T[:, 2 * m + j, :],
                                 start=True, stop=True)
                ins.then_inc(mw_mm, 1)

            def project(b, after):
                for kind in range(3):
                    if kind == 2:
                        pe.wait_ge(a_ok, 3 * b + 1)
                    dst = AB[kind % 2]
                    for m in range(KT):
                        for k in range(KT):
                            ins = mm(dst[:, m, :], a_w[:, k, kind * D + m * P:kind * D + m * P + P], HT[:, k, ds(b * S, S)],
                                     start=(k == 0), stop=(k == KT - 1))
                    ins.then_inc(a_mm, 1)
                pe.wait_ge(a_ok, 3 * b + 3)
                for t in range(TB):
                    for m in range(KT):
                        ins = nc.tensor.transpose(bank[1][:, t * D + m * P:t * D + m * P + P], a_vT[:, m, t * P:t * P + P], ident[:, :])
                ins.then_inc(av_tr, 1)
                pe.wait_ge(av_ok, b + 1)

            def attend(b, between=None):
                for n in range(H1 + 2):
                    if n < H1:
                        m, g, o = n // 8, n % 8 // 2, n % 2
                        rows = slice(32 * g, 32 * g + 32)
                        if n >= 2:
                            pe.wait_ge(as_exp, H1 * b + n - 1)
                        for t in range(TB):
                            ins = mm(AS[n % 2][:, t, :], a_q[rows, m, t * P:t * P + P], a_k[rows, o, m, :], start=True, stop=True)
                        ins.then_inc(as_mm, 1)
                    if 1 <= n <= H1:
                        pe.wait_ge(as_exp, H1 * b + n)
                        q = n - 1
                        if q >= 2:
                            (pe.wait_ge(at_ev, H1 // 2 * b + q // 2) if q % 2 == 0 else pe.wait_ge(at_od, H1 // 2 * b + q // 2))
                        for t in range(TB):
                            for l in range(TB):
                                ins = nc.tensor.transpose(AT[q % 2][:, 2 * t + l, :], a_p[:, q % 2, t, l * P:l * P + P], ident[:, :])
                        ins.then_inc(at_mm, 1)
                    if n >= 2:
                        q = n - 2
                        (pe.wait_ge(at_ev, H1 // 2 * b + q // 2 + 1) if q % 2 == 0 else pe.wait_ge(at_od, H1 // 2 * b + q // 2 + 1))
                        if q == 0 and between:
                            pe.wait_ge(cn_ok, b)
                        for t in range(TB):
                            for l in range(TB):
                                ins = mm(AV[t][:, q, :], a_pT[:, q % 2, 2 * t + l, :], a_v[:, l, q, :], start=(l == 0), stop=(l == TB - 1))
                ins.then_inc(av_mm, 1)

            def project_out(b):
                pe.wait_ge(cn_ok, b + 1)
                for t in range(TB):
                    for c in range(KT):
                        ins = nc.tensor.transpose(AB[1][:, t, c * P:c * P + P], a_cn[:, t, c * P:c * P + P], ident[:, :])
                ins.then_inc(cn_tr, 1)
                pe.wait_ge(cn_T, b + 1)
                for t in range(TB):
                    for c in range(KT):
                        ins = mm(AB[0][:, t, :], a_cT[:, 2 * t + c, :], a_ow[:, c, :], start=(c == 0), stop=(c == KT - 1))
                ins.then_inc(ao_mm, 1)

            pe.wait_ge(gw_ok, 4)
            pe.wait_ge(mw_ok, 4)
            pe.wait_ge(ld_4, 16 * 7)
            pe.wait_ge(consts, 4)
            project(0, False)
            attend(0)
            with nc.tensor.Fori(1, B) as b:
                project(b, True)
                project_out(b - 1)
                attend(b, True)
                ln_turn(4, b - 1, bank[1], 0, 0)
                pe.wait_ge(ln_ht, 4 * B + b)
                pe.wait_ge(ao_read, b)
            project_out(B - 1)
            ln_turn(4, B - 1, bank[1], 0, 0)

            def head_key(p, q, after):
                j, c = q // 2, q % 2
                if j == 0:
                    pe.wait_ge(ld_w5[0], 16 * p + 16)
                    if after:
                        pe.wait_ge(lut_ok, 2 * p + c - 1)
                else:
                    pe.wait_ge(ld_w5[1], 16 * p + 16)
                    pe.wait_ge(l_q_ok, 4 * p + c + 1)
                for k in range(KT):
                    ins = mm(bank[c][:, :], w5[:, j, k * K2:k * K2 + K2], HT[:, k, 512 * c:512 * c + 512],
                             start=(k == 0), stop=(k == KT - 1))
                ins.then_inc(l_q_mm, 1)

            def head_latent(p, r, after):
                j, c = r // 2, r % 2
                pe.wait_ge(l_q_ok, 4 * p + r + 1)
                if after:
                    pe.wait_ge(lb_rot, 4 * p + r)
                for o in range(2):
                    ins = mm(LR[o][0:QH, :], w5[:, j, 2 * K2 + o * QH:2 * K2 + o * QH + QH], l_q[:, 512 * c:512 * c + 512],
                             start=True, stop=True)
                ins.then_inc(lb_mm, 1)

            def head_query(p, r, after):
                j, c = r // 2, r % 2
                pe.wait_ge(lb_add, 4 * p + r + 1)
                if c == 0 and (after or j):
                    pe.wait_ge(lu_ok, 2 * p + j)
                for t in range(4 * c, 4 * c + 4):
                    for o in range(2):
                        ins = mm(LU[:, t, :], l_rot[:, o, t * P:t * P + P], Gw[:, o, ds(2 * p + j, 1), :].rearrange("p o c -> p (o c)"),
                                 start=(o == 0), stop=(o == 1))
                ins.then_inc(lu_mm, 1)

            def unit_turn(u, after):
                pe.wait_ge(ls_exp, u + 1)
                if after:
                    pe.wait_ge(lt_ok, u)
                for t in range(TB):
                    for l in range(TB):
                        ins = nc.tensor.transpose(LT[:, 2 * t + l, :], l_p[:, t, l * P:l * P + P], ident[:, :])
                ins.then_inc(lt_mm, 1)

            def unit_scores(u, n, after):
                j, b = n // B, n % B
                rows = slice(XC * j, XC * j + XC)
                if after:
                    pe.wait_ge(ls_exp, u)
                for t in range(TB):
                    ins = mm(LS[:, t, :], l_uT[rows, (TB * b + t) * P:(TB * b + t + 1) * P], latT[rows, b * S:b * S + S],
                             start=True, stop=True)
                ins.then_inc(ls_mm, 1)

            def unit_values(u, n, after):
                b = n % B
                pe.wait_ge(lt_ok, u + 1)
                if after:
                    pe.wait_ge(lc_ok, u)
                for t in range(TB):
                    for l in range(TB):
                        ins = mm(LV[:, t, :], l_pT[:, 2 * t + l, :], lat[:, TB * b + l, :], start=(l == 0), stop=(l == TB - 1))
                ins.then_inc(lv_mm, 1)

            def pair(p, make, use, after):
                for k in range(10):
                    if make:
                        if k in (0, 1, 3, 5):
                            head_key(p, (0, 1, 3, 5).index(k), after)
                        if k in (2, 4, 6, 7):
                            r = (2, 4, 6, 7).index(k)
                            head_latent(p, r, after or r)
                        if k in (5, 6, 8):
                            r = (5, 6, 8).index(k)
                            head_query(p, r, after)
                    u = 8 * p - 8 + k
                    if use and k >= 2:
                        unit_turn(u - 2, k > 2 or after > 1)
                    if use and 1 <= k <= 8:
                        if k == 1:
                            pe.wait_ge(lut_ok, 2 * p)
                        unit_scores(u - 1, k - 1, k > 1 or after > 1)
                    if use and k >= 2:
                        unit_values(u - 2, k - 2, k > 2 or after > 1)
                if make:
                    head_query(p, 3, after)
                    pe.wait_ge(lu_ok, 2 * p + 2)
                    pe.wait_ge(l_q_ok, 4 * p + 4)
                    for t in range(NT):
                        ins = nc.tensor.transpose(bank[t // 4][:, t % 4 * P:t % 4 * P + P], l_u[:, t, :], ident[:, :])
                        if t % 4 == 3:
                            ins.then_inc(lut_mm, 1)

            pe.wait_ge(ln_ht, 5 * B)
            pe.wait_ge(ao_read, B)
            pair(0, True, False, 0)
            pair(1, True, True, 1)
            with nc.tensor.Fori(2, H2 // 2) as p:
                pair(p, True, True, 2)
            pair(H2 // 2, False, True, 2)
            for t in range(NT + 1):
                if t < NT:
                    pe.wait_ge(lc_ok, 8 * (H2 // 2 - 1) + 8)
                    for n in range(2):
                        if t:
                            pe.wait_ge(lf_T, 2 * t + n - 1)
                        for m in range(4 * n, 4 * n + 4):
                            ins = nc.tensor.transpose(bank[n][:, m % 4 * P:m % 4 * P + P], l_cn[:, t, m * P:m * P + P], ident[:, :])
                        ins.then_inc(lf_tr, 1)
                if t:
                    q = t - 1
                    pe.wait_ge(lf_T, 2 * q + 2)
                    if q >= 2:
                        pe.wait_ge(lf_read, q - 1)
                    for m in range(8):
                        ins = mm(bank[2 + q % 2][:, 0:D], l_cT[:, q % 2, m, :], Mw[:, m, :], start=(m == 0), stop=(m == 7))
                    ins.then_inc(lf_mm, 1)
                if t >= 4 and t % 2 == 0:
                    b = t // 2 - 2
                    ln_turn(5, b, bank[6 + b % 2])
            ln_turn(5, 3, bank[7])

            def expert_up(b, u, after):
                U = (E6 + SF) * b + u
                if after or u >= 2:
                    pe.wait_ge(eg_ok, U - 1)
                for gu in range(2):
                    for k in range(KT):
                        w = e_gu[:, k, u, gu * I6:gu * I6 + I6] if u < E6 else e_sgu[:, k, gu * SH6 + (u - E6) * P:gu * SH6 + (u - E6) * P + P]
                        ins = mm(EG[u % 2][:, gu, :], w, HT[:, k, ds(b * S, S)], start=(k == 0), stop=(k == KT - 1))
                ins.then_inc(eg_mm, 1)

            def expert_down(b, u, after):
                U = (E6 + SF) * b + u
                pe.wait_ge(eg_ok, U + 1)
                if u < E6:
                    if after or u >= 2:
                        pe.wait_ge(ey_ok, E6 * b + u - 1)
                    for t in range(TB):
                        ins = mm(EY[u % 2][:, t, :], e_act[:, u % 2, t * P:t * P + P], e_dn[:, u, :], start=True, stop=True)
                    ins.then_inc(ey_mm, 1)
                else:
                    f = u - E6
                    if f == 0 and after:
                        pe.wait_ge(x_done, b)
                    for t in range(TB):
                        ins = mm(ES[t][:, 0:D], e_act[:, u % 2, t * P:t * P + P], e_sdn[:, f, :], start=(f == 0), stop=(f == SF - 1))
                    if f == SF - 1:
                        ins.then_inc(es_mm, 1)

            def moe(b, after):
                for u in range(E6 + SF + 1):
                    if u < E6 + SF:
                        expert_up(b, u, after)
                    if u:
                        expert_down(b, u - 1, after)

            pe.wait_ge(ln_ht, 6 * B)
            pe.wait_ge(lf_read, NT)
            for t in range(NT):
                for k in range(KT):
                    ins = mm(EL[:, t, :], HT[:, k, t * P:t * P + P], e_gate[:, k, :], start=(k == 0), stop=(k == KT - 1))
            ins.then_inc(er_mm, 1)
            pe.wait_ge(ld_6, 16 * 4)
            moe(0, False)
            with nc.tensor.Fori(1, B) as b:
                moe(b, True)


def kernel(**inputs):
    import numpy as np
    import concourse.bacc as bacc
    from concourse.bass_utils import run_bass_kernel_spmd

    g = {k: np.asarray(v) for k, v in inputs.items()}
    arrays = lay_out(np, g)
    arrays.update(constants(np))
    nc = bacc.Bacc("TRN2", target_bir_lowering=False, num_devices=1)
    feeds, args = {}, {}
    for name, value in arrays.items():
        value = np.ascontiguousarray(value)
        feeds[f"in_{name}"] = value
        args[name] = nc.dram_tensor(f"in_{name}", value.shape, mybir.dt.from_np(value.dtype), kind="ExternalInput").ap()
    out = nc.dram_tensor("out_x", (B, S, D), F32, kind="ExternalOutput").ap()
    decoder(nc, args, out)
    return run_bass_kernel_spmd(nc, [feeds], core_ids=[0]).results[0]["out_x"]
```

```python
from contextlib import ExitStack, contextmanager

import concourse.bass as bass
from concourse import mybir

F32 = mybir.dt.float32
F32R = mybir.dt.float32r
ALU = mybir.AluOpType
ACT = mybir.ActivationFunctionType
AX_X = mybir.AxisListType.X
ds = bass.ds

P = 128
B, S, D = 4, 256, 256
T = B * S
NT = T // P
KT = D // P
TB = S // P
LN_EPS = 1e-5

H0, D0, CHUNK = 16, 128, 64
NORM_FLOOR = (1e-12 ** 2) * D0

XC = 64
X0_EPS = 1e-6
X0_SCALE = 256 ** -0.5

FK, FR = 8, 64
FM = FK * FR // P

H1, D1 = 16, 16
HM = P // D1
LN_AT = 4

H2, K2, Q2, R2 = 16, 128, 192, 64
QH = Q2 // 2
KEY_AT = (0, 0, 2, 4)
ROT_AT = (1, 3, 5, 7)
LAT_AT = (4, 6, 8)
LAST_AT = 1

E6, I6, SH6 = 8, 128, 512
SF = SH6 // P


WOVEN = [(2, 0), (2, 1), (3, 0), (2, 2), (3, 1), (2, 3), (3, 2), (3, 3)]


def ln_before(s, b):
    return 2 * B + WOVEN.index((s, b)) if s in (2, 3) else B * s + b


class Chain:

    def __init__(self, eng, sem):
        self.eng, self.sem, self.n, self.loop = eng, sem, 0, None

    def value(self):
        if self.loop is None:
            return self.n
        i, first, start, per = self.loop
        return (i - first) * per + self.n

    def __call__(self, ins):
        ins.then_inc(self.sem, 1)
        self.n += 1
        self.eng.wait_ge(self.sem, self.value())

    @contextmanager
    def over(self, i, first, last, per):
        start = self.n
        self.loop = (i, first, start, per)
        yield
        assert self.n == start + per, (self.n - start, per)
        self.n = start + per * (last - first)
        self.loop = None


def lay_out(np, g):
    def tiles(w):
        return w.reshape(-1, P, w.shape[1]).transpose(1, 0, 2)

    heads = np.stack([g[f"L0_attn_{n}_w"].reshape(H0, D0, KT, P).transpose(0, 3, 2, 1)
                      for n in ("q", "k", "v", "og")], axis=3)
    return {
        "x": g["x"],
        "w_head": heads.reshape(H0, P, KT * 4 * D0),
        "qkv_b": np.stack([g[f"L0_attn_{n}_b"].reshape(H0, D0) for n in "qkv"], axis=1).reshape(H0, 3 * D0),
        "o_w": g["L0_attn_o_w"].reshape(D, H0, D0).transpose(2, 1, 0),
        "b_w": tiles(g["L0_attn_b_w"].T),
        "bb": g["L0_attn_b_b"],
        "ob": g["L0_attn_o_b"],
        "ctx": g["ctx_512"].reshape(NT, P, XC).transpose(1, 0, 2),
        "ctxT": g["ctx_512"].reshape(T, XC).T,
        "wk_T": g["L0_xattn_W_k"].T,
        "bk": g["L0_xattn_b_k"].reshape(XC, 1),
        "gam": g["L0_xattn_ln_gamma"],
        "bet": g["L0_xattn_ln_beta"],
        "f_w1": tiles(g["L0_ffn_W1"]),
        "f_b1": g["L0_ffn_b1"].reshape(KT, P).T,
        "f_w2": tiles(g["L0_ffn_W2"]),
        "f_b2": g["L0_ffn_b2"],
        "f_v": tiles(g["L0_ffn_V"].reshape(FK * FR, D).T),
        "f_u": tiles(g["L0_ffn_U"].transpose(0, 2, 1).reshape(FK * FR, D)),
        "a_w": tiles(g["L1_attn_Wqkv_w"].T),
        "a_b": g["L1_attn_Wqkv_b"].reshape(6, P).T,
        "a_ow": tiles(g["L1_attn_out_w"].T),
        "aob": g["L1_attn_out_b"],
        "w5": np.concatenate([g["L1_xattn_Wq"].reshape(H2, K2, KT, P).transpose(0, 3, 2, 1).reshape(H2, P, KT * K2),
                              g["L1_xattn_w_kc_q"]], axis=2),
        "qr_T": g["L1_xattn_W_qr"].transpose(2, 0, 1),
        "kr_T": g["L1_xattn_W_kr"].transpose(2, 0, 1),
        "kc_kv": g["L1_xattn_w_kc_kv"].transpose(1, 0, 2),
        "wo_T": g["L1_xattn_Wo"].reshape(D, H2, K2).transpose(2, 1, 0),
        "e_gate": tiles(g["L1_ffn_w_gate"]),
        "e_gu": g["L1_ffn_w_gate_up"].reshape(E6, KT, P, 2 * I6).transpose(2, 1, 0, 3),
        "e_sgu": tiles(g["L1_ffn_w_sh_gate_up"]),
        "e_dn": g["L1_ffn_w_down"].transpose(1, 0, 2),
        "e_sdn": tiles(g["L1_ffn_w_sh_down"]),
    }


def constants(np):
    i = np.arange(P)
    same = (i[:, None] // CHUNK == i[None, :] // CHUNK) & (i[:, None] <= i[None, :])
    def tables(length, dim):
        inv = np.float32(1.0) / np.float32(10000.0) ** (np.arange(0, dim, 2, dtype=np.float32) / np.float32(dim))
        f = np.arange(length, dtype=np.float32)[:, None] * inv[None, :]
        return np.repeat(np.sin(f), 2, axis=-1), np.repeat(np.cos(f), 2, axis=-1)

    sin_k, cos_k = tables(S, XC)
    sin_k[:, 0:XC // 2] *= -1
    sin_q, cos_q = tables(S, Q2)
    rows = np.arange(P) % 32 // 16
    pick = (np.arange(P)[None, None, :] // FR + 2 * np.arange(FM)[None, :, None] == np.arange(FK)[:, None, None])
    return {
        "cos_k": cos_k.reshape(TB, P, XC).transpose(1, 0, 2),
        "sin_k": sin_k.reshape(TB, P, XC).transpose(1, 0, 2),
        "cos_q": cos_q.T.reshape(2, QH, S).transpose(1, 0, 2),
        "sin_q": sin_q.T.reshape(2, QH, S).transpose(1, 0, 2),
        "f_sel": pick.astype(np.float32),
        "a_par": np.stack([rows == 0, rows == 1], axis=1).astype(np.float32),
        "e_rev": np.arange(E6, 0, -1).astype(np.float32),
        "ident": np.eye(P, dtype=np.float32),
        "mask": (0.5 * same).astype(np.float32),
    }


def decoder(nc, a, out):
    ctx = ExitStack()
    with ctx:
        def sb(name, shape, dt=F32):
            return ctx.enter_context(nc.sbuf_tensor(name, shape, dt))

        def sem(name):
            return ctx.enter_context(nc.semaphore(name))

        bank = [ctx.enter_context(nc.psum_tensor(f"bank{n}", [P, 512], F32)) for n in range(8)]

        X = sb("X", [P, NT, D])
        HN = sb("HN", [P, NT, D])
        HT = sb("HT", [P, KT, T])
        ident = sb("ident", [P, P])
        ones = sb("ones", [P, 1])
        ln_stat = sb("ln_stat", [P, NT, 6])
        ln_mv = sb("ln_mv", [P, NT, 2])
        ln_var = sb("ln_var", [P, NT])
        ln_r = sb("ln_r", [P, NT])
        ln_t = sb("ln_t", [P, NT])
        ln_rstd = sb("ln_rstd", [P, NT])
        ln_none = sb("ln_none", [P, 1])
        half = sb("half", [P, 2 * NT])
        big = sb("big", [P, 16384])
        work = sb("work", [P, 9216])

        o_w = sb("o_w", [P, H0, D])
        b_w = sb("b_w", [P, KT, H0])
        bb_row = sb("bb_row", [P, H0])
        ob_row = sb("ob_row", [P, D])
        mask = sb("mask", [P, P])
        beta = sb("beta", [P, NT, H0])
        bt = work[:, 4 * T:4 * T + 6 * NT * H0].rearrange("p (n c) -> p n c", n=6)
        norm = sb("norm", [P, 4, 2 * NT])
        sumsq = sb("sumsq", [P, 2, 2, NT])
        outT = big[:, :].rearrange("p (h t) -> p h t", h=H0)
        qkT = work[:, 0:2 * T].rearrange("p (n t) -> p n t", n=2)
        qk_tok = work[:, 2 * T:3 * T].rearrange("p (t c) -> p t c", t=4)
        attn = work[:, 3 * T:4 * T].rearrange("p (t i) -> p t i", t=NT)
        v_tok = work[:, 4 * T:6 * T].rearrange("p (j t d) -> p j t d", j=2, t=NT)
        gate = work[:, 6 * T:8 * T].rearrange("p (j t d) -> p j t d", j=2, t=NT)
        tanh_g = work[:, 8 * T:8 * T + 256].rearrange("p (n d) -> p n d", n=2)
        qkv_b = work[:, 8 * T + 256:9 * T].rearrange("p (j c) -> p j c", j=2)
        gated = HN[:, 0:NT // 2, :].rearrange("p (t o) d -> p t o d", t=NT // 2).rearrange("p t o (u d) -> p (t o u) d", u=2)
        w_new = HN[:, NT // 2:NT, :].rearrange("p t d -> p (t d)")
        sq_out = sb("sq_out", [P, 2, D0])
        PJ = bank[0:3]
        TQ = bank[3][:, :].rearrange("p (n t) -> p n t", n=2)
        SC = [b[:, :].rearrange("p (t i) -> p t i", t=4) for b in bank[4:6]]
        OV = [b[:, :].rearrange("p (t d) -> p t d", t=4) for b in bank[6:8]]
        PRB = bank[4][:, 0:NT * H0]


        ctx_tok = work[:, 3 * T:3 * T + NT * XC].rearrange("p (t c) -> p t c", t=NT)
        ctxT = work[0:XC, 2 * T:3 * T]
        wk_T = sb("wk_T", [XC, XC])
        bk_col = sb("bk_col", [XC, 1])
        bk_row = sb("bk_row", [P, XC])
        kvT = sb("kvT", [XC, T])
        kv = sb("kv", [P, NT, XC])
        cos_k = work[:, 0:2 * XC].rearrange("p (t c) -> p t c", t=TB)
        sin_k = work[:, 2 * XC:4 * XC].rearrange("p (t c) -> p t c", t=TB)
        rot_k = work[:, 4 * XC:4 * XC + NT * XC].rearrange("p (t c) -> p t c", t=NT)
        lat2 = work[:, T:2 * T].rearrange("p (t c) -> p t c", t=NT)
        lat = sb("lat", [P, NT, XC])
        latT = sb("latT", [P, T])

        x_sim = work[:, 0:1024].rearrange("p (n t j) -> p n t j", n=2, t=TB)
        x_e = work[:, 1024:2048].rearrange("p (n t j) -> p n t j", n=2, t=TB)
        x_oT = work[0:XC, 2048:2560].rearrange("p (n i) -> p n i", n=2)
        x_stat = sb("x_stat", [P, TB, 6])
        x_mv = sb("x_mv", [P, TB, 2])
        x_v = sb("x_v", [P, 4, TB])
        x_nm = sb("x_nm", [P, 2, TB])
        x_sum = sb("x_sum", [P, 2, TB])
        x_rc = sb("x_rc", [P, TB])
        XO = bank[4]
        XS = bank[5][:, :].rearrange("p (t j) -> p t j", t=TB)

        f_b1 = sb("f_b1", [P, KT])
        f_w2 = sb("f_w2", [P, KT, FK])
        f_b2 = sb("f_b2", [P, FK])
        f_h = work[:, 2560:3072].rearrange("p (m t) -> p m t", m=KT)
        f_vx = work[:, 3072:4096].rearrange("p (m t) -> p m t", m=FM)
        f_ax = work[:, 4096:5120].rearrange("p (m t) -> p m t", m=FM)
        f_aT = work[0:FK, 5120:5376]
        f_al = sb("f_al", [P, 4, TB, FK])
        f_st = sb("f_st", [P, 3, TB])
        FH = bank[0][:, :].rearrange("p (m t) -> p m t", m=KT)
        FL = bank[1][:, 0:TB * FK].rearrange("p (t k) -> p t k", t=TB)
        FT = bank[1][0:FK, 0:S]
        FA = [b[:, :].rearrange("p (m t) -> p m t", m=2) for b in bank[2:4]]
        FX = FA
        FO = bank[0][:, :].rearrange("p (t d) -> p t d", t=TB)

        wo_T = o_w[:, :, :]
        Mw = o_w[:, 0:H2 // 2, :]
        WP = bank[6]
        kc_kv = big[:, 8192:8192 + H2 * XC].rearrange("p (h c) -> p h c", h=H2)
        qr_T = big[0:R2, 9216:9216 + H2 * Q2].rearrange("p (h q) -> p h q", h=H2)
        kr_T = big[0:R2, 12288:12288 + H2 * XC].rearrange("p (h c) -> p h c", h=H2)

        a_b = sb("a_b", [P, 6])
        a_bs = sb("a_bs", [P, 6])
        a_par = sb("a_par", [P, 2])
        aob_row = sb("aob_row", [P, D])
        a_q = work[:, 0:512].rearrange("p (m t) -> p m t", m=KT)
        a_k = work[:, 512:1536].rearrange("p (o m t) -> p o m t", o=2, m=KT)
        a_vT = work[:, 1536:2048].rearrange("p (m t) -> p m t", m=KT)
        a_v = work[:, 2048:2048 + TB * H1 * P].rearrange("p (l h c) -> p l h c", l=TB, h=H1)
        a_vd = [work[:, 2048 + n * HM * P:2048 + n * HM * P + HM * (P + D1)].rearrange("p (h c) -> p h c", h=HM)[:, :, 0:D1]
                for n in range(TB * KT)]
        a_p = work[:, 6272:7808].rearrange("p (n t s) -> p n t s", n=3, t=TB)
        a_cT = HN[:, TB:2 * TB, :]
        a_pT = HN[:, 2 * TB:4 * TB, :].rearrange("p (n l) t -> p n l t", n=2)
        a_nm = sb("a_nm", [P, 3, TB])
        a_sum = sb("a_sum", [P, 3, TB])
        a_rc = sb("a_rc", [P, 3, TB])
        AS = [b[:, :].rearrange("p (t s) -> p t s", t=TB) for b in (bank[2], bank[3], bank[0])]
        AT = [b[:, :].rearrange("p (l t) -> p l t", l=TB) for b in bank[4:6]]
        AC = bank[6:8]
        AB = [b[:, :].rearrange("p (m t) -> p m t", m=KT) for b in bank[0:2]]

        l_q = work[:, 0:1024]
        l_rot = work[0:QH, 1024:3072].rearrange("p (o t) -> p o t", o=2)
        l_pr = work[0:QH, 3072:5120].rearrange("p (n t) -> p n t", n=4)
        l_p = work[:, 6144:7168].rearrange("p (n t l) -> p n t l", n=2, t=TB)
        l_pT = work[:, 7680:8192].rearrange("p (l t) -> p l t", l=TB)
        l_cT = big[:, 8192:16384].rearrange("p (m t) -> p m t", m=H2 // 2)
        g_now = work[0:QH, 8192:8192 + 8 * XC].rearrange("p (o j n c) -> p o j n c", o=2, j=2, n=2)
        l_nm = sb("l_nm", [P, 2, TB])
        l_sum = sb("l_sum", [P, 2, TB])
        l_rc = sb("l_rc", [P, 2, TB])
        LR = bank[2:4]
        LU = bank[4]
        LS = bank[5][:, :].rearrange("p (t l) -> p t l", t=TB)
        LT = bank[6][:, :].rearrange("p (l t) -> p l t", l=TB)
        LC = bank[7][:, :].rearrange("p (n t) -> p n t", n=2)

        e_gate = sb("e_gate", [P, KT, E6])
        e_rev = sb("e_rev", [P, E6])
        e_gu = big[:, 0:4096].rearrange("p (k e f) -> p k e f", k=KT, e=E6)
        e_sgu = big[:, 4096:6144].rearrange("p (k f) -> p k f", k=KT)
        e_dn = big[:, 6144:8192].rearrange("p (e d) -> p e d", e=E6)
        e_r = work[:, 4096:4096 + 6 * NT * E6].rearrange("p (n t e) -> p n t e", n=6, t=NT)
        e_s = sb("e_s", [P, 6, NT])
        e_comb = sb("e_comb", [P, NT, E6])
        e_th = work[:, 2048:2560].rearrange("p (n t) -> p n t", n=2)
        e_sg = work[:, 2560:3072].rearrange("p (n t) -> p n t", n=2)
        e_act = work[:, 3072:3584].rearrange("p (n t) -> p n t", n=2)
        EG = [b[:, :].rearrange("p (g t) -> p g t", g=2) for b in bank[0:2]]
        EY = [b[:, :].rearrange("p (t d) -> p t d", t=TB) for b in bank[2:4]]
        ES = bank[4:6]
        EL = bank[6][:, 0:NT * E6].rearrange("p (t e) -> p t e", t=NT)

        def passing(stack, name, shape, dt=F32):
            return stack.enter_context(nc.sbuf_tensor(name, shape, dt))

        with ExitStack() as early:
            H_hi, H_lo = passing(early, "H_hi", [P, KT, T], F32R), passing(early, "H_lo", [P, KT, T], F32R)
            W_hi, W_lo = [passing(early, n, [P, 2, KT, 4 * D0], F32R) for n in ("W_hi", "W_lo")]

        w5 = sb("w5", [P, 2, KT * K2 + Q2])
        e_sdn = sb("e_sdn", [P, SF, D])
        cos_q = sb("cos_q", [QH, 2, S])
        sin_q = sb("sin_q", [QH, 2, S])
        Gw = sb("Gw", [QH, 2, H2, XC])

        with ExitStack() as mid:
            f_wvu = passing(mid, "f_wvu", [P, 2048])
            gam_row = passing(mid, "gam_row", [P, S])
            bet_row = passing(mid, "bet_row", [P, S])
            f_w1 = passing(mid, "f_w1", [P, KT, D])
            f_sel = passing(mid, "f_sel", [FK, FM, P])
            a_w = passing(mid, "a_w", [P, KT, 3 * D])
            a_ow = passing(mid, "a_ow", [P, KT, D])
        f_v = f_wvu[:, 0:1024].rearrange("p (k c) -> p k c", k=KT)
        f_u = f_wvu[:, 1024:2048].rearrange("p (m d) -> p m d", m=FM)
        with ExitStack() as late:
            l_u = passing(late, "l_u", [P, 2, T], F32R)
            lat_hi, lat_lo = passing(late, "lat_hi", [P, T], F32R), passing(late, "lat_lo", [P, T], F32R)

        ld_x = [sem(f"ld_x{b}") for b in range(B)]
        ld_c = sem("ld_c")
        ld_1 = sem("ld_1")
        ld_w = sem("ld_w")
        ld_b = [sem(f"ld_b{j}") for j in range(2)]
        h_hi = sem("h_hi")
        h_lo = sem("h_lo")
        w_hi = sem("w_hi")
        w_lo = sem("w_lo")
        ld_o = sem("ld_o")
        dve = sem("dve")
        act_own = sem("act_own")
        pool_own = sem("pool_own")
        consts = sem("consts")
        ln_ve = sem("ln_ve")
        ln_pw = sem("ln_pw")
        ln_h = sem("ln_h")
        ln_tr = sem("ln_tr")
        ln_ht = sem("ln_ht")
        x_bias = sem("x_bias")
        bt_mm = sem("bt_mm")
        bt_abs = sem("bt_abs")
        bt_exp = sem("bt_exp")
        bt_w = sem("bt_w")
        bt_ln = sem("bt_ln")
        pj_mm = sem("pj_mm")
        tanh_done = sem("tanh_done")
        qkv_ok = sem("qkv_ok")
        pj_read = sem("pj_read")
        sq_ok = sem("sq_ok")
        ss_read = sem("ss_read")
        ss_pow = sem("ss_pow")
        tq_mm = sem("tq_mm")
        tq_ok = sem("tq_ok")
        sc_mm = sem("sc_mm")
        masked = sem("masked")
        pv_mm = sem("pv_mm")
        gated_ok = sem("gated_ok")
        tr_mm = sem("tr_mm")
        outT_ok = sem("outT_ok")
        o_mm = sem("o_mm")
        o_read = sem("o_read")
        ld_cx = sem("ld_cx")
        ld_2 = sem("ld_2")
        ld_3 = sem("ld_3")
        ld_4 = sem("ld_4")
        ld_p = sem("ld_p")
        ld_t = sem("ld_t")
        ld_6 = sem("ld_6")
        ld_7 = sem("ld_7")
        kvt_mm = sem("kvt_mm")
        kvt_ok = sem("kvt_ok")
        kvn_mm = sem("kvn_mm")
        kvn_ok = sem("kvn_ok")
        lat_ok = sem("lat_ok")
        lat_mm = sem("lat_mm")
        latT_ok = sem("latT_ok")
        xo_mm = sem("xo_mm")
        xo_ok = sem("xo_ok")
        xs_mm = sem("xs_mm")
        xs_ve = sem("xs_ve")
        xs_pw = sem("xs_pw")
        xs_nm = sem("xs_nm")
        xs_exp = sem("xs_exp")
        xs_free = sem("xs_free")
        fh_mm = sem("fh_mm")
        fh_ok = sem("fh_ok")
        fx_mm = sem("fx_mm")
        fx_ok = sem("fx_ok")
        fl_mm = sem("fl_mm")
        fl_ex = sem("fl_ex")
        fl_al = sem("fl_al")
        fl_e = sem("fl_e")
        fa_tr = sem("fa_tr")
        fa_T = sem("fa_T")
        fa_mm = sem("fa_mm")
        fa_ok = sem("fa_ok")
        fo_mm = sem("fo_mm")
        fo_read = sem("fo_read")
        wp_mm = sem("wp_mm")
        wp_ok = sem("wp_ok")
        a_mm = sem("a_mm")
        a_ok = sem("a_ok")
        av_tr = sem("av_tr")
        av_ok = sem("av_ok")
        as_mm = sem("as_mm")
        as_nm = sem("as_nm")
        as_exp = sem("as_exp")
        at_mm = sem("at_mm")
        at_ev = sem("at_ev")
        at_od = sem("at_od")
        as_rc = sem("as_rc")
        ap_ok = sem("ap_ok")
        ac_mm = sem("ac_mm")
        ac_T = sem("ac_T")
        ao_mm = sem("ao_mm")
        ao_read = sem("ao_read")
        l_q_mm = sem("l_q_mm")
        l_q_ok = sem("l_q_ok")
        lb_mm = sem("lb_mm")
        lb_rot = sem("lb_rot")
        lb_add = sem("lb_add")
        g_ok = sem("g_ok")
        lat_r = sem("lat_r")
        lu_mm = sem("lu_mm")
        lu_hi = sem("lu_hi")
        lu_ok = sem("lu_ok")
        ls_mm = sem("ls_mm")
        ls_nm = sem("ls_nm")
        ls_exp = sem("ls_exp")
        lt_mm = sem("lt_mm")
        lt_ok = sem("lt_ok")
        lv_mm = sem("lv_mm")
        lp_ok = sem("lp_ok")
        lc_ok = sem("lc_ok")
        lf_mm = sem("lf_mm")
        lf_read = sem("lf_read")
        er_mm = sem("er_mm")
        er_sub = sem("er_sub")
        er_exp = sem("er_exp")
        eg_mm = sem("eg_mm")
        eg_th = sem("eg_th")
        eg_ok = sem("eg_ok")
        ey_mm = sem("ey_mm")
        ey_ok = sem("ey_ok")
        es_mm = sem("es_mm")
        x_done = sem("x_done")
        ld_w5 = [sem(f"ld_w5{j}") for j in range(2)]
        s_out = sem("s_out")

        block = ctx.enter_context(nc.Block())

        xv = a["x"].rearrange("b (t p) d -> p (b t) d", p=P)
        ov = out.rearrange("b (t p) d -> p (b t) d", p=P)

        @block.sync
        def _(sp):
            for b in range(B):
                sp.dma_start(X[:, TB * b:TB * b + TB, :], xv[:, TB * b:TB * b + TB, :]).then_inc(ld_x[b], 16)
                if b == 0:
                    sp.dma_start(ident[:, :], a["ident"]).then_inc(ld_c, 16)
            for dst, src in ((ctxT, "ctxT"), (wk_T[:, :], "wk_T"), (bk_col[:, :], "bk"), (ctx_tok, "ctx"),
                             (cos_k, "cos_k"), (sin_k, "sin_k")):
                sp.dma_start(dst, a[src]).then_inc(ld_cx, 16)
            sp.dma_start(bk_row[:, :], a["bk"].rearrange("c o -> (c o)").partition_broadcast(P)).then_inc(ld_cx, 16)
            for dst, src in ((b_w, "b_w"), (mask, "mask")):
                sp.dma_start(dst[:], a[src]).then_inc(ld_1, 16)
            for dst, src in ((bb_row, "bb"), (ob_row, "ob")):
                sp.dma_start(dst[:, :], a[src].partition_broadcast(P)).then_inc(ld_1, 16)
            sp.wait_ge(ln_tr, B)
            sp.dma_start(w_new, a["w_head"][0]).then_inc(ld_w, 16)
            for j in range(2):
                sp.dma_start(qkv_b[:, j], a["qkv_b"][j].partition_broadcast(P)).then_inc(ld_b[j], 16)
            sp.wait_ge(w_lo, 1)
            sp.dma_start(w_new, a["w_head"][1]).then_inc(ld_w, 16)
            sp.dma_start(o_w[:], a["o_w"]).then_inc(ld_o, 16)
            with nc.sync.Fori(1, H0 // 2) as i:
                for j in range(2):
                    sp.wait_ge(w_lo, 2 * i + j)
                    sp.dma_start(w_new, a["w_head"][2 * i + j]).then_inc(ld_w, 16)
                    sp.wait_ge(qkv_ok, 2 * NT * i - NT + NT * j)
                    sp.dma_start(qkv_b[:, j], a["qkv_b"][2 * i + j].partition_broadcast(P)).then_inc(ld_b[j], 16)
            sp.wait_ge(pj_mm, NT * H0)
            for dst, src in ((gam_row, "gam"), (bet_row, "bet")):
                sp.dma_start(dst[:, :], a[src].partition_broadcast(P)).then_inc(ld_2, 16)
            for dst, src in ((f_w1[:], "f_w1"), (f_b1[:], "f_b1"), (f_w2[:], "f_w2"), (f_sel[:], "f_sel"), (f_v, "f_v"), (f_u, "f_u")):
                sp.dma_start(dst, a[src]).then_inc(ld_3, 16)
            sp.dma_start(f_b2[:, :], a["f_b2"].partition_broadcast(P)).then_inc(ld_3, 16)
            for dst, src in ((a_w, "a_w"), (a_b, "a_b"), (a_par, "a_par"), (a_ow, "a_ow"), (e_gate, "e_gate")):
                sp.dma_start(dst[:], a[src]).then_inc(ld_4, 16)
            for dst, src in ((aob_row, "aob"), (e_rev, "e_rev")):
                sp.dma_start(dst[:, :], a[src].partition_broadcast(P)).then_inc(ld_4, 16)
            sp.wait_ge(o_mm, NT)
            for dst, src in ((wo_T, "wo_T"), (kc_kv, "kc_kv"), (qr_T, "qr_T"), (kr_T, "kr_T")):
                sp.dma_start(dst, a[src]).then_inc(ld_p, 16)
            for dst, src in ((cos_q, "cos_q"), (sin_q, "sin_q")):
                sp.dma_start(dst[:], a[src]).then_inc(ld_t, 16)
            for j in range(2):
                sp.dma_start(w5[:, j, :], a["w5"][j]).then_inc(ld_w5[j], 16)
            for dst, src in ((e_gu, "e_gu"), (e_sgu, "e_sgu"), (e_dn, "e_dn"), (e_sdn[:], "e_sdn")):
                sp.dma_start(dst, a[src]).then_inc(ld_6, 16)
            with nc.sync.Fori(1, H2 // 2) as p:
                for j in range(2):
                    sp.wait_ge(lb_mm, 4 * p - 2 + 2 * j)
                    sp.dma_start(w5[:, j, :], a["w5"][2 * p + j]).then_inc(ld_w5[j], 16)
            for b in range(B):
                sp.wait_ge(x_done, b + 1)
                sp.dma_start(ov[:, TB * b:TB * b + TB, :], X[:, TB * b:TB * b + TB, :]).then_inc(s_out, 16)
            sp.wait_ge(s_out, 16 * B)

        @block.gpsimd
        def _(pool):
            nc.gpsimd.memset(ones[:, :], 1.0)
            nc.gpsimd.memset(half[:, :], -0.5).then_inc(consts, 1)
            pool.wait_ge(consts, 1)

            def ln_power(s, b, place=None):
                at = TB * b if place is None else place
                pool.wait_ge(ln_ve, ln_before(s, b) + 1)
                nc.gpsimd.tensor_tensor(ln_r[:, at:at + TB], ln_var[:, at:at + TB], half[:, 0:TB],
                                        ALU.pow).then_inc(ln_pw, 1)

            for b in range(B):
                ln_power(0, b)
            for b in range(B):
                pool.wait_ge(h_hi, b + 1)
                nc.gpsimd.tensor_tensor(H_lo[:, :, b * S:b * S + S], HT[:, :, b * S:b * S + S],
                                        H_hi[:, :, b * S:b * S + S].bitcast(F32), ALU.subtract).then_inc(h_lo, 1)

            def weights_lo(h, j, after):
                pool.wait_ge(w_hi, h + 1)
                nc.gpsimd.tensor_tensor(W_lo[:, j].rearrange("p k c -> p (k c)"), w_new,
                                        W_hi[:, j].bitcast(F32).rearrange("p k c -> p (k c)"), ALU.subtract).then_inc(w_lo, 1)

            weights_lo(0, 0, False)
            pool.wait_ge(ln_h, B)
            pool.wait_ge(ld_1, 16 * 4)
            nc.gpsimd.tensor_tensor(X[:, :, :], X[:, :, :], ob_row[:, :].unsqueeze(1).broadcast_to([P, NT, D]),
                                    ALU.add).then_inc(x_bias, 1)

            def norm_power(h):
                pool.wait_ge(ss_read, h + 1)
                nc.gpsimd.tensor_tensor(norm[:, 1, :], norm[:, 0, :], half[:, :], ALU.pow).then_inc(ss_pow, 1)

            weights_lo(1, 1, False)
            norm_power(0)
            with nc.gpsimd.Fori(1, H0 // 2) as i:
                for j in range(2):
                    weights_lo(2 * i + j, j, True)
                    norm_power(2 * i + j - 1)
            norm_power(H0 - 1)
            def similarity_power(b):
                pool.wait_ge(xs_ve, b + 1)
                nc.gpsimd.tensor_tensor(x_v[:, 1, :], x_v[:, 0, :], half[:, 0:TB], ALU.pow).then_inc(xs_pw, 1)

            for b in range(B):
                ln_power(1, b)
                if b >= 2:
                    similarity_power(b - 2)
            for n in range(1, B + 2):
                if n <= B:
                    ln_power(2, n - 1)
                if n + 1 < B:
                    similarity_power(n + 1)
                if n >= 2:
                    ln_power(3, n - 2)
            pool.wait_ge(fo_read, B)
            nc.gpsimd.memset(work[:, 2048:6272], 0.0).then_inc(consts, 1)
            pool.wait_ge(ln_h, 4 * B)
            pool.wait_ge(ld_4, 16 * 7)
            nc.gpsimd.tensor_tensor(X[:, :, :], X[:, :, :], aob_row[:, :].unsqueeze(1).broadcast_to([P, NT, D]),
                                    ALU.add).then_inc(x_bias, 1)

            def normalise(b, n):
                pool.wait_ge(as_rc, H1 * b + n + 1)
                nc.gpsimd.tensor_tensor(a_p[:, n % 3], a_p[:, n % 3],
                                        a_rc[:, n % 3, :].unsqueeze(2).broadcast_to([P, TB, S]), ALU.mult).then_inc(ap_ok, 1)

            for n in range(H1):
                normalise(0, n)
            with nc.gpsimd.Fori(1, B) as b:
                for n in range(H1):
                    if n == LN_AT:
                        ln_power(4, b - 1, 0)
                    normalise(b, n)
            ln_power(4, B - 1, 0)
            def rotate_sum(r, c, after):
                if after:
                    pool.wait_ge(lu_mm, r - 1)
                pool.wait_ge(lb_rot, 2 * r + 2)
                cols = slice(512 * c, 512 * c + 512)
                nc.gpsimd.tensor_tensor(l_rot[:, 0, cols], l_pr[:, 0, :], l_pr[:, 1, :], ALU.subtract)
                nc.gpsimd.tensor_tensor(l_rot[:, 1, cols], l_pr[:, 2, :], l_pr[:, 3, :], ALU.add).then_inc(lb_add, 1)

            def pair_sums(p, use):
                if use:
                    pool.wait_ge(lu_mm, 4 * p)
                for n in range(2):
                    ins = nc.gpsimd.tensor_copy(g_now[:, :, :, n, :], Gw[:, :, ds(2 * p, 2), :])
                ins.then_inc(g_ok, 1)
                for r in range(4):
                    rotate_sum(4 * p + r, r % 2, use or r >= 2)

            pair_sums(0, False)
            pool.wait_ge(lat_r, 1)
            nc.gpsimd.tensor_tensor(lat_lo[:, :], latT[:, :], lat_hi[:, :].bitcast(F32), ALU.subtract).then_inc(lat_r, 1)
            with nc.gpsimd.Fori(1, H2 // 2) as p:
                pair_sums(p, True)
            for b in range(B):
                ln_power(5, b)

        @block.vector
        def _(v):
            link = Chain(v, dve)

            def ln_rows(s, b, place=None):
                at = TB * b if place is None else place
                two = slice(at, at + TB)
                for i in range(TB):
                    ins = nc.vector.bn_stats(ln_stat[:, at + i, :], X[:, ds(TB * b + i, 1), :].rearrange("p o c -> p (o c)"))
                link(ins)
                if place is not None:
                    nc.vector.memset(ln_none[:, :], 0.0)
                for i in range(TB):
                    ins = nc.vector.bn_aggr(ln_mv[:, at + i, :], ln_stat[:, at + i, :])
                link(ins)
                nc.vector.tensor_scalar(ln_var[:, two], ln_mv[:, two, 1], LN_EPS, None, ALU.add).then_inc(ln_ve, 1)
                v.wait_ge(ln_pw, ln_before(s, b) + 1)
                link(nc.vector.scalar_tensor_tensor(out=ln_t[:, two], in0=ln_r[:, two], scalar=-0.5, in1=ln_r[:, two],
                                                    op0=ALU.mult, op1=ALU.mult))
                link(nc.vector.tensor_tensor(ln_t[:, two], ln_t[:, two], ln_var[:, two], ALU.mult))
                link(nc.vector.scalar_tensor_tensor(out=ln_rstd[:, two], in0=ln_t[:, two], scalar=1.5, in1=ln_r[:, two],
                                                    op0=ALU.add, op1=ALU.mult))
                for i in range(TB):
                    ins = nc.vector.tensor_scalar(HN[:, at + i:at + i + 1, :], X[:, ds(TB * b + i, 1), :],
                                                  ln_mv[:, at + i, 0:1], ln_rstd[:, at + i:at + i + 1],
                                                  ALU.subtract, ALU.mult)
                ins.then_inc(ln_h, 1)

            for b in range(B):
                v.wait_ge(ld_x[b], 16)
                ln_rows(0, b)

            v.wait_ge(ld_cx, 16 * 7)
            hf = XC // 2
            for b in range(B):
                two = slice(TB * b, TB * b + TB)
                nc.vector.tensor_tensor(rot_k[:, two, 0:hf], ctx_tok[:, two, hf:XC], sin_k[:, :, 0:hf], ALU.mult)
                nc.vector.tensor_tensor(rot_k[:, two, hf:XC], ctx_tok[:, two, 0:hf], sin_k[:, :, hf:XC], ALU.mult)
                ins = nc.vector.tensor_tensor(lat[:, two, :], ctx_tok[:, two, :], cos_k, ALU.mult)
            link(ins)
            link(nc.vector.tensor_tensor(lat[:, :, :], lat[:, :, :], rot_k, ALU.add))
            for j in range(2):
                ins = nc.vector.tensor_copy(lat2[:, :, j * XC:j * XC + XC], lat[:, :, :])
            ins.then_inc(lat_ok, 1)
            v.wait_ge(kvn_mm, 1)
            nc.vector.tensor_tensor(kv[:, :, :], bank[3][:, :].rearrange("p (t c) -> p t c", t=NT),
                                    bk_row[:, :].unsqueeze(1).broadcast_to([P, NT, XC]), ALU.add).then_inc(kvn_ok, 1)

            z, m, u, w, lw, c = [bt[:, n, :] for n in range(6)]
            v.wait_ge(bt_mm, 1)
            v.wait_ge(ld_1, 16 * 4)
            link(nc.vector.tensor_tensor(z.rearrange("p (t h) -> p t h", t=NT), PRB.rearrange("p (t h) -> p t h", t=NT),
                                         bb_row[:, :].unsqueeze(1).broadcast_to([P, NT, H0]), ALU.add))
            link(nc.vector.tensor_scalar(m, z, -1.0, None, ALU.mult))
            nc.vector.tensor_tensor(c, z, m, ALU.max).then_inc(bt_abs, 1)
            v.wait_ge(bt_abs, 1)
            v.wait_ge(bt_exp, 1)
            nc.vector.tensor_scalar(w, u, 1.0, None, ALU.add).then_inc(bt_w, 1)
            v.wait_ge(bt_w, 1)
            link(nc.vector.tensor_scalar(c, w, -1.0, None, ALU.add))
            link(nc.vector.tensor_tensor(c, u, c, ALU.subtract))
            link(nc.vector.reciprocal(m, w))
            link(nc.vector.tensor_tensor(c, c, m, ALU.mult))
            link(nc.vector.tensor_scalar(m, z, 0.0, None, ALU.max))
            link(nc.vector.tensor_tensor(c, c, m, ALU.add))
            v.wait_ge(bt_ln, 1)
            link(nc.vector.tensor_tensor(beta[:, :, :].rearrange("p t h -> p (t h)"), c, lw, ALU.add))

            def norms_of(g, j):
                v.wait_ge(sq_ok, NT * g + NT)
                nc.vector.tensor_scalar(norm[:, 0, :], sumsq[:, j].rearrange("p n t -> p (n t)"), NORM_FLOOR, None, ALU.max).then_inc(ss_read, 1)

            def scale_of(g):
                v.wait_ge(ss_pow, g + 1)
                link(nc.vector.scalar_tensor_tensor(out=norm[:, 2, :], in0=norm[:, 1, :], scalar=-0.5,
                                                    in1=norm[:, 1, :], op0=ALU.mult, op1=ALU.mult))
                link(nc.vector.tensor_tensor(norm[:, 2, :], norm[:, 2, :], norm[:, 0, :], ALU.mult))
                link(nc.vector.scalar_tensor_tensor(out=norm[:, 3, :], in0=norm[:, 2, :], scalar=1.5,
                                                    in1=norm[:, 1, :], op0=ALU.add, op1=ALU.mult))
                link(nc.vector.tensor_tensor(norm[:, 3, NT:2 * NT], norm[:, 3, NT:2 * NT],
                                             beta[:, :, ds(g, 1)].rearrange("p t o -> p (t o)"), ALU.mult))

            def mask_scores(g, n):
                v.wait_ge(sc_mm, 2 * g + n + 1)
                for t in range(4 * n, 4 * n + 4):
                    ins = nc.vector.scalar_tensor_tensor(out=attn[:, t, :], in0=SC[n][:, t % 4, :],
                                                         scalar=norm[:, 3, NT + t:NT + t + 1], in1=mask[:, :],
                                                         op0=ALU.mult, op1=ALU.mult)
                ins.then_inc(masked, 1)

            def gate_out(g, j, n, after):
                if after and n == 0:
                    v.wait_ge(tr_mm, 2 * g)
                v.wait_ge(pv_mm, 2 * g + n + 1)
                for t in range(4 * n, 4 * n + 4):
                    ins = nc.vector.scalar_tensor_tensor(out=gated[:, t, :], in0=OV[n][:, t % 4, :],
                                                         scalar=norm[:, 3, t:t + 1], in1=gate[:, j, t, :],
                                                         op0=ALU.mult, op1=ALU.mult)
                ins.then_inc(gated_ok, 1)

            def take_tile(h, j, t, after, bias_after):
                if t == 0:
                    v.wait_ge(ld_b[j], 16 * bias_after + 16)
                    if after > 1:
                        v.wait_ge(gated_ok, 2 * h - 2)
                if after or t >= 4:
                    v.wait_ge(tq_mm, 4 * h + (t - 4) // 2 + 1)
                    v.wait_ge(sq_ok, NT * h + t - 3)
                v.wait_ge(tanh_done, NT * h + t + 1)
                nc.vector.tensor_tensor(qk_tok[:, t % 4, :], PJ[t % 3][:, 0:2 * D0], qkv_b[:, j, 0:2 * D0], ALU.add)
                nc.vector.tensor_tensor(v_tok[:, j, t, :], PJ[t % 3][:, 2 * D0:3 * D0], qkv_b[:, j, 2 * D0:3 * D0],
                                        ALU.add).then_inc(qkv_ok, 1)
                nc.vector.scalar_tensor_tensor(out=gate[:, j, t, :], in0=tanh_g[:, t % 2], scalar=1.0,
                                               in1=PJ[t % 3][:, 3 * D0:4 * D0], op0=ALU.add,
                                               op1=ALU.mult).then_inc(pj_read, 1)

            def head_rows(h, j, after, pairs):
                for t in range(NT):
                    take_tile(h, j, t, after, pairs)
                    if after and t == 0:
                        norms_of(h - 1, 1 - j)
                    if after and t == 2:
                        scale_of(h - 1)
                        mask_scores(h - 1, 0)
                    if after and t == 3:
                        mask_scores(h - 1, 1)
                    if after and t in (6, 7):
                        gate_out(h - 1, 1 - j, t - 6, after > 1)

            head_rows(0, 0, 0, 0)
            head_rows(1, 1, 1, 0)
            with nc.vector.Fori(1, H0 // 2) as i, link.over(i, 1, H0 // 2, 8):
                for j in range(2):
                    head_rows(2 * i + j, j, 2, i)
            v.wait_ge(gated_ok, 2 * H0 - 2)
            norms_of(H0 - 1, 1)
            scale_of(H0 - 1)
            for n in range(2):
                mask_scores(H0 - 1, n)
            for n in range(2):
                gate_out(H0 - 1, 1, n, True)

            def similarity(b):
                n = b % 2
                v.wait_ge(xs_mm, b + 1)
                if b >= 2:
                    v.wait_ge(xs_exp, b - 1)
                for t in range(TB):
                    ins = nc.vector.bn_stats(x_stat[:, t, :], XS[:, t, :])
                link(ins)
                for t in range(TB):
                    ins = nc.vector.bn_aggr(x_mv[:, t, :], x_stat[:, t, :])
                link(ins)
                nc.vector.tensor_scalar(x_v[:, 0, :], x_mv[:, :, 1], X0_EPS, None, ALU.add).then_inc(xs_ve, 1)
                for t in range(TB):
                    ins = nc.vector.scalar_tensor_tensor(out=x_sim[:, n, t, :], in0=XS[:, t, :],
                                                         scalar=x_mv[:, t, 0:1], in1=gam_row[:, :],
                                                         op0=ALU.subtract, op1=ALU.mult)
                ins.then_inc(xs_free, 1)
                v.wait_ge(xs_pw, b + 1)
                link(nc.vector.scalar_tensor_tensor(out=x_v[:, 2, :], in0=x_v[:, 1, :], scalar=-0.5, in1=x_v[:, 1, :],
                                                    op0=ALU.mult, op1=ALU.mult))
                link(nc.vector.tensor_tensor(x_v[:, 2, :], x_v[:, 2, :], x_v[:, 0, :], ALU.mult))
                link(nc.vector.scalar_tensor_tensor(out=x_v[:, 3, :], in0=x_v[:, 2, :], scalar=1.5, in1=x_v[:, 1, :],
                                                    op0=ALU.add, op1=ALU.mult))
                for t in range(TB):
                    ins = nc.vector.scalar_tensor_tensor(out=x_sim[:, n, t, :], in0=x_sim[:, n, t, :],
                                                         scalar=x_v[:, 3, t:t + 1], in1=bet_row[:, :],
                                                         op0=ALU.mult, op1=ALU.add)
                link(ins)
                nc.vector.tensor_reduce(x_nm[:, n, :], x_sim[:, n], AX_X, ALU.max, negate=True).then_inc(xs_nm, 1)

            def attend_context(b):
                n = b % 2
                v.wait_ge(xs_exp, b + 1)
                link(nc.vector.reciprocal(x_rc[:, :], x_sum[:, n, :]))
                for t in range(TB):
                    ins = nc.vector.scalar_tensor_tensor(out=X[:, TB * b + t, :], in0=x_e[:, n, t, :],
                                                         scalar=x_rc[:, t:t + 1], in1=X[:, TB * b + t, :],
                                                         op0=ALU.mult, op1=ALU.add)
                link(ins)

            def mixture(b):
                wide = [P, TB, FK]
                lg, ex, al = f_al[:, 0], f_al[:, 1], f_al[:, 2]
                v.wait_ge(fl_mm, b + 1)
                link(nc.vector.tensor_tensor(lg, FL, f_b2[:, :].unsqueeze(1).broadcast_to(wide), ALU.add))
                link(nc.vector.tensor_reduce(f_st[:, 0, :], lg, AX_X, ALU.max))
                nc.vector.tensor_tensor(lg, lg, f_st[:, 0, :].unsqueeze(2).broadcast_to(wide), ALU.subtract).then_inc(fl_ex, 1)
                v.wait_ge(fl_e, b + 1)
                link(nc.vector.tensor_reduce(f_st[:, 1, :], ex, AX_X, ALU.add))
                link(nc.vector.reciprocal(f_st[:, 2, :], f_st[:, 1, :]))
                nc.vector.tensor_tensor(al, ex, f_st[:, 2, :].unsqueeze(2).broadcast_to(wide), ALU.mult).then_inc(fl_al, 1)

            def weigh(b):
                for n in range(2):
                    v.wait_ge(fa_mm, 2 * b + n + 1)
                    v.wait_ge(fx_ok, 2 * b + n + 1)
                    nc.vector.tensor_tensor(f_ax[:, 2 * n:2 * n + 2, :], f_vx[:, 2 * n:2 * n + 2, :], FA[n],
                                            ALU.mult).then_inc(fa_ok, 1)
                v.wait_ge(fo_mm, b + 1)
                nc.vector.tensor_tensor(X[:, TB * b:TB * b + TB, :], X[:, TB * b:TB * b + TB, :], FO, ALU.add).then_inc(fo_read, 1)
                v.wait_ge(fo_read, b + 1)

            v.wait_ge(x_bias, 1)
            v.wait_ge(ld_2, 32)
            for t in range(NT):
                v.wait_ge(o_mm, t + 1)
                nc.vector.tensor_tensor(X[:, t, :], X[:, t, :], bank[t % 2][:, 0:D], ALU.add).then_inc(o_read, 1)
                if t % TB == TB - 1:
                    v.wait_ge(o_read, t + 1)
                    ln_rows(1, t // TB)
                    if t // TB >= 2:
                        similarity(t // TB - 2)

            v.wait_ge(ld_3, 16 * 7)
            for n in range(1, B + 2):
                if n <= B:
                    attend_context(n - 1)
                    ln_rows(2, n - 1)
                if n + 1 < B:
                    similarity(n + 1)
                if n >= 2:
                    mixture(n - 2)
                    weigh(n - 2)
                    ln_rows(3, n - 2)

            def value_rows(b):
                v.wait_ge(av_tr, b + 1)
                for n in range(TB * KT):
                    ins = nc.vector.tensor_copy(a_vd[n], AC[1][:, n * P:n * P + P].rearrange("p (h c) -> p h c", h=HM))
                ins.then_inc(av_ok, 1)

            def heads(b, between):
                for n in range(H1 + 2):
                    if n < H1:
                        v.wait_ge(as_mm, H1 * b + n + 1)
                        nc.vector.tensor_reduce(a_nm[:, n % 3, :], AS[n % 3], AX_X, ALU.max, negate=True).then_inc(as_nm, 1)
                    if 1 <= n <= H1:
                        v.wait_ge(as_exp, H1 * b + n)
                        nc.vector.reciprocal(a_rc[:, (n - 1) % 3, :], a_sum[:, (n - 1) % 3, :]).then_inc(as_rc, 1)
                    if n >= 2 and n % 2:
                        v.wait_ge(at_mm, H1 * b + n - 1)
                        nc.vector.tensor_copy(a_pT[:, 1], AT[1]).then_inc(at_od, 1)
                    if n == LN_AT and between:
                        attend_self(b - 1)
                        ln_rows(4, b - 1, 0)

            def attend_self(b):
                v.wait_ge(ao_mm, b + 1)
                xb = X[:, ds(TB * b, TB), :]
                link(nc.vector.tensor_tensor(xb, xb, AB[1], ALU.add))
                v.sem_inc(ao_read, 1)

            v.wait_ge(ld_4, 16 * 7)
            nc.vector.tensor_scalar(a_bs[:, 0:2], a_b[:, 0:2], D1 ** -0.5, None, ALU.mult)
            nc.vector.tensor_scalar(a_bs[:, 2:4], a_b[:, 2:4], a_par[:, 0:1], None, ALU.mult)
            nc.vector.tensor_scalar(a_bs[:, 4:6], a_b[:, 2:4], a_par[:, 1:2], None, ALU.mult).then_inc(consts, 1)
            v.wait_ge(x_bias, 2)
            value_rows(0)
            heads(0, False)
            with nc.vector.Fori(1, B) as b, link.over(b, 1, B, 6):
                value_rows(b)
                heads(b, True)
            attend_self(B - 1)
            ln_rows(4, B - 1, 0)

            def rotate(r, part, after):
                if part == 0:
                    v.wait_ge(lb_mm, r + 1)
                    if after:
                        v.wait_ge(lb_add, r)
                products = ((0, cos_q[:, 0]), (1, sin_q[:, 0]), (1, cos_q[:, 1]), (0, sin_q[:, 1]))
                for n in (2 * part, 2 * part + 1):
                    src, table = products[n]
                    ins = nc.vector.tensor_tensor(l_pr[:, n, :].rearrange("p (b s) -> p b s", b=2),
                                                  LR[src][0:QH, :].rearrange("p (b s) -> p b s", b=2),
                                                  table.unsqueeze(1).broadcast_to([QH, 2, S]), ALU.mult)
                ins.then_inc(lb_rot, 1)

            def row_max(u, n):
                v.wait_ge(ls_mm, u + 1)
                nc.vector.tensor_reduce(l_nm[:, n % 2, :], LS, AX_X, ALU.max, negate=True).then_inc(ls_nm, 1)

            def query_lo(p, r):
                j, c = r // 2, r % 2
                upper, cols = slice(XC, 2 * XC), slice(512 * c, 512 * c + 512)
                v.wait_ge(lu_hi, 4 * p + r + 1)
                nc.vector.tensor_tensor(l_u[upper, j, cols], LU[upper, :], l_u[upper, j, cols].bitcast(F32),
                                        ALU.subtract).then_inc(lu_ok, 1)

            def row_scale(u, n):
                v.wait_ge(ls_exp, u + 1)
                link(nc.vector.reciprocal(l_rc[:, n % 2, :], l_sum[:, n % 2, :]))
                for t in range(TB):
                    ins = nc.vector.tensor_scalar(l_p[:, n % 2, t, :], l_p[:, n % 2, t, :], l_rc[:, n % 2, t:t + 1], None, ALU.mult)
                ins.then_inc(lp_ok, 1)

            def pair_rows(p, make, use):
                for k in range(10):
                    if use and k < 8 and k != LAST_AT:
                        row_max(8 * p - 8 + k, k)
                    if use and 1 <= k <= 8:
                        row_scale(8 * p - 8 + k - 1, k - 1)
                    if use and k == LAST_AT:
                        row_max(8 * p - 8 + k, k)
                    if make and k in ROT_AT:
                        r = ROT_AT.index(k)
                        for part in range(2):
                            rotate(4 * p + r, part, use or r)
                    if make and k in LAT_AT:
                        query_lo(p, LAT_AT.index(k))
                    if use and k == LAST_AT:
                        query_lo(p - 1, 3)

            v.wait_ge(ld_t, 32)
            pair_rows(0, True, False)
            with nc.vector.Fori(1, H2 // 2) as p, link.over(p, 1, H2 // 2, 8):
                pair_rows(p, True, True)
            pair_rows(H2 // 2, False, True)
            for t in range(NT):
                v.wait_ge(lf_mm, t + 1)
                nc.vector.tensor_tensor(X[:, t, :], X[:, t, :], bank[2 + t % 2][:, 0:D], ALU.add).then_inc(lf_read, 1)
                if t % TB == TB - 1:
                    v.wait_ge(lf_read, t + 1)
                    ln_rows(5, t // TB)

            def first_best(p, best, one, sc, mi):
                wide = [P, NT, E6]
                link(nc.vector.tensor_reduce(best, p, AX_X, ALU.max))
                link(nc.vector.tensor_tensor(sc, p, best.unsqueeze(2).broadcast_to(wide), ALU.is_equal))
                link(nc.vector.tensor_tensor(sc, sc, e_rev[:, :].unsqueeze(1).broadcast_to(wide), ALU.mult))
                link(nc.vector.tensor_reduce(mi, sc, AX_X, ALU.max))
                link(nc.vector.tensor_tensor(one, sc, mi.unsqueeze(2).broadcast_to(wide), ALU.is_equal))

            def route():
                wide = [P, NT, E6]
                lg, ex, p, one1, one2, sc = [e_r[:, n] for n in range(6)]
                mx, sm, rc, b1, b2, mi = [e_s[:, n, :] for n in range(6)]
                v.wait_ge(er_mm, 1)
                link(nc.vector.tensor_reduce(mx, EL, AX_X, ALU.max))
                nc.vector.tensor_tensor(lg, EL, mx.unsqueeze(2).broadcast_to(wide), ALU.subtract).then_inc(er_sub, 1)
                v.wait_ge(er_exp, 1)
                link(nc.vector.tensor_reduce(sm, ex, AX_X, ALU.add))
                link(nc.vector.reciprocal(rc, sm))
                link(nc.vector.tensor_tensor(p, ex, rc.unsqueeze(2).broadcast_to(wide), ALU.mult))
                first_best(p, b1, one1, sc, mi)
                link(nc.vector.scalar_tensor_tensor(out=lg.rearrange("p t e -> p (t e)"), in0=one1.rearrange("p t e -> p (t e)"),
                                                    scalar=-4.0, in1=p.rearrange("p t e -> p (t e)"), op0=ALU.mult, op1=ALU.add))
                first_best(lg, b2, one2, sc, mi)
                link(nc.vector.tensor_tensor(one1, one1, one2, ALU.add))
                link(nc.vector.tensor_tensor(sm, b1, b2, ALU.add))
                link(nc.vector.reciprocal(rc, sm))
                link(nc.vector.tensor_scalar(rc, rc, 0.5, None, ALU.mult))
                link(nc.vector.tensor_tensor(p, p, one1, ALU.mult))
                link(nc.vector.tensor_tensor(e_comb[:, :, :], p, rc.unsqueeze(2).broadcast_to(wide), ALU.mult))

            def gated_unit(b, u):
                U = (E6 + SF) * b + u
                n = u % 2
                v.wait_ge(eg_th, U + 1)
                link(nc.vector.scalar_tensor_tensor(out=e_sg[:, n, :], in0=e_th[:, n, :], scalar=1.0, in1=EG[n][:, 0, :],
                                                    op0=ALU.add, op1=ALU.mult))
                nc.vector.tensor_tensor(e_act[:, n, :], e_sg[:, n, :], EG[n][:, 1, :], ALU.mult).then_inc(eg_ok, 1)

            def add_expert(b, e, after):
                v.wait_ge(ey_mm, E6 * b + e + 1)
                if after:
                    v.wait_ge(ey_ok, E6 * b + e)
                for t in range(TB):
                    xt = X[:, ds(TB * b + t, 1), :].rearrange("p o d -> p (o d)")
                    ins = nc.vector.scalar_tensor_tensor(out=xt, in0=EY[e % 2][:, t, :],
                                                         scalar=e_comb[:, ds(TB * b + t, 1), e].rearrange("p o -> p o"), in1=xt,
                                                         op0=ALU.mult, op1=ALU.add)
                ins.then_inc(ey_ok, 1)

            def moe_batch(b, after):
                for u in range(E6 + SF):
                    gated_unit(b, u)
                    if 1 <= u <= E6:
                        add_expert(b, u - 1, after or u > 1)
                v.wait_ge(es_mm, b + 1)
                v.wait_ge(ey_ok, E6 * b + E6)
                for t in range(TB):
                    xt = X[:, ds(TB * b + t, 1), :].rearrange("p o d -> p (o d)")
                    ins = nc.vector.scalar_tensor_tensor(out=xt, in0=ES[t][:, 0:D], scalar=0.5, in1=xt,
                                                         op0=ALU.mult, op1=ALU.add)
                ins.then_inc(x_done, 1)

            route()
            moe_batch(0, False)
            with nc.vector.Fori(1, B) as b, link.over(b, 1, B, E6 + SF):
                moe_batch(b, True)

        @block.scalar
        def _(act):
            def ln_columns(s, b, src):
                act.wait_ge(ln_tr, ln_before(s, b) + 1)
                nc.scalar.copy(HT[:, :, ds(S * b, S)], src[:, :].rearrange("p (k t) -> p k t", k=KT)).then_inc(ln_ht, 1)

            act.wait_ge(ld_cx, 16 * 7)
            for n in range(2):
                act.wait_ge(kvt_mm, n + 1)
                nc.scalar.activation(kvT[:, 512 * n:512 * n + 512], bank[n][0:XC, :], ACT.Identity,
                                     bias=bk_col[:, :]).then_inc(kvt_ok, 1)
            for b in range(B):
                ln_columns(0, b, bank[6 + b % 2])
                act.wait_ge(ln_ht, b + 1)
                nc.scalar.copy(H_hi[:, :, b * S:b * S + S], HT[:, :, b * S:b * S + S]).then_inc(h_hi, 1)
            for n in range(2):
                act.wait_ge(lat_mm, n + 1)
                nc.scalar.copy(latT[:, 512 * n:512 * n + 512], bank[4 + n][:, :]).then_inc(latT_ok, 1)
            z, m, u, w, lw, c = [bt[:, n, :] for n in range(6)]
            act.wait_ge(bt_abs, 1)
            nc.scalar.activation(u, c, ACT.Exp, scale=-1.0).then_inc(bt_exp, 1)
            act.wait_ge(bt_w, 1)
            nc.scalar.activation(lw, w, ACT.Ln).then_inc(bt_ln, 1)

            def weights_hi(h, j, after):
                act.wait_ge(ld_w, 16 * h + 16)
                if after:
                    act.wait_ge(pj_mm, NT * h - NT)
                nc.scalar.copy(W_hi[:, j].rearrange("p k c -> p (k c)"), w_new).then_inc(w_hi, 1)

            def squares(h, j, t, after):
                if after or t:
                    act.wait_ge(sq_ok, NT * h + t)
                act.wait_ge(qkv_ok, NT * h + t + 1)
                for n in range(2):
                    ins = nc.scalar.activation(sq_out[:, n, :], qk_tok[:, t % 4, n * D0:n * D0 + D0], ACT.Square,
                                               accum_out=sumsq[:, j, n, t:t + 1])
                ins.then_inc(sq_ok, 1)

            def columns(h, n):
                act.wait_ge(tq_mm, 4 * h + n + 1)
                nc.scalar.copy(qkT[:, :, n * S:n * S + S], TQ).then_inc(tq_ok, 1)

            def head_out(g):
                for n in range(2):
                    act.wait_ge(tr_mm, 2 * g + n + 1)
                    nc.scalar.copy(outT[:, ds(g, 1), 512 * n:512 * n + 512].rearrange("p o t -> p (o t)"),
                                   OV[n][:, :, :].rearrange("p t d -> p (t d)")).then_inc(outT_ok, 1)

            def head_columns(h, j, after, more):
                for t in range(NT):
                    act.wait_ge(pj_mm, NT * h + t + 1)
                    if after or t >= 2:
                        act.wait_ge(pj_read, NT * h + t - 1)
                    nc.scalar.activation(tanh_g[:, t % 2], PJ[t % 3][:, 3 * D0:4 * D0], ACT.Tanh,
                                         scale=0.5).then_inc(tanh_done, 1)
                    if t:
                        squares(h, j, t - 1, after)
                    if t in (3, 5, 7):
                        columns(h, (t - 3) // 2)
                    if after and t == 0:
                        columns(h - 1, 3)
                    if more and t == 1:
                        weights_hi(h + 1, 1 - j, after)
                    if after > 1 and t == 4:
                        head_out(h - 2)
                squares(h, j, NT - 1, after)

            act.wait_ge(ld_1, 16 * 4)
            weights_hi(0, 0, False)
            head_columns(0, 0, 0, True)
            head_columns(1, 1, 1, True)
            with nc.scalar.Fori(1, H0 // 2 - 1) as i:
                for j in range(2):
                    head_columns(2 * i + j, j, 2, True)
            head_columns(H0 - 2, 0, 2, True)
            head_columns(H0 - 1, 1, 2, False)
            columns(H0 - 1, 3)
            head_out(H0 - 2)
            head_out(H0 - 1)
            def context_out(b):
                act.wait_ge(xo_mm, b + 1)
                nc.scalar.activation(x_oT[:, b % 2, :], XO[0:XC, 0:S], ACT.Copy, scale=X0_SCALE).then_inc(xo_ok, 1)

            def context_exp(b):
                n = b % 2
                act.wait_ge(xs_nm, b + 1)
                for t in range(TB):
                    ins = nc.scalar.activation(x_e[:, n, t, :], x_sim[:, n, t, :], ACT.Exp, bias=x_nm[:, n, t:t + 1],
                                               accum_out=x_sum[:, n, t:t + 1])
                ins.then_inc(xs_exp, 1)

            def hidden(b):
                act.wait_ge(fh_mm, b + 1)
                for m in range(KT):
                    ins = nc.scalar.activation(f_h[:, m, :], FH[:, m, :], ACT.Relu, bias=f_b1[:, m:m + 1])
                ins.then_inc(fh_ok, 1)
                for n in range(2):
                    act.wait_ge(fx_mm, 2 * b + n + 1)
                    nc.scalar.copy(f_vx[:, 2 * n:2 * n + 2, :], FX[n]).then_inc(fx_ok, 1)

            def mixture_exp(b):
                act.wait_ge(fl_ex, b + 1)
                nc.scalar.activation(f_al[:, 1], f_al[:, 0], ACT.Exp).then_inc(fl_e, 1)
                act.wait_ge(fa_tr, b + 1)
                nc.scalar.copy(f_aT, FT).then_inc(fa_T, 1)

            def keep_G(n):
                act.wait_ge(wp_mm, 2 * n + 1)
                nc.scalar.copy(Gw[:, n // 2, 8 * (n % 2):8 * (n % 2) + 8, :], WP[0:QH, :].rearrange("p (h c) -> p h c", h=8)).then_inc(wp_ok, 1)

            def keep_M(n):
                act.wait_ge(wp_mm, 2 * n + 2)
                nc.scalar.copy(Mw[:, 2 * n:2 * n + 2, :], WP[:, :].rearrange("p (m d) -> p m d", m=2)).then_inc(wp_ok, 1)

            for b in range(B):
                ln_columns(1, b, bank[6 + b % 2])
                if b in (1, 2):
                    context_out(b - 1)
                if b >= 2:
                    context_exp(b - 2)

            for n in range(1, B + 2):
                if n + 1 < B:
                    context_out(n + 1)
                if n <= B:
                    keep_G(n - 1)
                if n >= 2:
                    hidden(n - 2)
                if n >= 3:
                    ln_columns(3, n - 3, bank[7])
                if n <= B:
                    ln_columns(2, n - 1, bank[7])
                    keep_M(n - 1)
                if n + 1 < B:
                    context_exp(n + 1)
                if n >= 2:
                    mixture_exp(n - 2)
            ln_columns(3, B - 1, bank[7])

            def project_columns(b):
                act.wait_ge(a_mm, 3 * b + 1)
                for m in range(KT):
                    ins = nc.scalar.activation(a_q[:, m, :], AB[0][:, m, :], ACT.Identity, bias=a_bs[:, m:m + 1],
                                               scale=D1 ** -0.5)
                ins.then_inc(a_ok, 1)
                act.wait_ge(a_mm, 3 * b + 2)
                for o in range(2):
                    for m in range(KT):
                        ins = nc.scalar.activation(a_k[:, o, m, :], AB[1][:, m, :], ACT.Identity,
                                                   bias=a_bs[:, 2 + 2 * o + m:3 + 2 * o + m], scale=a_par[:, o:o + 1])
                ins.then_inc(a_ok, 1)
                act.wait_ge(a_mm, 3 * b + 3)
                for m in range(KT):
                    ins = nc.scalar.activation(a_vT[:, m, :], AB[0][:, m, :], ACT.Identity, bias=a_b[:, 4 + m:5 + m])
                ins.then_inc(a_ok, 1)

            def context_columns(b, m):
                act.wait_ge(ac_mm, KT * b + m + 1)
                nc.scalar.copy(a_cT[:, m, :], AC[m][:, 0:S]).then_inc(ac_T, 1)

            def head_exps(b, between):
                for n in range(H1 + 2):
                    if n < H1:
                        act.wait_ge(as_nm, H1 * b + n + 1)
                        for t in range(TB):
                            ins = nc.scalar.activation(a_p[:, n % 3, t, :], AS[n % 3][:, t, :], ACT.Exp,
                                                       bias=a_nm[:, n % 3, t:t + 1], accum_out=a_sum[:, n % 3, t:t + 1])
                        ins.then_inc(as_exp, 1)
                    if n >= 2 and n % 2 == 0:
                        act.wait_ge(at_mm, H1 * b + n - 1)
                        nc.scalar.copy(a_pT[:, 0], AT[0]).then_inc(at_ev, 1)
                    if n == HM + 3:
                        context_columns(b, 0)
                    if n == LN_AT + 2 and between:
                        ln_columns(4, b - 1, bank[1])

            act.wait_ge(consts, 3)
            project_columns(0)
            head_exps(0, False)
            with nc.scalar.Fori(1, B) as b:
                context_columns(b - 1, 1)
                project_columns(b)
                head_exps(b, True)
            context_columns(B - 1, 1)
            ln_columns(4, B - 1, bank[1])

            def query_keys(p, q, c):
                act.wait_ge(l_q_mm, 4 * p + q + 1)
                nc.scalar.copy(l_q[:, 512 * c:512 * c + 512], bank[c][:, :]).then_inc(l_q_ok, 1)

            def query_latents(p, r, use):
                j, c = r // 2, r % 2
                act.wait_ge(lu_mm, 4 * p + r + 1)
                if use:
                    act.wait_ge(ls_mm, 8 * p - 8 + 2 * (2 * c + 1) + j + 1)
                nc.scalar.copy(l_u[:, j, 512 * c:512 * c + 512], LU[:, :]).then_inc(lu_hi, 1)

            def attended(p, u, n):
                b = n // 2
                act.wait_ge(lv_mm, u + 1)
                nc.scalar.copy(l_cT[:, ds(p - 1, 1), b * S:b * S + S].rearrange("p o t -> p (o t)"), LC[:, b % 2, :]).then_inc(lc_ok, 1)

            def unit_exp(u, n):
                act.wait_ge(ls_nm, u + 1)
                for t in range(TB):
                    ins = nc.scalar.activation(l_p[:, n % 2, t, :], LS[:, t, :], ACT.Exp, bias=l_nm[:, n % 2, t:t + 1],
                                               accum_out=l_sum[:, n % 2, t:t + 1])
                ins.then_inc(ls_exp, 1)

            def pair_columns(p, make, use):
                for k in range(10):
                    if use and k >= 2:
                        act.wait_ge(lt_mm, 8 * p - 8 + k - 1)
                        nc.scalar.copy(l_pT, LT).then_inc(lt_ok, 1)
                    if use and k > 2 and k % 2 == 0:
                        attended(p, 8 * p - 8 + k - 3, k - 3)
                    if use and 2 <= k < 8:
                        unit_exp(8 * p - 8 + k, k)
                    for r in range(4):
                        if make and k == KEY_AT[r]:
                            query_keys(p, r, r % 2)
                        if make and r < 3 and k == LAT_AT[r]:
                            query_latents(p, r, use)
                    if use and k < 2:
                        unit_exp(8 * p - 8 + k, k)
                    if use and k == LAST_AT:
                        query_latents(p - 1, 3, False)
                if use:
                    attended(p, 8 * p - 1, 7)

            act.wait_ge(ao_mm, B)
            nc.scalar.copy(lat_hi[:, :], latT[:, :]).then_inc(lat_r, 1)
            pair_columns(0, True, False)
            with nc.scalar.Fori(1, H2 // 2) as p:
                pair_columns(p, True, True)
            pair_columns(H2 // 2, False, True)
            for b in range(2):
                ln_columns(5, b, bank[6 + b])
            ln_columns(5, 2, bank[6])
            ln_columns(5, 3, bank[7])

            def moe_tanh(b):
                for u in range(E6 + SF):
                    act.wait_ge(eg_mm, (E6 + SF) * b + u + 1)
                    nc.scalar.activation(e_th[:, u % 2, :], EG[u % 2][:, 0, :], ACT.Tanh, scale=0.5).then_inc(eg_th, 1)

            act.wait_ge(er_sub, 1)
            nc.scalar.activation(e_r[:, 1], e_r[:, 0], ACT.Exp).then_inc(er_exp, 1)
            with nc.scalar.Fori(0, B) as b:
                moe_tanh(b)

        @block.tensor
        def _(pe):
            mm = nc.tensor.matmul

            def ln_turn(s, b, dst, place=None, behind=1):
                if s or b >= 2:
                    pe.wait_ge(ln_ht, ln_before(s, b) - behind)
                pe.wait_ge(ln_h, ln_before(s, b) + 1)
                for t in range(TB):
                    for k in range(KT):
                        ins = nc.tensor.transpose(dst[:, k * S + t * P:k * S + t * P + P],
                                                  HN[:, (TB * b if place is None else place) + t, k * P:k * P + P],
                                                  ident[:, :])
                ins.then_inc(ln_tr, 1)

            pe.wait_ge(ld_cx, 16 * 7)
            for n in range(2):
                mm(bank[n][0:XC, :], wk_T[:, :], ctxT[:, 512 * n:512 * n + 512], start=True, stop=True).then_inc(kvt_mm, 1)
            for t in range(NT):
                ins = mm(bank[3][:, t * XC:t * XC + XC], ctxT[:, t * P:t * P + P], wk_T[:, :], start=True, stop=True)
            ins.then_inc(kvn_mm, 1)

            pe.wait_ge(ld_c, 16)
            for b in range(B):
                ln_turn(0, b, bank[6 + b % 2])
            pe.wait_ge(lat_ok, 1)
            for t in range(NT):
                ins = nc.tensor.transpose(bank[4 + t // 4][:, t % 4 * P:t % 4 * P + P], lat2[:, t, :], ident[:, :])
                if t % 4 == 3:
                    ins.then_inc(lat_mm, 1)
            pe.wait_ge(kvt_ok, 2)
            pe.wait_ge(kvn_ok, 1)
            pe.wait_ge(latT_ok, 2)
            pe.wait_ge(ln_ht, B)
            pe.wait_ge(ld_1, 16 * 4)
            for t in range(NT):
                for k in range(KT):
                    ins = mm(PRB[:, t * H0:t * H0 + H0], HT[:, k, t * P:t * P + P], b_w[:, k, :],
                             start=(k == 0), stop=(k == KT - 1))
            ins.then_inc(bt_mm, 1)

            def project_tile(h, j, t, after):
                if t == 0:
                    pe.wait_ge(w_lo, h + 1)
                if t >= 3 or after:
                    pe.wait_ge(pj_read, NT * h + (t - 3 if t >= 3 else (-2, -1, -3)[t]) + 1)
                cols = slice(t * P, t * P + P)
                for k in range(KT):
                    for m, (x_part, w_part) in enumerate(((H_hi, W_hi), (H_hi, W_lo), (H_lo, W_hi))):
                        ins = mm(PJ[t % 3][:, :], x_part[:, k, cols], w_part[:, j, k, :],
                                 start=(k == 0 and m == 0), stop=(k == KT - 1 and m == 2))
                ins.then_inc(pj_mm, 1)

            def turn_queries(h, n, after):
                if after or n:
                    pe.wait_ge(tq_ok, 4 * h + n)
                pe.wait_ge(qkv_ok, NT * h + 2 * n + 2)
                for c in range(2):
                    for t in range(2):
                        ins = nc.tensor.transpose(TQ[:, c, t * P:t * P + P], qk_tok[:, (2 * n + t) % 4, c * D0:c * D0 + D0], ident[:, :])
                ins.then_inc(tq_mm, 1)

            def scores(g, after):
                pe.wait_ge(tq_ok, 4 * g + 4)
                if not after:
                    pe.wait_ge(bt_abs, 1)
                for n in range(2):
                    if after:
                        pe.wait_ge(masked, 2 * g + n - 1)
                    for t in range(4 * n, 4 * n + 4):
                        ins = mm(SC[n][:, t % 4, :], qkT[:, 1, t * P:t * P + P], qkT[:, 0, t * P:t * P + P],
                                 start=True, stop=True)
                    ins.then_inc(sc_mm, 1)

            def values(g, j, n, after):
                if after:
                    pe.wait_ge(outT_ok, 2 * g + n - 1)
                pe.wait_ge(masked, 2 * g + n + 1)
                for t in range(4 * n, 4 * n + 4):
                    ins = mm(OV[n][:, t % 4, :], attn[:, t, :], v_tok[:, j, t, :], start=True, stop=True)
                ins.then_inc(pv_mm, 1)

            def turn_head(g, n):
                pe.wait_ge(gated_ok, 2 * g + n + 1)
                for t in range(4 * n, 4 * n + 4):
                    ins = nc.tensor.transpose(OV[n][:, t % 4, :], gated[:, t, :], ident[:, :])
                ins.then_inc(tr_mm, 1)

            def head(h, j, after):
                for t in range(NT):
                    project_tile(h, j, t, after)
                    if after:
                        if t == 0:
                            turn_queries(h - 1, 3, after)
                        if t == 1:
                            scores(h - 1, after > 1)
                        if t in (5, 6):
                            values(h - 1, 1 - j, t - 5, after > 1)
                        if t in (2, 3) and after > 1:
                            turn_head(h - 2, t - 2)
                    if t in (2, 4, 6):
                        turn_queries(h, t // 2 - 1, after)

            pe.wait_ge(consts, 1)
            pe.wait_ge(h_lo, B)
            head(0, 0, 0)
            head(1, 1, 1)
            with nc.tensor.Fori(1, H0 // 2) as i:
                for j in range(2):
                    head(2 * i + j, j, 2)
            turn_queries(H0 - 1, 3, True)
            scores(H0 - 1, True)
            for n in range(2):
                turn_head(H0 - 2, n)
            for n in range(2):
                values(H0 - 1, 1, n, True)
            for n in range(2):
                turn_head(H0 - 1, n)

            def context_product(b):
                pe.wait_ge(ln_ht, B + b + 1)
                if b:
                    pe.wait_ge(xo_ok, b)
                for k in range(KT):
                    ins = mm(XO[0:XC, 0:S], kv[:, TB * b + k, :], HT[:, k, b * S:b * S + S],
                             start=(k == 0), stop=(k == KT - 1))
                ins.then_inc(xo_mm, 1)

            def context_similarity(b):
                pe.wait_ge(xo_ok, b + 1)
                if b:
                    pe.wait_ge(xs_free, b)
                for t in range(TB):
                    ins = mm(XS[:, t, :], x_oT[:, b % 2, t * P:t * P + P], kvT[:, b * S:b * S + S],
                             start=True, stop=True)
                ins.then_inc(xs_mm, 1)

            pe.wait_ge(pj_read, NT * H0)
            pe.wait_ge(ld_o, 16)
            pe.wait_ge(outT_ok, 2 * H0)
            for t in range(NT):
                if t >= 2:
                    pe.wait_ge(o_read, t - 1)
                for h in range(H0):
                    ins = mm(bank[t % 2][:, 0:D], outT[:, h, t * P:t * P + P], o_w[:, h, :],
                             start=(h == 0), stop=(h == H0 - 1))
                ins.then_inc(o_mm, 1)
                if t % TB == 0 and t:
                    ln_turn(1, t // TB - 1, bank[6 + (t // TB - 1) % 2])
                    if t // TB >= 2:
                        context_product(t // TB - 2)
                        context_similarity(t // TB - 2)
            ln_turn(1, B - 1, bank[7])

            def ffn_front(b):
                if b:
                    pe.wait_ge(fo_read, b)
                for m in range(KT):
                    for k in range(KT):
                        ins = mm(FH[:, m, :], f_w1[:, k, m * P:m * P + P], HT[:, k, b * S:b * S + S],
                                 start=(k == 0), stop=(k == KT - 1))
                ins.then_inc(fh_mm, 1)
                for m in range(FM):
                    if b and m % 2 == 0:
                        pe.wait_ge(fa_ok, 2 * b - 1 + m // 2)
                    for k in range(KT):
                        ins = mm(FX[m // 2][:, m % 2, :], f_v[:, k, m * P:m * P + P], HT[:, k, b * S:b * S + S],
                                 start=(k == 0), stop=(k == KT - 1))
                    if m % 2:
                        ins.then_inc(fx_mm, 1)
                pe.wait_ge(fh_ok, b + 1)
                if b:
                    pe.wait_ge(fa_T, b)
                for t in range(TB):
                    for k in range(KT):
                        ins = mm(FL[:, t, :], f_h[:, k, t * P:t * P + P], f_w2[:, k, :], start=(k == 0), stop=(k == KT - 1))
                ins.then_inc(fl_mm, 1)

            def ffn_back(b):
                pe.wait_ge(fl_al, b + 1)
                for t in range(TB):
                    ins = nc.tensor.transpose(FT[:, t * P:t * P + P], f_al[:, 2, t, :], ident[:, :])
                ins.then_inc(fa_tr, 1)
                pe.wait_ge(fa_T, b + 1)
                pe.wait_ge(fx_ok, 2 * b + 2)
                for m in range(FM):
                    ins = mm(FA[m // 2][:, m % 2, :], f_sel[:, m, :], f_aT, start=True, stop=True)
                    if m % 2:
                        ins.then_inc(fa_mm, 1)
                pe.wait_ge(fa_ok, 2 * b + 2)
                for t in range(TB):
                    for m in range(FM):
                        ins = mm(FO[:, t, :], f_ax[:, m, t * P:t * P + P], f_u[:, m, :], start=(m == 0), stop=(m == FM - 1))
                ins.then_inc(fo_mm, 1)

            def product_G(n):
                if n:
                    pe.wait_ge(wp_ok, 2 * n)
                for h in range(8 * (n % 2), 8 * (n % 2) + 8):
                    ins = mm(WP[0:QH, (h % 8) * XC:(h % 8 + 1) * XC], qr_T[:, h, n // 2 * QH:n // 2 * QH + QH], kr_T[:, h, :],
                             start=True, stop=True)
                ins.then_inc(wp_mm, 1)

            def product_M(n):
                pe.wait_ge(wp_ok, 2 * n + 1)
                for m in range(2 * n, 2 * n + 2):
                    for j in range(2):
                        ins = mm(WP[j * XC:j * XC + XC, (m % 2) * D:(m % 2) * D + D], kc_kv[:, 2 * m + j, :], wo_T[:, 2 * m + j, :],
                                 start=True, stop=True)
                ins.then_inc(wp_mm, 1)

            pe.wait_ge(ln_ht, 2 * B)
            pe.wait_ge(o_read, NT)
            pe.wait_ge(ld_3, 16 * 7)
            for n in range(1, B + 2):
                if n + 1 < B:
                    context_product(n + 1)
                    context_similarity(n + 1)
                if n == 1:
                    pe.wait_ge(ld_p, 16 * 4)
                if n <= B:
                    product_G(n - 1)
                if n >= 2:
                    ffn_front(n - 2)
                if n >= 3:
                    ln_turn(3, n - 3, bank[7], behind=0)
                if n <= B:
                    ln_turn(2, n - 1, bank[7], behind=0)
                    product_M(n - 1)
                if n >= 2:
                    ffn_back(n - 2)
            ln_turn(3, B - 1, bank[7], behind=0)

            def project(b, after):
                for kind in range(3):
                    if kind == 2:
                        pe.wait_ge(a_ok, 3 * b + 1)
                        if after:
                            pe.wait_ge(a_ok, 3 * b + 2)
                            project_out(b - 1)
                    dst = AB[kind % 2]
                    for m in range(KT):
                        for k in range(KT):
                            ins = mm(dst[:, m, :], a_w[:, k, kind * D + m * P:kind * D + m * P + P], HT[:, k, ds(b * S, S)],
                                     start=(k == 0), stop=(k == KT - 1))
                    ins.then_inc(a_mm, 1)
                pe.wait_ge(a_ok, 3 * b + 3)
                for t in range(TB):
                    for m in range(KT):
                        ins = nc.tensor.transpose(AC[1][:, t * D + m * P:t * D + m * P + P], a_vT[:, m, t * P:t * P + P], ident[:, :])
                ins.then_inc(av_tr, 1)

            def attend(b, between):
                for n in range(H1 + 3):
                    if n < H1:
                        m, g, o = n // 8, n % 8 // 2, n % 2
                        rows = slice(32 * g, 32 * g + 32)
                        if n >= 3:
                            pe.wait_ge(as_exp, H1 * b + n - 2)
                        for t in range(TB):
                            ins = mm(AS[n % 3][:, t, :], a_q[rows, m, t * P:t * P + P], a_k[rows, o, m, :], start=True, stop=True)
                        ins.then_inc(as_mm, 1)
                    if 2 <= n < H1 + 2:
                        q = n - 2
                        pe.wait_ge(ap_ok, H1 * b + q + 1)
                        if q >= 2:
                            (pe.wait_ge(at_ev, H1 // 2 * b + q // 2) if q % 2 == 0 else pe.wait_ge(at_od, H1 // 2 * b + q // 2))
                        for l in range(TB):
                            for t in range(TB):
                                ins = nc.tensor.transpose(AT[q % 2][:, l, t * P:t * P + P], a_p[:, q % 3, t, l * P:l * P + P], ident[:, :])
                        ins.then_inc(at_mm, 1)
                    if n >= 3:
                        q = n - 3
                        (pe.wait_ge(at_ev, H1 // 2 * b + q // 2 + 1) if q % 2 == 0 else pe.wait_ge(at_od, H1 // 2 * b + q // 2 + 1))
                        if q == 0:
                            pe.wait_ge(av_ok, b + 1)
                        for l in range(TB):
                            ins = mm(AC[q // HM][:, 0:S], a_v[:, l, q, :], a_pT[:, q % 2, l, :],
                                     start=(q % HM == 0 and l == 0), stop=(q % HM == HM - 1 and l == TB - 1))
                        if q % HM == HM - 1:
                            ins.then_inc(ac_mm, 1)
                    if n == LN_AT + 2 and between:
                        pe.wait_ge(ao_read, b)
                        ln_turn(4, b - 1, bank[1], 0, 0)

            def project_out(b):
                pe.wait_ge(ac_T, KT * b + KT)
                for t in range(TB):
                    for c in range(KT):
                        ins = mm(AB[1][:, t, :], a_cT[:, c, t * P:t * P + P], a_ow[:, c, :], start=(c == 0), stop=(c == KT - 1))
                ins.then_inc(ao_mm, 1)

            pe.wait_ge(wp_ok, 8)
            pe.wait_ge(ld_4, 16 * 7)
            pe.wait_ge(consts, 3)
            project(0, False)
            attend(0, False)
            with nc.tensor.Fori(1, B) as b:
                pe.wait_ge(ln_ht, 4 * B + b - 1)
                pe.wait_ge(as_exp, H1 * b)
                project(b, True)
                attend(b, True)
            project_out(B - 1)
            pe.wait_ge(ao_read, B)
            ln_turn(4, B - 1, bank[1], 0, 0)

            def head_key(p, q, after):
                j, c = q // 2, q % 2
                pe.wait_ge(ld_w5[j], 16 * p + 16)
                if j:
                    pe.wait_ge(l_q_ok, 4 * p + c + 1)
                for k in range(KT):
                    ins = mm(bank[c][:, :], w5[:, j, k * K2:k * K2 + K2], HT[:, k, 512 * c:512 * c + 512],
                             start=(k == 0), stop=(k == KT - 1))
                ins.then_inc(l_q_mm, 1)

            def head_rotated(p, r, after):
                j, c = r // 2, r % 2
                pe.wait_ge(l_q_ok, 4 * p + r + 1)
                if after:
                    pe.wait_ge(lb_rot, 8 * p + 2 * r)
                for o in range(2):
                    ins = mm(LR[o][0:QH, :], w5[:, j, 2 * K2 + o * QH:2 * K2 + o * QH + QH], l_q[:, 512 * c:512 * c + 512],
                             start=True, stop=True)
                ins.then_inc(lb_mm, 1)

            def head_query(p, r, after):
                j, c = r // 2, r % 2
                if r == 0:
                    pe.wait_ge(g_ok, p + 1)
                pe.wait_ge(lb_add, 4 * p + r + 1)
                if after:
                    pe.wait_ge(lu_ok, 4 * p + r)
                for o in range(2):
                    ins = mm(LU[:, :], g_now[:, o, j, :, :].rearrange("p n c -> p (n c)"), l_rot[:, o, 512 * c:512 * c + 512],
                             start=(o == 0), stop=(o == 1))
                ins.then_inc(lu_mm, 1)

            def unit_turn(u, n):
                pe.wait_ge(lp_ok, u + 1)
                for l in range(TB):
                    for t in range(TB):
                        ins = nc.tensor.transpose(LT[:, l, t * P:t * P + P], l_p[:, n % 2, t, l * P:l * P + P], ident[:, :])
                ins.then_inc(lt_mm, 1)

            def unit_scores(u, n, after):
                b, j = n // 2, n % 2
                if after:
                    pe.wait_ge(ls_exp, u)
                for t in range(TB):
                    for m, part in enumerate((lat_hi, lat_lo)):
                        ins = mm(LS[:, t, :], l_u[:, j, (TB * b + t) * P:(TB * b + t + 1) * P], part[:, b * S:b * S + S],
                                 start=(m == 0), stop=(m == 1))
                ins.then_inc(ls_mm, 1)

            def unit_values(p, u, n, after):
                b, j = n // 2, n % 2
                pe.wait_ge(lt_ok, u + 1)
                if j == 0 and after:
                    pe.wait_ge(lc_ok, B * p - B + b)
                for l in range(TB):
                    ins = mm(LC[XC * j:XC * j + XC, b % 2, :], lat[:, TB * b + l, :], l_pT[:, l, :], start=(l == 0), stop=(l == TB - 1))
                ins.then_inc(lv_mm, 1)

            def pair(p, make, use, after):
                def make_query(k):
                    for r in range(4):
                        if k == KEY_AT[r]:
                            head_key(p, r, after)
                        if k == ROT_AT[r]:
                            head_rotated(p, r, after or r)
                        if r < 3 and k == LAT_AT[r]:
                            head_query(p, r, after or r)

                for k in range(10):
                    u = 8 * p - 8 + k
                    if make and k in (0, 1):
                        make_query(k)
                    if use and k >= 2:
                        unit_turn(u - 2, k - 2)
                    if use and k < 8:
                        if k == 0:
                            pe.wait_ge(lu_ok, 4 * p - 1)
                        if k == 5:
                            pe.wait_ge(lu_ok, 4 * p)
                        unit_scores(u, k, k or after > 1)
                    if use and k == LAST_AT:
                        head_query(p - 1, 3, True)
                    if make and 1 < k < 9:
                        make_query(k)
                    if use and k >= 2:
                        unit_values(p, u - 2, k - 2, k > 2 or after > 1)

            pe.wait_ge(ln_ht, 5 * B)
            pe.wait_ge(ao_read, B)
            pair(0, True, False, 0)
            pe.wait_ge(lat_r, 2)
            pair(1, True, True, 1)
            with nc.tensor.Fori(2, H2 // 2) as p:
                pair(p, True, True, 2)
            pair(H2 // 2, False, True, 2)
            pe.wait_ge(lc_ok, B * (H2 // 2))
            for t in range(NT):
                if t >= 2:
                    pe.wait_ge(lf_read, t - 1)
                for m in range(H2 // 2):
                    ins = mm(bank[2 + t % 2][:, 0:D], l_cT[:, m, t * P:t * P + P], Mw[:, m, :], start=(m == 0), stop=(m == H2 // 2 - 1))
                ins.then_inc(lf_mm, 1)
                if t >= 2 and t % 2 == 0:
                    b = t // 2 - 1
                    ln_turn(5, b, bank[6 + b % 2])
            ln_turn(5, 3, bank[7])

            def expert_up(b, u, after):
                U = (E6 + SF) * b + u
                if after or u >= 2:
                    pe.wait_ge(eg_ok, U - 1)
                for gu in range(2):
                    for k in range(KT):
                        w = e_gu[:, k, u, gu * I6:gu * I6 + I6] if u < E6 else e_sgu[:, k, gu * SH6 + (u - E6) * P:gu * SH6 + (u - E6) * P + P]
                        ins = mm(EG[u % 2][:, gu, :], w, HT[:, k, ds(b * S, S)], start=(k == 0), stop=(k == KT - 1))
                ins.then_inc(eg_mm, 1)

            def expert_down(b, u, after):
                U = (E6 + SF) * b + u
                pe.wait_ge(eg_ok, U + 1)
                if u < E6:
                    if after or u >= 2:
                        pe.wait_ge(ey_ok, E6 * b + u - 1)
                    for t in range(TB):
                        ins = mm(EY[u % 2][:, t, :], e_act[:, u % 2, t * P:t * P + P], e_dn[:, u, :], start=True, stop=True)
                    ins.then_inc(ey_mm, 1)
                else:
                    f = u - E6
                    if f == 0 and after:
                        pe.wait_ge(x_done, b)
                    for t in range(TB):
                        ins = mm(ES[t][:, 0:D], e_act[:, u % 2, t * P:t * P + P], e_sdn[:, f, :], start=(f == 0), stop=(f == SF - 1))
                    if f == SF - 1:
                        ins.then_inc(es_mm, 1)

            def moe(b, after):
                for u in range(E6 + SF + 1):
                    if u < E6 + SF:
                        expert_up(b, u, after)
                    if u:
                        expert_down(b, u - 1, after)

            pe.wait_ge(ln_ht, 6 * B)
            pe.wait_ge(lf_read, NT)
            for t in range(NT):
                for k in range(KT):
                    ins = mm(EL[:, t, :], HT[:, k, t * P:t * P + P], e_gate[:, k, :], start=(k == 0), stop=(k == KT - 1))
            ins.then_inc(er_mm, 1)
            pe.wait_ge(ld_6, 16 * 4)
            moe(0, False)
            with nc.tensor.Fori(1, B) as b:
                moe(b, True)


def kernel(**inputs):
    import numpy as np
    import concourse.bacc as bacc
    from concourse.bass_utils import run_bass_kernel_spmd

    g = {k: np.asarray(v) for k, v in inputs.items()}
    arrays = lay_out(np, g)
    arrays.update(constants(np))
    nc = bacc.Bacc("TRN2", target_bir_lowering=False, num_devices=1)
    feeds, args = {}, {}
    for name, value in arrays.items():
        value = np.ascontiguousarray(value)
        feeds[f"in_{name}"] = value
        args[name] = nc.dram_tensor(f"in_{name}", value.shape, mybir.dt.from_np(value.dtype), kind="ExternalInput").ap()
    out = nc.dram_tensor("out_x", (B, S, D), F32, kind="ExternalOutput").ap()
    decoder(nc, args, out)
    return run_bass_kernel_spmd(nc, [feeds], core_ids=[0]).results[0]["out_x"]
```

```python
from contextlib import ExitStack, contextmanager

import concourse.bass as bass
from concourse import mybir

F32 = mybir.dt.float32
F32R = mybir.dt.float32r
ALU = mybir.AluOpType
ACT = mybir.ActivationFunctionType
AX_X = mybir.AxisListType.X
ds = bass.ds

P = 128
B, S, D = 4, 256, 256
T = B * S
NT = T // P
KT = D // P
TB = S // P
LN_EPS = 1e-5

H0, D0, CHUNK = 16, 128, 64
NORM_FLOOR = (1e-12 ** 2) * D0

XC = 64
X0_EPS = 1e-6
X0_SCALE = 256 ** -0.5

FK, FR = 8, 64
FM = FK * FR // P

H1, D1 = 16, 16
HM = P // D1
NEXT_AT = (9, 11, 13, 15)
LN_AT = 4

H2, K2, Q2, R2 = 16, 128, 192, 64
QH = Q2 // 2
KEY_AT = (0, 0, 2, 4)
ROT_AT = (1, 3, 5, 7)
LAT_AT = (4, 6, 8)
LAST_AT = 1

E6, I6, SH6 = 8, 128, 512
SF = SH6 // P
UNITS = E6 + SF


WOVEN = [(2, 0), (2, 1), (3, 0), (2, 2), (3, 1), (2, 3), (3, 2), (3, 3)]


def ln_before(s, b):
    return 2 * B + WOVEN.index((s, b)) if s in (2, 3) else B * s + b


class Chain:

    def __init__(self, eng, sem):
        self.eng, self.sem, self.n, self.loop = eng, sem, 0, None

    def value(self):
        if self.loop is None:
            return self.n
        i, first, start, per = self.loop
        return (i - first) * per + self.n

    def __call__(self, ins):
        ins.then_inc(self.sem, 1)
        self.n += 1
        self.eng.wait_ge(self.sem, self.value())

    @contextmanager
    def over(self, i, first, last, per):
        start = self.n
        self.loop = (i, first, start, per)
        yield
        assert self.n == start + per, (self.n - start, per)
        self.n = start + per * (last - first)
        self.loop = None


def lay_out(np, g):
    def tiles(w):
        return w.reshape(-1, P, w.shape[1]).transpose(1, 0, 2)

    heads = np.stack([g[f"L0_attn_{n}_w"].reshape(H0, D0, KT, P).transpose(0, 3, 2, 1)
                      for n in ("q", "k", "v", "og")], axis=3)
    return {
        "x": g["x"],
        "w_head": heads.reshape(H0, P, KT * 4 * D0),
        "qkv_b": np.stack([g[f"L0_attn_{n}_b"].reshape(H0, D0) for n in "qkv"], axis=1).reshape(H0, 3 * D0),
        "o_w": g["L0_attn_o_w"].reshape(D, H0, D0).transpose(2, 1, 0),
        "b_w": tiles(g["L0_attn_b_w"].T),
        "bb": g["L0_attn_b_b"],
        "ob": g["L0_attn_o_b"],
        "ctx": g["ctx_512"].reshape(NT, P, XC).transpose(1, 0, 2),
        "ctxT": g["ctx_512"].reshape(T, XC).T,
        "wk_T": g["L0_xattn_W_k"].T,
        "bk": g["L0_xattn_b_k"].reshape(XC, 1),
        "gam": g["L0_xattn_ln_gamma"],
        "bet": g["L0_xattn_ln_beta"],
        "f_w1": tiles(g["L0_ffn_W1"]),
        "f_b1": g["L0_ffn_b1"].reshape(KT, P).T,
        "f_w2": tiles(g["L0_ffn_W2"]),
        "f_b2": g["L0_ffn_b2"],
        "f_v": tiles(g["L0_ffn_V"].reshape(FK * FR, D).T),
        "f_u": tiles(g["L0_ffn_U"].transpose(0, 2, 1).reshape(FK * FR, D)),
        "a_w": tiles(g["L1_attn_Wqkv_w"].T),
        "a_b": g["L1_attn_Wqkv_b"].reshape(6, P).T,
        "a_ow": tiles(g["L1_attn_out_w"].T),
        "aob": g["L1_attn_out_b"],
        "w5": np.concatenate([g["L1_xattn_Wq"].reshape(H2, K2, KT, P).transpose(0, 3, 2, 1).reshape(H2, P, KT * K2),
                              g["L1_xattn_w_kc_q"]], axis=2),
        "qr_T": g["L1_xattn_W_qr"].transpose(2, 0, 1),
        "kr_T": g["L1_xattn_W_kr"].transpose(2, 0, 1),
        "kc_kv": g["L1_xattn_w_kc_kv"].transpose(1, 0, 2),
        "wo_T": g["L1_xattn_Wo"].reshape(D, H2, K2).transpose(2, 1, 0),
        "e_gate": tiles(g["L1_ffn_w_gate"]),
        "e_gu": g["L1_ffn_w_gate_up"].reshape(E6, KT, P, 2 * I6).transpose(2, 1, 0, 3),
        "e_sgu": tiles(g["L1_ffn_w_sh_gate_up"]),
        "e_dn": g["L1_ffn_w_down"].transpose(1, 0, 2),
        "e_sdn": tiles(g["L1_ffn_w_sh_down"]),
    }


def constants(np):
    i = np.arange(P)
    same = (i[:, None] // CHUNK == i[None, :] // CHUNK) & (i[:, None] <= i[None, :])

    def tables(length, dim):
        inv = np.float32(1.0) / np.float32(10000.0) ** (np.arange(0, dim, 2, dtype=np.float32) / np.float32(dim))
        f = np.arange(length, dtype=np.float32)[:, None] * inv[None, :]
        return np.repeat(np.sin(f), 2, axis=-1), np.repeat(np.cos(f), 2, axis=-1)

    sin_k, cos_k = tables(S, XC)
    sin_k[:, 0:XC // 2] *= -1
    sin_q, cos_q = tables(S, Q2)
    rows = np.arange(P) % 32 // 16
    pick = (np.arange(P)[None, None, :] // FR + 2 * np.arange(FM)[None, :, None] == np.arange(FK)[:, None, None])
    return {
        "cos_k": cos_k.reshape(TB, P, XC).transpose(1, 0, 2),
        "sin_k": sin_k.reshape(TB, P, XC).transpose(1, 0, 2),
        "cos_q": cos_q.T.reshape(2, QH, S).transpose(1, 0, 2),
        "sin_q": sin_q.T.reshape(2, QH, S).transpose(1, 0, 2),
        "f_sel": pick.astype(np.float32),
        "a_par": np.stack([rows == 0, rows == 1], axis=1).astype(np.float32),
        "e_rev": np.arange(E6, 0, -1).astype(np.float32),
        "ident": np.eye(P, dtype=np.float32),
        "mask": (0.5 * same).astype(np.float32),
    }


def decoder(nc, a, out):
    with ExitStack() as kept:
        def sb(name, shape, dt=F32):
            return kept.enter_context(nc.sbuf_tensor(name, shape, dt))

        def passing(stack, name, shape, dt=F32):
            return stack.enter_context(nc.sbuf_tensor(name, shape, dt))

        def sem(name):
            return kept.enter_context(nc.semaphore(name))

        bank = [kept.enter_context(nc.psum_tensor(f"bank{n}", [P, 512], F32)) for n in range(8)]

        X = sb("X", [P, NT, D])
        HN = sb("HN", [P, NT, D])
        HT = sb("HT", [P, KT, T])
        ident = sb("ident", [P, P])
        ln_stat = sb("ln_stat", [P, NT, 6])
        ln_mv = sb("ln_mv", [P, NT, 2])
        ln_var = sb("ln_var", [P, NT])
        ln_r = sb("ln_r", [P, NT])
        ln_t = sb("ln_t", [P, NT])
        ln_rstd = sb("ln_rstd", [P, NT])
        ln_none = sb("ln_none", [P, 1])
        half = sb("half", [P, 2 * NT])
        with ExitStack() as at_end:
            passing(at_end, "big_first_half", [P, 8192])
            down_hi, down_lo = [passing(at_end, n, [P, UNITS, D], F32R) for n in ("down_hi", "down_lo")]
            act_hi, act_lo = [passing(at_end, n, [P, 3, S], F32R) for n in ("act_hi", "act_lo")]
        big = sb("big", [P, 16384])
        work = sb("work", [P, 9216])

        o_w = sb("o_w", [P, H0, D])
        b_w = sb("b_w", [P, KT, H0])
        bb_row = sb("bb_row", [P, H0])
        ob_row = sb("ob_row", [P, D])
        mask = sb("mask", [P, P])
        beta = sb("beta", [P, NT, H0])
        bt = work[:, 7 * T:7 * T + 6 * NT * H0].rearrange("p (n c) -> p n c", n=6)
        norm = sb("norm", [P, 4, 2 * NT])
        sumsq = sb("sumsq", [P, 2, 2, NT])
        outT = big[:, :].rearrange("p (h t) -> p h t", h=H0)
        qkT = work[:, 0:2 * T].rearrange("p (n t) -> p n t", n=2)
        qk_tok = work[:, 2 * T:3 * T].rearrange("p (t c) -> p t c", t=4)
        attn = work[:, 3 * T:4 * T].rearrange("p (t i) -> p t i", t=NT)
        v_tok = work[:, 4 * T:6 * T].rearrange("p (j t d) -> p j t d", j=2, t=NT)
        gate = work[:, 6 * T:8 * T].rearrange("p (j t d) -> p j t d", j=2, t=NT)
        tanh_g = work[:, 8 * T:8 * T + 256].rearrange("p (n d) -> p n d", n=2)
        qkv_b = work[:, 8 * T + 256:9 * T].rearrange("p (j c) -> p j c", j=2)
        gated = HN[:, 0:NT // 2, :].rearrange("p (t o) d -> p t o d", t=NT // 2).rearrange("p t o (u d) -> p (t o u) d", u=2)
        w_new = HN[:, NT // 2:NT, :].rearrange("p t d -> p (t d)")
        w_first = o_w[:, 0:KT * 4 * D0 // D, :].rearrange("p h d -> p (h d)")
        sq_out = sb("sq_out", [P, 2, D0])
        PJ = bank[0:3]
        TQ = bank[3][:, :].rearrange("p (n t) -> p n t", n=2)
        SC = [b[:, :].rearrange("p (t i) -> p t i", t=4) for b in bank[4:6]]
        OV = [b[:, :].rearrange("p (t d) -> p t d", t=4) for b in bank[6:8]]
        PRB = bank[6][:, 0:NT * H0]

        ctx_tok = work[:, 3 * T:3 * T + NT * XC].rearrange("p (t c) -> p t c", t=NT)
        ctxT = work[0:XC, 2 * T:3 * T]
        wk_T = sb("wk_T", [XC, XC])
        bk_col = sb("bk_col", [XC, 1])
        bk_row = sb("bk_row", [P, XC])
        kvT = sb("kvT", [XC, T])
        kv = sb("kv", [P, NT, XC])
        cos_k = work[:, 0:2 * XC].rearrange("p (t c) -> p t c", t=TB)
        sin_k = work[:, 2 * XC:4 * XC].rearrange("p (t c) -> p t c", t=TB)
        rot_k = work[:, 4 * XC:4 * XC + NT * XC].rearrange("p (t c) -> p t c", t=NT)
        lat2 = work[:, 5 * T:6 * T].rearrange("p (t c) -> p t c", t=NT)
        lat = sb("lat", [P, NT, XC])
        latT = sb("latT", [P, T])

        x_sim = work[:, 0:1024].rearrange("p (n t j) -> p n t j", n=2, t=TB)
        x_e = work[:, 1024:2048].rearrange("p (n t j) -> p n t j", n=2, t=TB)
        x_oT = work[0:XC, 2048:2560].rearrange("p (n i) -> p n i", n=2)
        x_stat = sb("x_stat", [P, TB, 6])
        x_mv = sb("x_mv", [P, TB, 2])
        x_v = sb("x_v", [P, 4, TB])
        x_nm = sb("x_nm", [P, 2, TB])
        x_sum = sb("x_sum", [P, 2, TB])
        x_rc = sb("x_rc", [P, TB])
        XO = bank[4]
        XS = bank[5][:, :].rearrange("p (t j) -> p t j", t=TB)

        f_b1 = sb("f_b1", [P, KT])
        f_w2 = sb("f_w2", [P, KT, FK])
        f_b2 = sb("f_b2", [P, FK])
        f_h = work[:, 2560:3072].rearrange("p (m t) -> p m t", m=KT)
        f_vx = work[:, 3072:4096].rearrange("p (m t) -> p m t", m=FM)
        f_ax = work[:, 4096:5120].rearrange("p (m t) -> p m t", m=FM)
        f_aT = work[0:FK, 5120:5376]
        f_al = sb("f_al", [P, 3, TB, FK])
        f_st = sb("f_st", [P, 3, TB])
        FH = bank[0][:, :].rearrange("p (m t) -> p m t", m=KT)
        FL = bank[1][:, 0:TB * FK].rearrange("p (t k) -> p t k", t=TB)
        FT = bank[1][0:FK, 0:S]
        FA = [b[:, :].rearrange("p (m t) -> p m t", m=2) for b in bank[2:4]]
        FX = FA
        FO = bank[4][:, :].rearrange("p (t d) -> p t d", t=TB)

        wo_T = o_w[:, :, :]
        Mw = o_w[:, 0:H2 // 2, :]
        WP = bank[6]
        kc_kv = big[:, 8192:8192 + H2 * XC].rearrange("p (h c) -> p h c", h=H2)
        qr_T = big[0:R2, 9216:9216 + H2 * Q2].rearrange("p (h q) -> p h q", h=H2)
        kr_T = big[0:R2, 12288:12288 + H2 * XC].rearrange("p (h c) -> p h c", h=H2)

        a_b = sb("a_b", [P, 6])
        a_bs = sb("a_bs", [P, 6])
        a_par = sb("a_par", [P, 2])
        aob_row = sb("aob_row", [P, D])
        a_q = work[:, 0:512].rearrange("p (m t) -> p m t", m=KT)
        a_k = work[:, 512:1536].rearrange("p (o m t) -> p o m t", o=2, m=KT)
        a_qn = big[:, 8192:8704].rearrange("p (m t) -> p m t", m=KT)
        a_kn = big[:, 8704:9728].rearrange("p (o m t) -> p o m t", o=2, m=KT)
        a_vT = work[:, 1536:2048].rearrange("p (m t) -> p m t", m=KT)
        a_v = work[:, 2048:2048 + TB * H1 * P].rearrange("p (l h c) -> p l h c", l=TB, h=H1)
        a_vd = [work[:, 2048 + n * HM * P:2048 + n * HM * P + HM * (P + D1)].rearrange("p (h c) -> p h c", h=HM)[:, :, 0:D1]
                for n in range(TB * KT)]
        a_p = work[:, 6272:7808].rearrange("p (n t s) -> p n t s", n=3, t=TB)
        a_cT = HN[:, TB:2 * TB, :]
        a_pT = HN[:, 2 * TB:4 * TB, :].rearrange("p (n l) t -> p n l t", n=2)
        a_nm = sb("a_nm", [P, 3, TB])
        a_sum = sb("a_sum", [P, 3, TB])
        a_rc = sb("a_rc", [P, 3, TB])
        AS = [b[:, :].rearrange("p (t s) -> p t s", t=TB) for b in (bank[2], bank[3], bank[0])]
        AT = [b[:, :].rearrange("p (l t) -> p l t", l=TB) for b in bank[4:6]]
        AC = bank[6:8]
        AB = bank[1][:, :].rearrange("p (m t) -> p m t", m=KT)

        l_q = work[:, 0:1024]
        l_rot = work[0:QH, 1024:3072].rearrange("p (o t) -> p o t", o=2)
        l_pr = work[0:QH, 3072:5120].rearrange("p (n t) -> p n t", n=4)
        l_p = work[:, 6144:7168].rearrange("p (n t l) -> p n t l", n=2, t=TB)
        l_pT = work[:, 7680:8192].rearrange("p (l t) -> p l t", l=TB)
        l_cT = big[:, 8192:16384].rearrange("p (m t) -> p m t", m=H2 // 2)
        g_now = work[0:QH, 8192:8192 + 8 * XC].rearrange("p (o j n c) -> p o j n c", o=2, j=2, n=2)
        l_nm = sb("l_nm", [P, 2, TB])
        l_sum = sb("l_sum", [P, 2, TB])
        l_rc = sb("l_rc", [P, 2, TB])
        LR = bank[2:4]
        LU = bank[4]
        LS = bank[5][:, :].rearrange("p (t l) -> p t l", t=TB)
        LT = bank[6][:, :].rearrange("p (l t) -> p l t", l=TB)
        LC = bank[7][:, :].rearrange("p (n t) -> p n t", n=2)

        e_gate = sb("e_gate", [P, KT, E6])
        e_rev = sb("e_rev", [P, E6])
        e_gu = big[:, 0:4096].rearrange("p (k e f) -> p k e f", k=KT, e=E6)
        e_sgu = big[:, 4096:6144].rearrange("p (k f) -> p k f", k=KT)
        e_dn = big[:, 6144:8192].rearrange("p (e d) -> p e d", e=E6)
        e_r = work[:, 4096:4096 + 6 * NT * E6].rearrange("p (n t e) -> p n t e", n=6, t=NT)
        e_s = sb("e_s", [P, 6, NT])
        e_comb = sb("e_comb", [P, NT, E6])
        e_th = work[:, 2048:2560].rearrange("p (n t) -> p n t", n=2)
        e_sg = work[:, 2560:3072].rearrange("p (n t) -> p n t", n=2)
        e_act = work[:, 3072:3584].rearrange("p (n t) -> p n t", n=2)
        EG = [b[:, :].rearrange("p (g t) -> p g t", g=2) for b in bank[0:2]]
        EY = [b[:, :].rearrange("p (t d) -> p t d", t=TB) for b in bank[2:4]]
        ES = bank[4:6]
        EL = bank[6][:, 0:NT * E6].rearrange("p (t e) -> p t e", t=NT)

        with ExitStack() as early:
            H_hi, H_lo = passing(early, "H_hi", [P, KT, T], F32R), passing(early, "H_lo", [P, KT, T], F32R)
            W_hi, W_lo = [passing(early, n, [P, 2, KT, 4 * D0], F32R) for n in ("W_hi", "W_lo")]

        w5 = sb("w5", [P, 2, KT * K2 + Q2])
        e_sdn = sb("e_sdn", [P, SF, D])
        cos_q = sb("cos_q", [QH, 2, S])
        sin_q = sb("sin_q", [QH, 2, S])
        Gw = sb("Gw", [QH, 2, H2, XC])

        with ExitStack() as mid:
            f_wvu = passing(mid, "f_wvu", [P, 2048])
            gam_row = passing(mid, "gam_row", [P, S])
            bet_row = passing(mid, "bet_row", [P, S])
            f_w1 = passing(mid, "f_w1", [P, KT, D])
            f_sel = passing(mid, "f_sel", [FK, FM, P])
            a_w = passing(mid, "a_w", [P, KT, 3 * D])
            a_ow = passing(mid, "a_ow", [P, KT, D])
        f_v = f_wvu[:, 0:1024].rearrange("p (k c) -> p k c", k=KT)
        f_u = f_wvu[:, 1024:2048].rearrange("p (m d) -> p m d", m=FM)
        with ExitStack() as late:
            l_u = passing(late, "l_u", [P, 2, T], F32R)
            lat_hi, lat_lo = passing(late, "lat_hi", [P, T], F32R), passing(late, "lat_lo", [P, T], F32R)
        with ExitStack() as last:
            E_hi, E_lo = passing(last, "E_hi", [P, KT, T], F32R), passing(last, "E_lo", [P, KT, T], F32R)
            U_hi, U_lo = [passing(last, n, [P, 2, KT, 2, I6], F32R) for n in ("U_hi", "U_lo")]

        def unit_weights(u):
            if u < E6:
                return e_gu[:, :, u, :].rearrange("p k (g f) -> p k g f", g=2)
            return e_sgu[:, :, :].rearrange("p k (g f) -> p k g f", g=2)[:, :, :, (u - E6) * P:(u - E6) * P + P]

        def down_weights(n):
            return e_dn[:, 4 * n:4 * n + 4, :] if 4 * n < E6 else e_sdn[:, :, :]

        ld_x = [sem(f"ld_x{b}") for b in range(B)]
        ld_c = sem("ld_c")
        ld_1 = sem("ld_1")
        ld_w = sem("ld_w")
        ld_b = [sem(f"ld_b{j}") for j in range(2)]
        h_hi = sem("h_hi")
        h_lo = sem("h_lo")
        w_hi = sem("w_hi")
        w_lo = sem("w_lo")
        ld_o = sem("ld_o")
        dve = sem("dve")
        consts = sem("consts")
        ln_ve = sem("ln_ve")
        ln_pw = sem("ln_pw")
        ln_h = sem("ln_h")
        ln_tr = sem("ln_tr")
        ln_ht = sem("ln_ht")
        x_bias = sem("x_bias")
        bt_mm = sem("bt_mm")
        bt_abs = sem("bt_abs")
        bt_exp = sem("bt_exp")
        bt_w = sem("bt_w")
        bt_ln = sem("bt_ln")
        pj_mm = sem("pj_mm")
        tanh_done = sem("tanh_done")
        qkv_ok = sem("qkv_ok")
        pj_read = sem("pj_read")
        sq_ok = sem("sq_ok")
        ss_read = sem("ss_read")
        ss_pow = sem("ss_pow")
        tq_mm = sem("tq_mm")
        tq_ok = sem("tq_ok")
        sc_mm = sem("sc_mm")
        masked = sem("masked")
        pv_mm = sem("pv_mm")
        gated_ok = sem("gated_ok")
        tr_mm = sem("tr_mm")
        outT_ok = sem("outT_ok")
        o_mm = sem("o_mm")
        o_read = sem("o_read")
        ld_cx = sem("ld_cx")
        ld_2 = sem("ld_2")
        ld_3 = sem("ld_3")
        ld_4 = sem("ld_4")
        ld_g = sem("ld_g")
        ld_p = sem("ld_p")
        ld_t = sem("ld_t")
        ld_6 = sem("ld_6")
        kvt_mm = sem("kvt_mm")
        kvt_ok = sem("kvt_ok")
        kvn_mm = sem("kvn_mm")
        kvn_ok = sem("kvn_ok")
        lat_ok = sem("lat_ok")
        lat_mm = sem("lat_mm")
        latT_ok = sem("latT_ok")
        xo_mm = sem("xo_mm")
        xo_ok = sem("xo_ok")
        xs_mm = sem("xs_mm")
        xs_ve = sem("xs_ve")
        xs_pw = sem("xs_pw")
        xs_nm = sem("xs_nm")
        xs_exp = sem("xs_exp")
        xs_free = sem("xs_free")
        fh_mm = sem("fh_mm")
        fh_ok = sem("fh_ok")
        fx_mm = sem("fx_mm")
        fx_ok = sem("fx_ok")
        fl_mm = sem("fl_mm")
        fl_ex = sem("fl_ex")
        fl_al = sem("fl_al")
        fl_e = sem("fl_e")
        fa_tr = sem("fa_tr")
        fa_T = sem("fa_T")
        fa_mm = sem("fa_mm")
        fa_ok = sem("fa_ok")
        fo_mm = sem("fo_mm")
        fo_read = sem("fo_read")
        wp_mm = sem("wp_mm")
        wp_ok = sem("wp_ok")
        a_bias = sem("a_bias")
        a_mm = sem("a_mm")
        a_ok = sem("a_ok")
        a_now = sem("a_now")
        av_tr = sem("av_tr")
        av_ok = sem("av_ok")
        as_mm = sem("as_mm")
        as_nm = sem("as_nm")
        as_exp = sem("as_exp")
        at_mm = sem("at_mm")
        at_ev = sem("at_ev")
        at_od = sem("at_od")
        as_rc = sem("as_rc")
        ap_ok = sem("ap_ok")
        ac_mm = sem("ac_mm")
        ac_T = sem("ac_T")
        ao_mm = sem("ao_mm")
        ao_read = sem("ao_read")
        l_q_mm = sem("l_q_mm")
        l_q_ok = sem("l_q_ok")
        lb_mm = sem("lb_mm")
        lb_rot = sem("lb_rot")
        lb_add = sem("lb_add")
        g_ok = sem("g_ok")
        lat_r = sem("lat_r")
        lu_mm = sem("lu_mm")
        lu_hi = sem("lu_hi")
        lu_ok = sem("lu_ok")
        ls_mm = sem("ls_mm")
        ls_nm = sem("ls_nm")
        ls_exp = sem("ls_exp")
        lt_mm = sem("lt_mm")
        lt_ok = sem("lt_ok")
        lv_mm = sem("lv_mm")
        lp_ok = sem("lp_ok")
        lc_ok = sem("lc_ok")
        lf_mm = sem("lf_mm")
        lf_read = sem("lf_read")
        er_mm = sem("er_mm")
        er_sub = sem("er_sub")
        er_exp = sem("er_exp")
        e_hi = sem("e_hi")
        e_lo = sem("e_lo")
        u_hi = sem("u_hi")
        u_lo = sem("u_lo")
        eg_mm = sem("eg_mm")
        eg_th = sem("eg_th")
        eg_ok = sem("eg_ok")
        ea_hi = sem("ea_hi")
        ea_lo = sem("ea_lo")
        d_hi = sem("d_hi")
        d_lo = sem("d_lo")
        ed_mm = sem("ed_mm")
        ey_ok = sem("ey_ok")
        x_done = sem("x_done")
        ld_w5 = [sem(f"ld_w5{j}") for j in range(2)]
        s_out = sem("s_out")

        block = kept.enter_context(nc.Block())

        xv = a["x"].rearrange("b (t p) d -> p (b t) d", p=P)
        ov = out.rearrange("b (t p) d -> p (b t) d", p=P)

        @block.sync
        def _(sp):
            for b in range(B):
                sp.dma_start(X[:, TB * b:TB * b + TB, :], xv[:, TB * b:TB * b + TB, :]).then_inc(ld_x[b], 16)
                if b == 0:
                    sp.dma_start(ident[:, :], a["ident"]).then_inc(ld_c, 16)
            sp.dma_start(w_first, a["w_head"][0]).then_inc(ld_w, 16)
            for dst, src in ((ctxT, "ctxT"), (wk_T[:, :], "wk_T"), (bk_col[:, :], "bk"), (ctx_tok, "ctx"),
                             (cos_k, "cos_k"), (sin_k, "sin_k")):
                sp.dma_start(dst, a[src]).then_inc(ld_cx, 16)
            sp.dma_start(bk_row[:, :], a["bk"].rearrange("c o -> (c o)").partition_broadcast(P)).then_inc(ld_cx, 16)
            for dst, src in ((b_w, "b_w"), (mask, "mask")):
                sp.dma_start(dst[:], a[src]).then_inc(ld_1, 16)
            for dst, src in ((bb_row, "bb"), (ob_row, "ob")):
                sp.dma_start(dst[:, :], a[src].partition_broadcast(P)).then_inc(ld_1, 16)
            for j in range(2):
                sp.dma_start(qkv_b[:, j], a["qkv_b"][j].partition_broadcast(P)).then_inc(ld_b[j], 16)
            sp.wait_ge(ln_tr, B)
            sp.dma_start(w_new, a["w_head"][1]).then_inc(ld_w, 16)
            sp.wait_ge(w_lo, 1)
            sp.dma_start(o_w[:], a["o_w"]).then_inc(ld_o, 16)
            with nc.sync.Fori(1, H0 // 2) as i:
                for j in range(2):
                    sp.wait_ge(w_lo, 2 * i + j)
                    sp.dma_start(w_new, a["w_head"][2 * i + j]).then_inc(ld_w, 16)
                    sp.wait_ge(qkv_ok, 2 * NT * i - NT + NT * j)
                    sp.dma_start(qkv_b[:, j], a["qkv_b"][2 * i + j].partition_broadcast(P)).then_inc(ld_b[j], 16)
            sp.wait_ge(pj_mm, NT * H0)
            for dst, src in ((gam_row, "gam"), (bet_row, "bet")):
                sp.dma_start(dst[:, :], a[src].partition_broadcast(P)).then_inc(ld_2, 16)
            for dst, src in ((f_w1[:], "f_w1"), (f_b1[:], "f_b1"), (f_w2[:], "f_w2"), (f_sel[:], "f_sel"), (f_v, "f_v"), (f_u, "f_u")):
                sp.dma_start(dst, a[src]).then_inc(ld_3, 16)
            sp.dma_start(f_b2[:, :], a["f_b2"].partition_broadcast(P)).then_inc(ld_3, 16)
            for dst, src in ((a_w, "a_w"), (a_b, "a_b"), (a_par, "a_par"), (a_ow, "a_ow"), (e_gate, "e_gate")):
                sp.dma_start(dst[:], a[src]).then_inc(ld_4, 16)
            for dst, src in ((aob_row, "aob"), (e_rev, "e_rev")):
                sp.dma_start(dst[:, :], a[src].partition_broadcast(P)).then_inc(ld_4, 16)
            sp.wait_ge(o_mm, NT)
            for dst, src in ((qr_T, "qr_T"), (kr_T, "kr_T")):
                sp.dma_start(dst, a[src]).then_inc(ld_g, 16)
            for dst, src in ((wo_T, "wo_T"), (kc_kv, "kc_kv")):
                sp.dma_start(dst, a[src]).then_inc(ld_p, 16)
            for dst, src in ((cos_q, "cos_q"), (sin_q, "sin_q")):
                sp.dma_start(dst[:], a[src]).then_inc(ld_t, 16)
            for j in range(2):
                sp.dma_start(w5[:, j, :], a["w5"][j]).then_inc(ld_w5[j], 16)
            for dst, src in ((e_gu, "e_gu"), (e_sgu, "e_sgu"), (e_dn, "e_dn"), (e_sdn[:], "e_sdn")):
                sp.dma_start(dst, a[src]).then_inc(ld_6, 16)
            with nc.sync.Fori(1, H2 // 2) as p:
                for j in range(2):
                    sp.wait_ge(lb_mm, 4 * p - 2 + 2 * j)
                    sp.dma_start(w5[:, j, :], a["w5"][2 * p + j]).then_inc(ld_w5[j], 16)
            for b in range(B):
                sp.wait_ge(x_done, b + 1)
                sp.dma_start(ov[:, TB * b:TB * b + TB, :], X[:, TB * b:TB * b + TB, :]).then_inc(s_out, 16)
            sp.wait_ge(s_out, 16 * B)

        @block.gpsimd
        def _(pool):
            nc.gpsimd.memset(half[:, :], -0.5).then_inc(consts, 1)
            pool.wait_ge(consts, 1)

            def ln_power(s, b, place=None):
                at = TB * b if place is None else place
                pool.wait_ge(ln_ve, ln_before(s, b) + 1)
                nc.gpsimd.tensor_tensor(ln_r[:, at:at + TB], ln_var[:, at:at + TB], half[:, 0:TB],
                                        ALU.pow).then_inc(ln_pw, 1)

            def weights_lo(h, j, src):
                pool.wait_ge(w_hi, h + 1)
                nc.gpsimd.tensor_tensor(W_lo[:, j].rearrange("p k c -> p (k c)"), src,
                                        W_hi[:, j].bitcast(F32).rearrange("p k c -> p (k c)"), ALU.subtract).then_inc(w_lo, 1)

            for b in range(B):
                ln_power(0, b)
                if b == 2:
                    weights_lo(0, 0, w_first)
            for b in range(B):
                pool.wait_ge(h_hi, b + 1)
                nc.gpsimd.tensor_tensor(H_lo[:, :, b * S:b * S + S], HT[:, :, b * S:b * S + S],
                                        H_hi[:, :, b * S:b * S + S].bitcast(F32), ALU.subtract).then_inc(h_lo, 1)

            pool.wait_ge(ln_h, B)
            pool.wait_ge(ld_1, 16 * 4)
            nc.gpsimd.tensor_tensor(X[:, :, :], X[:, :, :], ob_row[:, :].unsqueeze(1).broadcast_to([P, NT, D]),
                                    ALU.add).then_inc(x_bias, 1)

            def norm_power(h):
                pool.wait_ge(ss_read, h + 1)
                nc.gpsimd.tensor_tensor(norm[:, 1, :], norm[:, 0, :], half[:, :], ALU.pow).then_inc(ss_pow, 1)

            weights_lo(1, 1, w_new)
            norm_power(0)
            with nc.gpsimd.Fori(1, H0 // 2) as i:
                for j in range(2):
                    weights_lo(2 * i + j, j, w_new)
                    norm_power(2 * i + j - 1)
            norm_power(H0 - 1)

            def similarity_power(b):
                pool.wait_ge(xs_ve, b + 1)
                nc.gpsimd.tensor_tensor(x_v[:, 1, :], x_v[:, 0, :], half[:, 0:TB], ALU.pow).then_inc(xs_pw, 1)

            for b in range(B):
                ln_power(1, b)
                if b >= 2:
                    similarity_power(b - 2)
            for n in range(1, B + 2):
                if n <= B:
                    ln_power(2, n - 1)
                if n + 1 < B:
                    similarity_power(n + 1)
                if n >= 2:
                    ln_power(3, n - 2)
            pool.wait_ge(fo_read, B)
            nc.gpsimd.memset(work[:, 2048:6272], 0.0).then_inc(consts, 1)
            pool.wait_ge(ln_h, 4 * B)
            pool.wait_ge(ld_4, 16 * 7)
            nc.gpsimd.tensor_tensor(X[:, :, :], X[:, :, :], aob_row[:, :].unsqueeze(1).broadcast_to([P, NT, D]),
                                    ALU.add).then_inc(x_bias, 1)

            def normalise(b, n):
                pool.wait_ge(as_rc, H1 * b + n + 1)
                nc.gpsimd.tensor_tensor(a_p[:, n % 3], a_p[:, n % 3],
                                        a_rc[:, n % 3, :].unsqueeze(2).broadcast_to([P, TB, S]), ALU.mult).then_inc(ap_ok, 1)

            for n in range(H1):
                normalise(0, n)
            with nc.gpsimd.Fori(1, B) as b:
                for n in range(H1):
                    if n == LN_AT + 1:
                        ln_power(4, b - 1, 0)
                    normalise(b, n)
            ln_power(4, B - 1, 0)

            def rotate_sum(r, c, after):
                if after:
                    pool.wait_ge(lu_mm, r - 1)
                pool.wait_ge(lb_rot, 2 * r + 2)
                cols = slice(512 * c, 512 * c + 512)
                nc.gpsimd.tensor_tensor(l_rot[:, 0, cols], l_pr[:, 0, :], l_pr[:, 1, :], ALU.subtract)
                nc.gpsimd.tensor_tensor(l_rot[:, 1, cols], l_pr[:, 2, :], l_pr[:, 3, :], ALU.add).then_inc(lb_add, 1)

            def pair_sums(p, use):
                if use:
                    pool.wait_ge(lu_mm, 4 * p)
                for n in range(2):
                    ins = nc.gpsimd.tensor_copy(g_now[:, :, :, n, :], Gw[:, :, ds(2 * p, 2), :])
                ins.then_inc(g_ok, 1)
                for r in range(4):
                    rotate_sum(4 * p + r, r % 2, use or r >= 2)
                    if r == 0 and not use:
                        pool.wait_ge(lat_r, 1)
                        nc.gpsimd.tensor_tensor(lat_lo[:, :], latT[:, :], lat_hi[:, :].bitcast(F32), ALU.subtract).then_inc(lat_r, 1)

            pair_sums(0, False)
            with nc.gpsimd.Fori(1, H2 // 2) as p:
                pair_sums(p, True)

            def layer_norm_lo(b):
                pool.wait_ge(e_hi, b + 1)
                cols = slice(b * S, b * S + S)
                nc.gpsimd.tensor_tensor(E_lo[:, :, cols], HT[:, :, cols], E_hi[:, :, cols].bitcast(F32), ALU.subtract).then_inc(e_lo, 1)

            def unit_lo(b, u):
                pool.wait_ge(u_hi, UNITS * b + u + 1)
                for k in range(KT):
                    ins = nc.gpsimd.tensor_tensor(U_lo[:, u % 2, k], unit_weights(u)[:, k], U_hi[:, u % 2, k].bitcast(F32),
                                                  ALU.subtract)
                ins.then_inc(u_lo, 1)

            for b in range(B):
                ln_power(5, b)
                if b:
                    layer_norm_lo(b - 1)
                if b == 2:
                    unit_lo(0, 0)
                    unit_lo(0, 1)
            layer_norm_lo(B - 1)
            for u in range(2, UNITS):
                unit_lo(0, u)
            with nc.gpsimd.Fori(1, B) as b:
                for u in range(UNITS):
                    unit_lo(b, u)

        @block.vector
        def _(v):
            link = Chain(v, dve)

            def ln_stats(s, b, place=None):
                at = TB * b if place is None else place
                two = slice(at, at + TB)
                for i in range(TB):
                    ins = nc.vector.bn_stats(ln_stat[:, at + i, :], X[:, ds(TB * b + i, 1), :].rearrange("p o c -> p (o c)"))
                link(ins)
                if place is not None:
                    nc.vector.memset(ln_none[:, :], 0.0)
                for i in range(TB):
                    ins = nc.vector.bn_aggr(ln_mv[:, at + i, :], ln_stat[:, at + i, :])
                link(ins)
                nc.vector.tensor_scalar(ln_var[:, two], ln_mv[:, two, 1], LN_EPS, None, ALU.add).then_inc(ln_ve, 1)

            def ln_apply(s, b, place=None):
                at = TB * b if place is None else place
                two = slice(at, at + TB)
                v.wait_ge(ln_pw, ln_before(s, b) + 1)
                link(nc.vector.scalar_tensor_tensor(out=ln_t[:, two], in0=ln_r[:, two], scalar=-0.5, in1=ln_r[:, two],
                                                    op0=ALU.mult, op1=ALU.mult))
                link(nc.vector.tensor_tensor(ln_t[:, two], ln_t[:, two], ln_var[:, two], ALU.mult))
                link(nc.vector.scalar_tensor_tensor(out=ln_rstd[:, two], in0=ln_t[:, two], scalar=1.5, in1=ln_r[:, two],
                                                    op0=ALU.add, op1=ALU.mult))
                for i in range(TB):
                    ins = nc.vector.tensor_scalar(HN[:, at + i:at + i + 1, :], X[:, ds(TB * b + i, 1), :],
                                                  ln_mv[:, at + i, 0:1], ln_rstd[:, at + i:at + i + 1],
                                                  ALU.subtract, ALU.mult)
                ins.then_inc(ln_h, 1)

            def ln_rows(s, b, place=None):
                ln_stats(s, b, place)
                ln_apply(s, b, place)

            for b in range(B):
                v.wait_ge(ld_x[b], 16)
                ln_rows(0, b)

            v.wait_ge(ld_cx, 16 * 7)
            v.wait_ge(kvn_mm, 1)
            nc.vector.tensor_tensor(kv[:, :, :], bank[3][:, :].rearrange("p (t c) -> p t c", t=NT),
                                    bk_row[:, :].unsqueeze(1).broadcast_to([P, NT, XC]), ALU.add).then_inc(kvn_ok, 1)
            hf = XC // 2
            for b in range(B):
                two = slice(TB * b, TB * b + TB)
                nc.vector.tensor_tensor(rot_k[:, two, 0:hf], ctx_tok[:, two, hf:XC], sin_k[:, :, 0:hf], ALU.mult)
                nc.vector.tensor_tensor(rot_k[:, two, hf:XC], ctx_tok[:, two, 0:hf], sin_k[:, :, hf:XC], ALU.mult)
                ins = nc.vector.tensor_tensor(lat[:, two, :], ctx_tok[:, two, :], cos_k, ALU.mult)
            link(ins)
            link(nc.vector.tensor_tensor(lat[:, :, :], lat[:, :, :], rot_k, ALU.add))
            for j in range(2):
                ins = nc.vector.tensor_copy(lat2[:, :, j * XC:j * XC + XC], lat[:, :, :])
            ins.then_inc(lat_ok, 1)
            v.wait_ge(ld_1, 16 * 4)

            def norms_of(g, j):
                v.wait_ge(sq_ok, NT * g + NT)
                nc.vector.tensor_scalar(norm[:, 0, :], sumsq[:, j].rearrange("p n t -> p (n t)"), NORM_FLOOR, None, ALU.max).then_inc(ss_read, 1)

            def scale_of(g):
                v.wait_ge(ss_pow, g + 1)
                link(nc.vector.scalar_tensor_tensor(out=norm[:, 2, :], in0=norm[:, 1, :], scalar=-0.5,
                                                    in1=norm[:, 1, :], op0=ALU.mult, op1=ALU.mult))
                link(nc.vector.tensor_tensor(norm[:, 2, :], norm[:, 2, :], norm[:, 0, :], ALU.mult))
                link(nc.vector.scalar_tensor_tensor(out=norm[:, 3, :], in0=norm[:, 2, :], scalar=1.5,
                                                    in1=norm[:, 1, :], op0=ALU.add, op1=ALU.mult))
                link(nc.vector.tensor_tensor(norm[:, 3, NT:2 * NT], norm[:, 3, NT:2 * NT],
                                             beta[:, :, ds(g, 1)].rearrange("p t o -> p (t o)"), ALU.mult))

            def mask_scores(g, n):
                v.wait_ge(sc_mm, 2 * g + n + 1)
                for t in range(4 * n, 4 * n + 4):
                    ins = nc.vector.scalar_tensor_tensor(out=attn[:, t, :], in0=SC[n][:, t % 4, :],
                                                         scalar=norm[:, 3, NT + t:NT + t + 1], in1=mask[:, :],
                                                         op0=ALU.mult, op1=ALU.mult)
                ins.then_inc(masked, 1)

            def gate_out(g, j, n, after):
                if after and n == 0:
                    v.wait_ge(tr_mm, 2 * g)
                v.wait_ge(pv_mm, 2 * g + n + 1)
                for t in range(4 * n, 4 * n + 4):
                    ins = nc.vector.scalar_tensor_tensor(out=gated[:, t, :], in0=OV[n][:, t % 4, :],
                                                         scalar=norm[:, 3, t:t + 1], in1=gate[:, j, t, :],
                                                         op0=ALU.mult, op1=ALU.mult)
                ins.then_inc(gated_ok, 1)

            def take_tile(h, j, t, after, bias_after):
                if t == 0:
                    v.wait_ge(ld_b[j], 16 * bias_after + 16)
                    if after > 1:
                        v.wait_ge(gated_ok, 2 * h - 2)
                if after or t >= 4:
                    v.wait_ge(tq_mm, 4 * h + (t - 4) // 2 + 1)
                    v.wait_ge(sq_ok, NT * h + t - 3)
                v.wait_ge(tanh_done, NT * h + t + 1)
                nc.vector.tensor_tensor(qk_tok[:, t % 4, :], PJ[t % 3][:, 0:2 * D0], qkv_b[:, j, 0:2 * D0], ALU.add)
                nc.vector.tensor_tensor(v_tok[:, j, t, :], PJ[t % 3][:, 2 * D0:3 * D0], qkv_b[:, j, 2 * D0:3 * D0],
                                        ALU.add).then_inc(qkv_ok, 1)
                nc.vector.scalar_tensor_tensor(out=gate[:, j, t, :], in0=tanh_g[:, t % 2], scalar=1.0,
                                               in1=PJ[t % 3][:, 3 * D0:4 * D0], op0=ALU.add,
                                               op1=ALU.mult).then_inc(pj_read, 1)

            def head_rows(h, j, after, pairs):
                for t in range(NT):
                    take_tile(h, j, t, after, pairs)
                    if after and t == 0:
                        norms_of(h - 1, 1 - j)
                    if after and t == 2:
                        scale_of(h - 1)
                        mask_scores(h - 1, 0)
                    if after and t == 3:
                        mask_scores(h - 1, 1)
                    if after and t in (6, 7):
                        gate_out(h - 1, 1 - j, t - 6, after > 1)

            head_rows(0, 0, 0, 0)
            z, m, u, w, lw, c = [bt[:, n, :] for n in range(6)]
            v.wait_ge(bt_mm, 1)
            v.wait_ge(ld_1, 16 * 4)
            link(nc.vector.tensor_tensor(z.rearrange("p (t h) -> p t h", t=NT), PRB.rearrange("p (t h) -> p t h", t=NT),
                                         bb_row[:, :].unsqueeze(1).broadcast_to([P, NT, H0]), ALU.add))
            link(nc.vector.tensor_scalar(m, z, -1.0, None, ALU.mult))
            nc.vector.tensor_tensor(c, z, m, ALU.max).then_inc(bt_abs, 1)
            v.wait_ge(bt_abs, 1)
            v.wait_ge(bt_exp, 1)
            nc.vector.tensor_scalar(w, u, 1.0, None, ALU.add).then_inc(bt_w, 1)
            v.wait_ge(bt_w, 1)
            link(nc.vector.tensor_scalar(c, w, -1.0, None, ALU.add))
            link(nc.vector.tensor_tensor(c, u, c, ALU.subtract))
            link(nc.vector.reciprocal(m, w))
            link(nc.vector.tensor_tensor(c, c, m, ALU.mult))
            link(nc.vector.tensor_scalar(m, z, 0.0, None, ALU.max))
            link(nc.vector.tensor_tensor(c, c, m, ALU.add))
            v.wait_ge(bt_ln, 1)
            link(nc.vector.tensor_tensor(beta[:, :, :].rearrange("p t h -> p (t h)"), c, lw, ALU.add))

            head_rows(1, 1, 1, 0)
            with nc.vector.Fori(1, H0 // 2) as i, link.over(i, 1, H0 // 2, 8):
                for j in range(2):
                    head_rows(2 * i + j, j, 2, i)
            v.wait_ge(gated_ok, 2 * H0 - 2)
            norms_of(H0 - 1, 1)
            scale_of(H0 - 1)
            for n in range(2):
                mask_scores(H0 - 1, n)
            for n in range(2):
                gate_out(H0 - 1, 1, n, True)

            def similarity(b):
                n = b % 2
                v.wait_ge(xs_mm, b + 1)
                if b >= 2:
                    v.wait_ge(xs_exp, b - 1)
                for t in range(TB):
                    ins = nc.vector.bn_stats(x_stat[:, t, :], XS[:, t, :])
                link(ins)
                for t in range(TB):
                    ins = nc.vector.bn_aggr(x_mv[:, t, :], x_stat[:, t, :])
                link(ins)
                nc.vector.tensor_scalar(x_v[:, 0, :], x_mv[:, :, 1], X0_EPS, None, ALU.add).then_inc(xs_ve, 1)
                for t in range(TB):
                    ins = nc.vector.scalar_tensor_tensor(out=x_sim[:, n, t, :], in0=XS[:, t, :],
                                                         scalar=x_mv[:, t, 0:1], in1=gam_row[:, :],
                                                         op0=ALU.subtract, op1=ALU.mult)
                ins.then_inc(xs_free, 1)
                v.wait_ge(xs_pw, b + 1)
                link(nc.vector.scalar_tensor_tensor(out=x_v[:, 2, :], in0=x_v[:, 1, :], scalar=-0.5, in1=x_v[:, 1, :],
                                                    op0=ALU.mult, op1=ALU.mult))
                link(nc.vector.tensor_tensor(x_v[:, 2, :], x_v[:, 2, :], x_v[:, 0, :], ALU.mult))
                link(nc.vector.scalar_tensor_tensor(out=x_v[:, 3, :], in0=x_v[:, 2, :], scalar=1.5, in1=x_v[:, 1, :],
                                                    op0=ALU.add, op1=ALU.mult))
                for t in range(TB):
                    ins = nc.vector.scalar_tensor_tensor(out=x_sim[:, n, t, :], in0=x_sim[:, n, t, :],
                                                         scalar=x_v[:, 3, t:t + 1], in1=bet_row[:, :],
                                                         op0=ALU.mult, op1=ALU.add)
                link(ins)
                nc.vector.tensor_reduce(x_nm[:, n, :], x_sim[:, n], AX_X, ALU.max, negate=True).then_inc(xs_nm, 1)

            def attend_context(b):
                n = b % 2
                v.wait_ge(xs_exp, b + 1)
                link(nc.vector.reciprocal(x_rc[:, :], x_sum[:, n, :]))
                for t in range(TB):
                    ins = nc.vector.scalar_tensor_tensor(out=X[:, TB * b + t, :], in0=x_e[:, n, t, :],
                                                         scalar=x_rc[:, t:t + 1], in1=X[:, TB * b + t, :],
                                                         op0=ALU.mult, op1=ALU.add)
                link(ins)

            def mixture(b):
                wide = [P, TB, FK]
                lg, ex, al = f_al[:, 0], f_al[:, 1], f_al[:, 2]
                v.wait_ge(fl_mm, b + 1)
                link(nc.vector.tensor_tensor(lg, FL, f_b2[:, :].unsqueeze(1).broadcast_to(wide), ALU.add))
                link(nc.vector.tensor_reduce(f_st[:, 0, :], lg, AX_X, ALU.max))
                nc.vector.tensor_tensor(lg, lg, f_st[:, 0, :].unsqueeze(2).broadcast_to(wide), ALU.subtract).then_inc(fl_ex, 1)
                v.wait_ge(fl_e, b + 1)
                link(nc.vector.tensor_reduce(f_st[:, 1, :], ex, AX_X, ALU.add))
                link(nc.vector.reciprocal(f_st[:, 2, :], f_st[:, 1, :]))
                nc.vector.tensor_tensor(al, ex, f_st[:, 2, :].unsqueeze(2).broadcast_to(wide), ALU.mult).then_inc(fl_al, 1)

            def weigh(b):
                for n in range(2):
                    v.wait_ge(fa_mm, 2 * b + n + 1)
                    v.wait_ge(fx_ok, 2 * b + n + 1)
                    nc.vector.tensor_tensor(f_ax[:, 2 * n:2 * n + 2, :], f_vx[:, 2 * n:2 * n + 2, :], FA[n],
                                            ALU.mult).then_inc(fa_ok, 1)
                v.wait_ge(fo_mm, b + 1)
                nc.vector.tensor_tensor(X[:, TB * b:TB * b + TB, :], X[:, TB * b:TB * b + TB, :], FO, ALU.add).then_inc(fo_read, 1)
                v.wait_ge(fo_read, b + 1)

            v.wait_ge(x_bias, 1)
            v.wait_ge(ld_2, 32)
            for t in range(NT):
                v.wait_ge(o_mm, t + 1)
                nc.vector.tensor_tensor(X[:, t, :], X[:, t, :], bank[t % 2][:, 0:D], ALU.add).then_inc(o_read, 1)
                if t % TB == TB - 1:
                    v.wait_ge(o_read, t + 1)
                    ln_rows(1, t // TB)
                    if t // TB >= 2:
                        similarity(t // TB - 2)

            v.wait_ge(ld_4, 16 * 7)
            nc.vector.tensor_scalar(a_bs[:, 0:2], a_b[:, 0:2], D1 ** -0.5, None, ALU.mult)
            nc.vector.tensor_scalar(a_bs[:, 2:4], a_b[:, 2:4], a_par[:, 0:1], None, ALU.mult)
            nc.vector.tensor_scalar(a_bs[:, 4:6], a_b[:, 2:4], a_par[:, 1:2], None, ALU.mult).then_inc(a_bias, 1)
            v.wait_ge(ld_3, 16 * 7)
            for n in range(1, B + 2):
                if n >= 2:
                    mixture(n - 2)
                if n <= B:
                    attend_context(n - 1)
                    ln_rows(2, n - 1)
                if n + 1 < B:
                    similarity(n + 1)
                if n >= 2:
                    weigh(n - 2)
                    ln_rows(3, n - 2)

            def value_rows(b, after):
                v.wait_ge(av_tr, b + 1)
                if after:
                    v.wait_ge(ac_mm, KT * b)
                for n in range(TB * KT):
                    ins = nc.vector.tensor_copy(a_vd[n], bank[1][:, n * P:n * P + P].rearrange("p (h c) -> p h c", h=HM))
                ins.then_inc(av_ok, 1)

            def next_keys(b):
                v.wait_ge(a_ok, 3 * b + 2)
                nc.vector.tensor_copy(a_k, a_kn).then_inc(a_now, 1)

            def heads(b, between, more):
                for n in range(H1 + 2):
                    if n < H1:
                        v.wait_ge(as_mm, H1 * b + n + 1)
                        nc.vector.tensor_reduce(a_nm[:, n % 3, :], AS[n % 3], AX_X, ALU.max, negate=True).then_inc(as_nm, 1)
                    if n == 0:
                        value_rows(b, between)
                    if 1 <= n <= H1:
                        v.wait_ge(as_exp, H1 * b + n)
                        nc.vector.reciprocal(a_rc[:, (n - 1) % 3, :], a_sum[:, (n - 1) % 3, :]).then_inc(as_rc, 1)
                    if n == H1 - 1 and more:
                        next_keys(b + 1)
                    if n >= 2 and n % 2:
                        v.wait_ge(at_mm, H1 * b + n - 1)
                        nc.vector.tensor_copy(a_pT[:, 1], AT[1]).then_inc(at_od, 1)
                    if n == LN_AT and between:
                        attend_self(b - 1)
                    if n == LN_AT + 1 and between:
                        ln_stats(4, b - 1, 0)
                    if n == LN_AT + 2 and between:
                        ln_apply(4, b - 1, 0)

            def attend_self(b):
                v.wait_ge(ao_mm, b + 1)
                xb = X[:, ds(TB * b, TB), :]
                link(nc.vector.tensor_tensor(xb, xb, AB, ALU.add))
                v.sem_inc(ao_read, 1)

            next_keys(0)
            heads(0, False, True)
            v.wait_ge(x_bias, 2)
            with nc.vector.Fori(1, B - 1) as b, link.over(b, 1, B - 1, 6):
                heads(b, True, True)
            heads(B - 1, True, False)
            attend_self(B - 1)
            ln_rows(4, B - 1, 0)

            def rotate(r, part, after):
                if part == 0:
                    v.wait_ge(lb_mm, r + 1)
                    if after:
                        v.wait_ge(lb_add, r)
                products = ((0, cos_q[:, 0]), (1, sin_q[:, 0]), (1, cos_q[:, 1]), (0, sin_q[:, 1]))
                for n in (2 * part, 2 * part + 1):
                    src, table = products[n]
                    ins = nc.vector.tensor_tensor(l_pr[:, n, :].rearrange("p (b s) -> p b s", b=2),
                                                  LR[src][0:QH, :].rearrange("p (b s) -> p b s", b=2),
                                                  table.unsqueeze(1).broadcast_to([QH, 2, S]), ALU.mult)
                ins.then_inc(lb_rot, 1)

            def row_max(u, n):
                v.wait_ge(ls_mm, u + 1)
                nc.vector.tensor_reduce(l_nm[:, n % 2, :], LS, AX_X, ALU.max, negate=True).then_inc(ls_nm, 1)

            def query_lo(p, r):
                j, c = r // 2, r % 2
                upper, cols = slice(XC, 2 * XC), slice(512 * c, 512 * c + 512)
                v.wait_ge(lu_hi, 4 * p + r + 1)
                nc.vector.tensor_tensor(l_u[upper, j, cols], LU[upper, :], l_u[upper, j, cols].bitcast(F32),
                                        ALU.subtract).then_inc(lu_ok, 1)

            def row_scale(u, n):
                v.wait_ge(ls_exp, u + 1)
                link(nc.vector.reciprocal(l_rc[:, n % 2, :], l_sum[:, n % 2, :]))
                for t in range(TB):
                    ins = nc.vector.tensor_scalar(l_p[:, n % 2, t, :], l_p[:, n % 2, t, :], l_rc[:, n % 2, t:t + 1], None, ALU.mult)
                ins.then_inc(lp_ok, 1)

            def pair_rows(p, make, use):
                for k in range(10):
                    if use and k < 8 and k != LAST_AT:
                        row_max(8 * p - 8 + k, k)
                    if use and 1 <= k <= 8:
                        row_scale(8 * p - 8 + k - 1, k - 1)
                    if use and k == LAST_AT:
                        row_max(8 * p - 8 + k, k)
                    if make and k in ROT_AT:
                        r = ROT_AT.index(k)
                        for part in range(2):
                            rotate(4 * p + r, part, use or r)
                    if make and k in LAT_AT:
                        query_lo(p, LAT_AT.index(k))
                    if use and k == LAST_AT:
                        query_lo(p - 1, 3)

            v.wait_ge(ld_t, 32)
            pair_rows(0, True, False)
            with nc.vector.Fori(1, H2 // 2) as p, link.over(p, 1, H2 // 2, 8):
                pair_rows(p, True, True)
            pair_rows(H2 // 2, False, True)
            for t in range(NT):
                v.wait_ge(lf_mm, t + 1)
                nc.vector.tensor_tensor(X[:, t, :], X[:, t, :], bank[2 + t % 2][:, 0:D], ALU.add).then_inc(lf_read, 1)
                if t % TB == TB - 1:
                    v.wait_ge(lf_read, t + 1)
                    ln_rows(5, t // TB)

            def first_best(p, best, one, sc, mi):
                wide = [P, NT, E6]
                link(nc.vector.tensor_reduce(best, p, AX_X, ALU.max))
                link(nc.vector.tensor_tensor(sc, p, best.unsqueeze(2).broadcast_to(wide), ALU.is_equal))
                link(nc.vector.tensor_tensor(sc, sc, e_rev[:, :].unsqueeze(1).broadcast_to(wide), ALU.mult))
                link(nc.vector.tensor_reduce(mi, sc, AX_X, ALU.max))
                link(nc.vector.tensor_tensor(one, sc, mi.unsqueeze(2).broadcast_to(wide), ALU.is_equal))

            def route():
                wide = [P, NT, E6]
                lg, ex, p, one1, one2, sc = [e_r[:, n] for n in range(6)]
                mx, sm, rc, b1, b2, mi = [e_s[:, n, :] for n in range(6)]
                v.wait_ge(er_mm, 1)
                link(nc.vector.tensor_reduce(mx, EL, AX_X, ALU.max))
                nc.vector.tensor_tensor(lg, EL, mx.unsqueeze(2).broadcast_to(wide), ALU.subtract).then_inc(er_sub, 1)
                v.wait_ge(er_exp, 1)
                link(nc.vector.tensor_reduce(sm, ex, AX_X, ALU.add))
                link(nc.vector.reciprocal(rc, sm))
                link(nc.vector.tensor_tensor(p, ex, rc.unsqueeze(2).broadcast_to(wide), ALU.mult))
                first_best(p, b1, one1, sc, mi)
                link(nc.vector.scalar_tensor_tensor(out=lg.rearrange("p t e -> p (t e)"), in0=one1.rearrange("p t e -> p (t e)"),
                                                    scalar=-4.0, in1=p.rearrange("p t e -> p (t e)"), op0=ALU.mult, op1=ALU.add))
                first_best(lg, b2, one2, sc, mi)
                link(nc.vector.tensor_tensor(one1, one1, one2, ALU.add))
                link(nc.vector.tensor_tensor(sm, b1, b2, ALU.add))
                link(nc.vector.reciprocal(rc, sm))
                link(nc.vector.tensor_scalar(rc, rc, 0.5, None, ALU.mult))
                link(nc.vector.tensor_tensor(p, p, one1, ALU.mult))
                link(nc.vector.tensor_tensor(e_comb[:, :, :], p, rc.unsqueeze(2).broadcast_to(wide), ALU.mult))

            def down_weights_lo(n):
                v.wait_ge(d_hi, n + 1)
                nc.vector.tensor_tensor(down_lo[:, 4 * n:4 * n + 4], down_weights(n),
                                        down_hi[:, 4 * n:4 * n + 4].bitcast(F32), ALU.subtract).then_inc(d_lo, 1)

            def gated_lo(U, n):
                v.wait_ge(ea_hi, U + 1)
                nc.vector.tensor_tensor(act_lo[:, n % 3], e_act[:, n % 2], act_hi[:, n % 3].bitcast(F32),
                                        ALU.subtract).then_inc(ea_lo, 1)

            def gated_unit(b, u):
                U = UNITS * b + u
                n = u % 2
                v.wait_ge(eg_th, U + 1)
                link(nc.vector.scalar_tensor_tensor(out=e_sg[:, n, :], in0=e_th[:, n, :], scalar=1.0, in1=EG[n][:, 0, :],
                                                    op0=ALU.add, op1=ALU.mult))
                nc.vector.tensor_tensor(e_act[:, n, :], e_sg[:, n, :], EG[n][:, 1, :], ALU.mult).then_inc(eg_ok, 1)

            def add_expert(b, e, after):
                v.wait_ge(ed_mm, UNITS * b + e + 1)
                if after:
                    v.wait_ge(ey_ok, E6 * b + e)
                for t in range(TB):
                    xt = X[:, ds(TB * b + t, 1), :].rearrange("p o d -> p (o d)")
                    ins = nc.vector.scalar_tensor_tensor(out=xt, in0=EY[e % 2][:, t, :],
                                                         scalar=e_comb[:, ds(TB * b + t, 1), e].rearrange("p o -> p o"), in1=xt,
                                                         op0=ALU.mult, op1=ALU.add)
                ins.then_inc(ey_ok, 1)

            def moe_batch(b, after):
                for u in range(UNITS):
                    if u == 1 and not after:
                        continue
                    if after or u > 2:
                        gated_lo(UNITS * b + u - 1, UNITS + u - 1)
                    gated_unit(b, u)
                    if u == 0 and not after:
                        down_weights_lo(2)
                        gated_lo(0, 0)
                        gated_unit(b, 1)
                        gated_lo(1, 1)
                        route()
                    if 2 <= u < E6 + 2:
                        add_expert(b, u - 2, after or u > 2)
                    if u == 1 and after:
                        add_shared(b - 1)

            def add_shared(b):
                v.wait_ge(ed_mm, UNITS * b + UNITS)
                v.wait_ge(ey_ok, E6 * b + E6)
                for t in range(TB):
                    xt = X[:, ds(TB * b + t, 1), :].rearrange("p o d -> p (o d)")
                    ins = nc.vector.scalar_tensor_tensor(out=xt, in0=ES[t][:, 0:D], scalar=0.5, in1=xt,
                                                         op0=ALU.mult, op1=ALU.add)
                ins.then_inc(x_done, 1)

            for n in range(2):
                down_weights_lo(n)
            moe_batch(0, False)
            with nc.vector.Fori(1, B) as b, link.over(b, 1, B, UNITS):
                moe_batch(b, True)
            gated_lo(UNITS * B - 1, UNITS - 1)
            add_shared(B - 1)

        @block.scalar
        def _(act):
            def ln_columns(s, b, src):
                act.wait_ge(ln_tr, ln_before(s, b) + 1)
                nc.scalar.copy(HT[:, :, ds(S * b, S)], src[:, :].rearrange("p (k t) -> p k t", k=KT)).then_inc(ln_ht, 1)

            def weights_hi(h, j, after, src=w_new):
                act.wait_ge(ld_w, 16 * h + 16)
                if after:
                    act.wait_ge(pj_mm, NT * h - NT)
                nc.scalar.copy(W_hi[:, j].rearrange("p k c -> p (k c)"), src).then_inc(w_hi, 1)

            for b in range(B):
                if b == 1:
                    weights_hi(0, 0, False, w_first)
                if b == 2:
                    act.wait_ge(ld_cx, 16 * 7)
                    for n in range(2):
                        act.wait_ge(kvt_mm, n + 1)
                        nc.scalar.activation(kvT[:, 512 * n:512 * n + 512], bank[n][0:XC, :], ACT.Identity,
                                             bias=bk_col[:, :]).then_inc(kvt_ok, 1)
                ln_columns(0, b, bank[6 + b % 2])
                act.wait_ge(ln_ht, b + 1)
                nc.scalar.copy(H_hi[:, :, b * S:b * S + S], HT[:, :, b * S:b * S + S]).then_inc(h_hi, 1)

            def squares(h, j, t, after):
                if after or t:
                    act.wait_ge(sq_ok, NT * h + t)
                act.wait_ge(qkv_ok, NT * h + t + 1)
                for n in range(2):
                    ins = nc.scalar.activation(sq_out[:, n, :], qk_tok[:, t % 4, n * D0:n * D0 + D0], ACT.Square,
                                               accum_out=sumsq[:, j, n, t:t + 1])
                ins.then_inc(sq_ok, 1)

            def columns(h, n):
                act.wait_ge(tq_mm, 4 * h + n + 1)
                nc.scalar.copy(qkT[:, :, n * S:n * S + S], TQ).then_inc(tq_ok, 1)

            def head_out(g):
                for n in range(2):
                    act.wait_ge(tr_mm, 2 * g + n + 1)
                    nc.scalar.copy(outT[:, ds(g, 1), 512 * n:512 * n + 512].rearrange("p o t -> p (o t)"),
                                   OV[n][:, :, :].rearrange("p t d -> p (t d)")).then_inc(outT_ok, 1)

            def head_columns(h, j, after, more):
                for t in range(NT):
                    act.wait_ge(pj_mm, NT * h + t + 1)
                    if after or t >= 2:
                        act.wait_ge(pj_read, NT * h + t - 1)
                    nc.scalar.activation(tanh_g[:, t % 2], PJ[t % 3][:, 3 * D0:4 * D0], ACT.Tanh,
                                         scale=0.5).then_inc(tanh_done, 1)
                    if t:
                        squares(h, j, t - 1, after)
                    if t in (3, 5, 7):
                        columns(h, (t - 3) // 2)
                    if after and t == 0:
                        columns(h - 1, 3)
                    if more and t == 1:
                        weights_hi(h + 1, 1 - j, after)
                    if after > 1 and t == 4:
                        head_out(h - 2)
                squares(h, j, NT - 1, after)

            head_columns(0, 0, 0, True)
            for n in range(2):
                act.wait_ge(lat_mm, n + 1)
                nc.scalar.copy(latT[:, 512 * n:512 * n + 512], bank[4 + n][:, :]).then_inc(latT_ok, 1)
            z, m, u, w, lw, c = [bt[:, n, :] for n in range(6)]
            act.wait_ge(bt_abs, 1)
            nc.scalar.activation(u, c, ACT.Exp, scale=-1.0).then_inc(bt_exp, 1)
            act.wait_ge(bt_w, 1)
            nc.scalar.activation(lw, w, ACT.Ln).then_inc(bt_ln, 1)

            head_columns(1, 1, 1, True)
            with nc.scalar.Fori(1, H0 // 2 - 1) as i:
                for j in range(2):
                    head_columns(2 * i + j, j, 2, True)
            head_columns(H0 - 2, 0, 2, True)
            head_columns(H0 - 1, 1, 2, False)
            columns(H0 - 1, 3)
            head_out(H0 - 2)
            head_out(H0 - 1)

            def context_out(b):
                act.wait_ge(xo_mm, b + 1)
                nc.scalar.activation(x_oT[:, b % 2, :], XO[0:XC, 0:S], ACT.Copy, scale=X0_SCALE).then_inc(xo_ok, 1)

            def context_exp(b):
                n = b % 2
                act.wait_ge(xs_nm, b + 1)
                for t in range(TB):
                    ins = nc.scalar.activation(x_e[:, n, t, :], x_sim[:, n, t, :], ACT.Exp, bias=x_nm[:, n, t:t + 1],
                                               accum_out=x_sum[:, n, t:t + 1])
                ins.then_inc(xs_exp, 1)

            def hidden(b):
                act.wait_ge(fh_mm, b + 1)
                for m in range(KT):
                    ins = nc.scalar.activation(f_h[:, m, :], FH[:, m, :], ACT.Relu, bias=f_b1[:, m:m + 1])
                ins.then_inc(fh_ok, 1)
                for n in range(2):
                    act.wait_ge(fx_mm, 2 * b + n + 1)
                    nc.scalar.copy(f_vx[:, 2 * n:2 * n + 2, :], FX[n]).then_inc(fx_ok, 1)

            def mixture_exp(b):
                act.wait_ge(fl_ex, b + 1)
                nc.scalar.activation(f_al[:, 1], f_al[:, 0], ACT.Exp).then_inc(fl_e, 1)
                act.wait_ge(fa_tr, b + 1)
                nc.scalar.copy(f_aT, FT).then_inc(fa_T, 1)

            def keep_G(n):
                act.wait_ge(wp_mm, 2 * n + 1)
                nc.scalar.copy(Gw[:, n // 2, 8 * (n % 2):8 * (n % 2) + 8, :], WP[0:QH, :].rearrange("p (h c) -> p h c", h=8)).then_inc(wp_ok, 1)

            def keep_M(n):
                act.wait_ge(wp_mm, 2 * n + 2)
                nc.scalar.copy(Mw[:, 2 * n:2 * n + 2, :], WP[:, :].rearrange("p (m d) -> p m d", m=2)).then_inc(wp_ok, 1)

            for b in range(B):
                ln_columns(1, b, bank[6 + b % 2])
                if b in (1, 2):
                    context_out(b - 1)
                if b >= 2:
                    context_exp(b - 2)

            for n in range(1, B + 2):
                if n + 1 < B:
                    context_out(n + 1)
                if n >= 2:
                    hidden(n - 2)
                if n >= 3:
                    ln_columns(3, n - 3, bank[7])
                if n >= 2:
                    mixture_exp(n - 2)
                if n <= B:
                    keep_G(n - 1)
                    ln_columns(2, n - 1, bank[7])
                    keep_M(n - 1)
                if n + 1 < B:
                    context_exp(n + 1)
            def next_columns(b, kind, after):
                act.wait_ge(a_mm, 3 * b + kind + 1)
                if kind == 0:
                    if after:
                        act.wait_ge(a_now, 2 * b)
                    for m in range(KT):
                        ins = nc.scalar.activation(a_qn[:, m, :], AB[:, m, :], ACT.Identity, bias=a_bs[:, m:m + 1],
                                                   scale=D1 ** -0.5)
                elif kind == 1:
                    for o in range(2):
                        for m in range(KT):
                            ins = nc.scalar.activation(a_kn[:, o, m, :], AB[:, m, :], ACT.Identity,
                                                       bias=a_bs[:, 2 + 2 * o + m:3 + 2 * o + m], scale=a_par[:, o:o + 1])
                else:
                    for m in range(KT):
                        ins = nc.scalar.activation(a_vT[:, m, :], AB[:, m, :], ACT.Identity, bias=a_b[:, 4 + m:5 + m])
                ins.then_inc(a_ok, 1)

            act.wait_ge(a_bias, 1)
            for kind in range(3):
                next_columns(0, kind, False)
            ln_columns(3, B - 1, bank[7])

            def next_queries(b):
                act.wait_ge(a_ok, 3 * b + 1)
                nc.scalar.copy(a_q, a_qn).then_inc(a_now, 1)

            def context_columns(b, m):
                act.wait_ge(ac_mm, KT * b + m + 1)
                nc.scalar.copy(a_cT[:, m, :], AC[m][:, 0:S]).then_inc(ac_T, 1)

            def head_exps(b, between, more):
                for n in range(H1 + 2):
                    if n == 0 and between:
                        context_columns(b - 1, 1)
                    if more and n in NEXT_AT[0:3]:
                        next_columns(b + 1, NEXT_AT.index(n), True)
                    if n < H1:
                        act.wait_ge(as_nm, H1 * b + n + 1)
                        for t in range(TB):
                            ins = nc.scalar.activation(a_p[:, n % 3, t, :], AS[n % 3][:, t, :], ACT.Exp,
                                                       bias=a_nm[:, n % 3, t:t + 1], accum_out=a_sum[:, n % 3, t:t + 1])
                        ins.then_inc(as_exp, 1)
                    if n == H1 - 1 and more:
                        next_queries(b + 1)
                    if n >= 2 and n % 2 == 0:
                        act.wait_ge(at_mm, H1 * b + n - 1)
                        nc.scalar.copy(a_pT[:, 0], AT[0]).then_inc(at_ev, 1)
                    if n == HM + 3:
                        context_columns(b, 0)
                    if n == LN_AT + 3 and between:
                        ln_columns(4, b - 1, bank[1])

            next_queries(0)
            head_exps(0, False, True)
            with nc.scalar.Fori(1, B - 1) as b:
                head_exps(b, True, True)
            head_exps(B - 1, True, False)
            context_columns(B - 1, 1)

            def query_keys(p, q, c):
                act.wait_ge(l_q_mm, 4 * p + q + 1)
                nc.scalar.copy(l_q[:, 512 * c:512 * c + 512], bank[c][:, :]).then_inc(l_q_ok, 1)

            def query_latents(p, r, use):
                j, c = r // 2, r % 2
                act.wait_ge(lu_mm, 4 * p + r + 1)
                if use:
                    act.wait_ge(ls_mm, 8 * p - 8 + 2 * (2 * c + 1) + j + 1)
                nc.scalar.copy(l_u[:, j, 512 * c:512 * c + 512], LU[:, :]).then_inc(lu_hi, 1)

            def attended(p, u, n):
                b = n // 2
                act.wait_ge(lv_mm, u + 1)
                nc.scalar.copy(l_cT[:, ds(p - 1, 1), b * S:b * S + S].rearrange("p o t -> p (o t)"), LC[:, b % 2, :]).then_inc(lc_ok, 1)

            def unit_exp(u, n):
                act.wait_ge(ls_nm, u + 1)
                for t in range(TB):
                    ins = nc.scalar.activation(l_p[:, n % 2, t, :], LS[:, t, :], ACT.Exp, bias=l_nm[:, n % 2, t:t + 1],
                                               accum_out=l_sum[:, n % 2, t:t + 1])
                ins.then_inc(ls_exp, 1)

            def pair_columns(p, make, use):
                for k in range(10):
                    if use and k >= 2:
                        act.wait_ge(lt_mm, 8 * p - 8 + k - 1)
                        nc.scalar.copy(l_pT, LT).then_inc(lt_ok, 1)
                    if use and k > 2 and k % 2 == 0:
                        attended(p, 8 * p - 8 + k - 3, k - 3)
                    if use and 2 <= k < 8:
                        unit_exp(8 * p - 8 + k, k)
                    for r in range(4):
                        if make and k == KEY_AT[r] and (use or r):
                            query_keys(p, r, r % 2)
                        if make and r < 3 and k == LAT_AT[r]:
                            query_latents(p, r, use)
                    if use and k < 2:
                        unit_exp(8 * p - 8 + k, k)
                    if use and k == LAST_AT:
                        query_latents(p - 1, 3, False)
                if use:
                    attended(p, 8 * p - 1, 7)

            query_keys(0, 0, 0)
            ln_columns(4, B - 1, bank[1])
            act.wait_ge(ao_mm, B)
            nc.scalar.copy(lat_hi[:, :], latT[:, :]).then_inc(lat_r, 1)
            pair_columns(0, True, False)
            with nc.scalar.Fori(1, H2 // 2) as p:
                pair_columns(p, True, True)
            pair_columns(H2 // 2, False, True)

            def unit_hi(b, u):
                act.wait_ge(eg_mm, UNITS * b + u - 1)
                nc.scalar.copy(U_hi[:, u % 2], unit_weights(u)).then_inc(u_hi, 1)

            def down_weights_hi(n):
                nc.scalar.copy(down_hi[:, 4 * n:4 * n + 4], down_weights(n)).then_inc(d_hi, 1)

            def gated_hi(U, n, after):
                act.wait_ge(eg_ok, U + 1)
                if after:
                    act.wait_ge(ed_mm, U - 2)
                nc.scalar.copy(act_hi[:, n % 3], e_act[:, n % 2]).then_inc(ea_hi, 1)

            for b in range(B):
                if b == B - 1:
                    act.wait_ge(lf_mm, NT)
                    for n in range(UNITS // 4):
                        down_weights_hi(n)
                ln_columns(5, b, bank[6 + b % 2])
                act.wait_ge(ln_ht, 5 * B + b + 1)
                nc.scalar.copy(E_hi[:, :, b * S:b * S + S], HT[:, :, b * S:b * S + S]).then_inc(e_hi, 1)
                if b == 1:
                    act.wait_ge(ld_6, 16 * 4)
                    for u in range(2):
                        nc.scalar.copy(U_hi[:, u], unit_weights(u)).then_inc(u_hi, 1)

            def moe_tanh(b, first, more):
                for u in range(UNITS):
                    if u + 1 < UNITS and u + 1 >= first:
                        unit_hi(b, u + 1)
                    if u + 1 == UNITS and more:
                        unit_hi(b + 1, 0)
                    if first == 1 or u not in (0, 2):
                        gated_hi(UNITS * b + u - 1, UNITS + u - 1, u >= 4 or first == 1)
                    act.wait_ge(eg_mm, UNITS * b + u + 1)
                    nc.scalar.activation(e_th[:, u % 2, :], EG[u % 2][:, 0, :], ACT.Tanh, scale=0.5).then_inc(eg_th, 1)
                    if u == 1 and first > 1:
                        gated_hi(1, 1, False)
                        act.wait_ge(er_sub, 1)
                        nc.scalar.activation(e_r[:, 1], e_r[:, 0], ACT.Exp).then_inc(er_exp, 1)

            moe_tanh(0, 2, True)
            with nc.scalar.Fori(1, B - 1) as b:
                moe_tanh(b, 1, True)
            moe_tanh(B - 1, 1, False)
            gated_hi(UNITS * B - 1, UNITS - 1, True)

        @block.tensor
        def _(pe):
            mm = nc.tensor.matmul

            def ln_turn(s, b, dst, place=None, behind=1):
                if s or b >= 2:
                    pe.wait_ge(ln_ht, ln_before(s, b) - behind)
                pe.wait_ge(ln_h, ln_before(s, b) + 1)
                for t in range(TB):
                    for k in range(KT):
                        ins = nc.tensor.transpose(dst[:, k * S + t * P:k * S + t * P + P],
                                                  HN[:, (TB * b if place is None else place) + t, k * P:k * P + P],
                                                  ident[:, :])
                ins.then_inc(ln_tr, 1)

            pe.wait_ge(ld_c, 16)
            for b in range(B):
                ln_turn(0, b, bank[6 + b % 2])
                if b == 1:
                    pe.wait_ge(ld_cx, 16 * 7)
                    for n in range(2):
                        mm(bank[n][0:XC, :], wk_T[:, :], ctxT[:, 512 * n:512 * n + 512], start=True, stop=True).then_inc(kvt_mm, 1)
                    for t in range(NT):
                        ins = mm(bank[3][:, t * XC:t * XC + XC], ctxT[:, t * P:t * P + P], wk_T[:, :], start=True, stop=True)
                    ins.then_inc(kvn_mm, 1)
            pe.wait_ge(kvt_ok, 2)
            pe.wait_ge(kvn_ok, 1)
            pe.wait_ge(ln_ht, B)
            def project_tile(h, j, t, after):
                if t == 0:
                    pe.wait_ge(w_lo, h + 1)
                if not after and t % TB == 0:
                    pe.wait_ge(h_lo, t // TB + 1)
                if t >= 3 or after:
                    pe.wait_ge(pj_read, NT * h + (t - 3 if t >= 3 else (-2, -1, -3)[t]) + 1)
                cols = slice(t * P, t * P + P)
                for k in range(KT):
                    for m, (x_part, w_part) in enumerate(((H_hi, W_hi), (H_hi, W_lo), (H_lo, W_hi))):
                        ins = mm(PJ[t % 3][:, :], x_part[:, k, cols], w_part[:, j, k, :],
                                 start=(k == 0 and m == 0), stop=(k == KT - 1 and m == 2))
                ins.then_inc(pj_mm, 1)

            def turn_queries(h, n, after):
                if after or n:
                    pe.wait_ge(tq_ok, 4 * h + n)
                pe.wait_ge(qkv_ok, NT * h + 2 * n + 2)
                for c in range(2):
                    for t in range(2):
                        ins = nc.tensor.transpose(TQ[:, c, t * P:t * P + P], qk_tok[:, (2 * n + t) % 4, c * D0:c * D0 + D0], ident[:, :])
                ins.then_inc(tq_mm, 1)

            def scores(g, after):
                pe.wait_ge(tq_ok, 4 * g + 4)
                if not after:
                    pe.wait_ge(latT_ok, 2)
                for n in range(2):
                    if after:
                        pe.wait_ge(masked, 2 * g + n - 1)
                    for t in range(4 * n, 4 * n + 4):
                        ins = mm(SC[n][:, t % 4, :], qkT[:, 1, t * P:t * P + P], qkT[:, 0, t * P:t * P + P],
                                 start=True, stop=True)
                    ins.then_inc(sc_mm, 1)

            def values(g, j, n, after):
                if after:
                    pe.wait_ge(outT_ok, 2 * g + n - 1)
                else:
                    pe.wait_ge(bt_abs, 1)
                pe.wait_ge(masked, 2 * g + n + 1)
                for t in range(4 * n, 4 * n + 4):
                    ins = mm(OV[n][:, t % 4, :], attn[:, t, :], v_tok[:, j, t, :], start=True, stop=True)
                ins.then_inc(pv_mm, 1)

            def turn_head(g, n):
                pe.wait_ge(gated_ok, 2 * g + n + 1)
                for t in range(4 * n, 4 * n + 4):
                    ins = nc.tensor.transpose(OV[n][:, t % 4, :], gated[:, t, :], ident[:, :])
                ins.then_inc(tr_mm, 1)

            def head(h, j, after):
                for t in range(NT):
                    project_tile(h, j, t, after)
                    if after:
                        if t == 0:
                            turn_queries(h - 1, 3, after)
                        if t == 1:
                            scores(h - 1, after > 1)
                        if t in (5, 6):
                            values(h - 1, 1 - j, t - 5, after > 1)
                        if t in (2, 3) and after > 1:
                            turn_head(h - 2, t - 2)
                    if t in (2, 4, 6):
                        turn_queries(h, t // 2 - 1, after)

            pe.wait_ge(consts, 1)
            head(0, 0, 0)
            pe.wait_ge(lat_ok, 1)
            for t in range(NT):
                ins = nc.tensor.transpose(bank[4 + t // 4][:, t % 4 * P:t % 4 * P + P], lat2[:, t, :], ident[:, :])
                if t % 4 == 3:
                    ins.then_inc(lat_mm, 1)
            pe.wait_ge(ld_1, 16 * 4)
            for t in range(NT):
                for k in range(KT):
                    ins = mm(PRB[:, t * H0:t * H0 + H0], HT[:, k, t * P:t * P + P], b_w[:, k, :],
                             start=(k == 0), stop=(k == KT - 1))
            ins.then_inc(bt_mm, 1)

            head(1, 1, 1)
            with nc.tensor.Fori(1, H0 // 2) as i:
                for j in range(2):
                    head(2 * i + j, j, 2)
            turn_queries(H0 - 1, 3, True)
            scores(H0 - 1, True)
            for n in range(2):
                turn_head(H0 - 2, n)
            for n in range(2):
                values(H0 - 1, 1, n, True)
            for n in range(2):
                turn_head(H0 - 1, n)

            def context_product(b):
                pe.wait_ge(ln_ht, B + b + 1)
                if b:
                    pe.wait_ge(xo_ok, b)
                for k in range(KT):
                    ins = mm(XO[0:XC, 0:S], kv[:, TB * b + k, :], HT[:, k, b * S:b * S + S],
                             start=(k == 0), stop=(k == KT - 1))
                ins.then_inc(xo_mm, 1)

            def context_similarity(b):
                pe.wait_ge(xo_ok, b + 1)
                if b:
                    pe.wait_ge(xs_free, b)
                for t in range(TB):
                    ins = mm(XS[:, t, :], x_oT[:, b % 2, t * P:t * P + P], kvT[:, b * S:b * S + S],
                             start=True, stop=True)
                ins.then_inc(xs_mm, 1)

            pe.wait_ge(pj_read, NT * H0)
            pe.wait_ge(ld_o, 16)
            pe.wait_ge(outT_ok, 2 * H0)
            for t in range(NT):
                if t >= 2:
                    pe.wait_ge(o_read, t - 1)
                for h in range(H0):
                    ins = mm(bank[t % 2][:, 0:D], outT[:, h, t * P:t * P + P], o_w[:, h, :],
                             start=(h == 0), stop=(h == H0 - 1))
                ins.then_inc(o_mm, 1)
                if t % TB == 0 and t:
                    ln_turn(1, t // TB - 1, bank[6 + (t // TB - 1) % 2])
                    if t // TB >= 2:
                        context_product(t // TB - 2)
                        context_similarity(t // TB - 2)
            ln_turn(1, B - 1, bank[7])

            def ffn_hidden(b):
                pe.wait_ge(ln_ht, ln_before(2, b) + 1)
                if b:
                    pe.wait_ge(fh_ok, b)
                for m in range(KT):
                    for k in range(KT):
                        ins = mm(FH[:, m, :], f_w1[:, k, m * P:m * P + P], HT[:, k, b * S:b * S + S],
                                 start=(k == 0), stop=(k == KT - 1))
                ins.then_inc(fh_mm, 1)

            def ffn_ranks(b, n):
                if b:
                    pe.wait_ge(fa_ok, 2 * b - 1 + n)
                for m in range(2):
                    for k in range(KT):
                        ins = mm(FX[n][:, m, :], f_v[:, k, (2 * n + m) * P:(2 * n + m + 1) * P], HT[:, k, b * S:b * S + S],
                                 start=(k == 0), stop=(k == KT - 1))
                ins.then_inc(fx_mm, 1)

            def ffn_logits(b):
                pe.wait_ge(fh_ok, b + 1)
                if b:
                    pe.wait_ge(fa_T, b)
                for t in range(TB):
                    for k in range(KT):
                        ins = mm(FL[:, t, :], f_h[:, k, t * P:t * P + P], f_w2[:, k, :], start=(k == 0), stop=(k == KT - 1))
                ins.then_inc(fl_mm, 1)

            def ffn_alpha(b):
                pe.wait_ge(fl_al, b + 1)
                for t in range(TB):
                    ins = nc.tensor.transpose(FT[:, t * P:t * P + P], f_al[:, 2, t, :], ident[:, :])
                ins.then_inc(fa_tr, 1)

            def ffn_spread(b):
                pe.wait_ge(fa_T, b + 1)
                pe.wait_ge(fx_ok, 2 * b + 2)
                for m in range(FM):
                    ins = mm(FA[m // 2][:, m % 2, :], f_sel[:, m, :], f_aT, start=True, stop=True)
                    if m % 2:
                        ins.then_inc(fa_mm, 1)

            def ffn_out(b):
                pe.wait_ge(fa_ok, 2 * b + 2)
                if b:
                    pe.wait_ge(fo_read, b)
                else:
                    pe.wait_ge(xo_ok, B)
                for t in range(TB):
                    for m in range(FM):
                        ins = mm(FO[:, t, :], f_ax[:, m, t * P:t * P + P], f_u[:, m, :], start=(m == 0), stop=(m == FM - 1))
                ins.then_inc(fo_mm, 1)

            def product_G(n):
                if n:
                    pe.wait_ge(wp_ok, 2 * n)
                for h in range(8 * (n % 2), 8 * (n % 2) + 8):
                    ins = mm(WP[0:QH, (h % 8) * XC:(h % 8 + 1) * XC], qr_T[:, h, n // 2 * QH:n // 2 * QH + QH], kr_T[:, h, :],
                             start=True, stop=True)
                ins.then_inc(wp_mm, 1)

            def product_M(n):
                if n == 0:
                    pe.wait_ge(ld_p, 16 * 2)
                pe.wait_ge(wp_ok, 2 * n + 1)
                for m in range(2 * n, 2 * n + 2):
                    for j in range(2):
                        ins = mm(WP[j * XC:j * XC + XC, (m % 2) * D:(m % 2) * D + D], kc_kv[:, 2 * m + j, :], wo_T[:, 2 * m + j, :],
                                 start=True, stop=True)
                ins.then_inc(wp_mm, 1)

            def project(b, kind):
                if kind:
                    pe.wait_ge(a_ok, 3 * b + kind)
                if kind < 3:
                    for m in range(KT):
                        for k in range(KT):
                            ins = mm(AB[:, m, :], a_w[:, k, kind * D + m * P:kind * D + m * P + P], HT[:, k, ds(b * S, S)],
                                     start=(k == 0), stop=(k == KT - 1))
                    ins.then_inc(a_mm, 1)
                else:
                    for t in range(TB):
                        for m in range(KT):
                            ins = nc.tensor.transpose(bank[1][:, t * D + m * P:t * D + m * P + P], a_vT[:, m, t * P:t * P + P], ident[:, :])
                    ins.then_inc(av_tr, 1)

            pe.wait_ge(ln_ht, 2 * B)
            pe.wait_ge(o_read, NT)
            pe.wait_ge(ld_3, 16 * 7)
            for n in range(1, B + 2):
                b = n - 2
                if n + 1 < B:
                    context_product(n + 1)
                    context_similarity(n + 1)
                if b >= 0:
                    ffn_hidden(b)
                    ffn_ranks(b, 0)
                    ffn_logits(b)
                    ffn_ranks(b, 1)
                if b >= 1:
                    ln_turn(3, b - 1, bank[7], behind=0)
                if b >= 0:
                    ffn_alpha(b)
                if n == 1:
                    pe.wait_ge(ld_g, 16 * 2)
                if n <= B:
                    product_G(n - 1)
                if b >= 0:
                    ffn_spread(b)
                if n <= B:
                    ln_turn(2, n - 1, bank[7], behind=0)
                    product_M(n - 1)
                if b == B - 1:
                    pe.wait_ge(ld_4, 16 * 7)
                    project(0, 0)
                if b >= 0:
                    ffn_out(b)
            for kind in (1, 2):
                project(0, kind)
            ln_turn(3, B - 1, bank[7], behind=0)


            def attend(b, between, more):
                pe.wait_ge(a_now, 2 * b + 2)
                for n in range(H1 + 3):
                    if more and n in NEXT_AT:
                        if n == NEXT_AT[0]:
                            pe.wait_ge(av_ok, b + 1)
                            pe.wait_ge(ln_ht, 4 * B + b)
                        project(b + 1, NEXT_AT.index(n))
                    if n < H1:
                        m, g, o = n // 8, n % 8 // 2, n % 2
                        rows = slice(32 * g, 32 * g + 32)
                        if n >= 3:
                            pe.wait_ge(as_exp, H1 * b + n - 2)
                        for t in range(TB):
                            ins = mm(AS[n % 3][:, t, :], a_q[rows, m, t * P:t * P + P], a_k[rows, o, m, :], start=True, stop=True)
                        ins.then_inc(as_mm, 1)
                    if between and n == 2:
                        pe.wait_ge(av_ok, b + 1)
                        project_out(b - 1)
                    if 2 <= n < H1 + 2:
                        q = n - 2
                        pe.wait_ge(ap_ok, H1 * b + q + 1)
                        if q >= 2:
                            (pe.wait_ge(at_ev, H1 // 2 * b + q // 2) if q % 2 == 0 else pe.wait_ge(at_od, H1 // 2 * b + q // 2))
                        for l in range(TB):
                            for t in range(TB):
                                ins = nc.tensor.transpose(AT[q % 2][:, l, t * P:t * P + P], a_p[:, q % 3, t, l * P:l * P + P], ident[:, :])
                        ins.then_inc(at_mm, 1)
                    if n >= 3:
                        q = n - 3
                        (pe.wait_ge(at_ev, H1 // 2 * b + q // 2 + 1) if q % 2 == 0 else pe.wait_ge(at_od, H1 // 2 * b + q // 2 + 1))
                        if q == 0:
                            pe.wait_ge(av_ok, b + 1)
                        for l in range(TB):
                            ins = mm(AC[q // HM][:, 0:S], a_v[:, l, q, :], a_pT[:, q % 2, l, :],
                                     start=(q % HM == 0 and l == 0), stop=(q % HM == HM - 1 and l == TB - 1))
                        if q % HM == HM - 1:
                            ins.then_inc(ac_mm, 1)
                    if n == LN_AT + 3 and between:
                        pe.wait_ge(ao_read, b)
                        ln_turn(4, b - 1, bank[1], 0, 0)

            def project_out(b):
                pe.wait_ge(ac_T, KT * b + KT)
                for t in range(TB):
                    for c in range(KT):
                        ins = mm(AB[:, t, :], a_cT[:, c, t * P:t * P + P], a_ow[:, c, :], start=(c == 0), stop=(c == KT - 1))
                ins.then_inc(ao_mm, 1)

            pe.wait_ge(wp_ok, 8)
            pe.wait_ge(consts, 2)
            project(0, 3)
            attend(0, False, True)
            with nc.tensor.Fori(1, B - 1) as b:
                attend(b, True, True)
            attend(B - 1, True, False)
            project_out(B - 1)

            def head_key(p, q):
                j, c = q // 2, q % 2
                pe.wait_ge(ld_w5[j], 16 * p + 16)
                if j:
                    pe.wait_ge(l_q_ok, 4 * p + c + 1)
                for k in range(KT):
                    ins = mm(bank[c][:, :], w5[:, j, k * K2:k * K2 + K2], HT[:, k, 512 * c:512 * c + 512],
                             start=(k == 0), stop=(k == KT - 1))
                ins.then_inc(l_q_mm, 1)

            def head_rotated(p, r, after):
                j, c = r // 2, r % 2
                pe.wait_ge(l_q_ok, 4 * p + r + 1)
                if after:
                    pe.wait_ge(lb_rot, 8 * p + 2 * r)
                for o in range(2):
                    ins = mm(LR[o][0:QH, :], w5[:, j, 2 * K2 + o * QH:2 * K2 + o * QH + QH], l_q[:, 512 * c:512 * c + 512],
                             start=True, stop=True)
                ins.then_inc(lb_mm, 1)

            def head_query(p, r, after):
                j, c = r // 2, r % 2
                if r == 0:
                    pe.wait_ge(g_ok, p + 1)
                pe.wait_ge(lb_add, 4 * p + r + 1)
                if after:
                    pe.wait_ge(lu_ok, 4 * p + r)
                for o in range(2):
                    ins = mm(LU[:, :], g_now[:, o, j, :, :].rearrange("p n c -> p (n c)"), l_rot[:, o, 512 * c:512 * c + 512],
                             start=(o == 0), stop=(o == 1))
                ins.then_inc(lu_mm, 1)

            def unit_turn(u, n):
                pe.wait_ge(lp_ok, u + 1)
                for l in range(TB):
                    for t in range(TB):
                        ins = nc.tensor.transpose(LT[:, l, t * P:t * P + P], l_p[:, n % 2, t, l * P:l * P + P], ident[:, :])
                ins.then_inc(lt_mm, 1)

            def unit_scores(u, n, after):
                b, j = n // 2, n % 2
                if after:
                    pe.wait_ge(ls_exp, u)
                for t in range(TB):
                    for m, part in enumerate((lat_hi, lat_lo)):
                        ins = mm(LS[:, t, :], l_u[:, j, (TB * b + t) * P:(TB * b + t + 1) * P], part[:, b * S:b * S + S],
                                 start=(m == 0), stop=(m == 1))
                ins.then_inc(ls_mm, 1)

            def unit_values(p, u, n, after):
                b, j = n // 2, n % 2
                pe.wait_ge(lt_ok, u + 1)
                if j == 0 and after:
                    pe.wait_ge(lc_ok, B * p - B + b)
                for l in range(TB):
                    ins = mm(LC[XC * j:XC * j + XC, b % 2, :], lat[:, TB * b + l, :], l_pT[:, l, :], start=(l == 0), stop=(l == TB - 1))
                ins.then_inc(lv_mm, 1)

            def pair(p, make, use, after):
                def make_query(k):
                    for r in range(4):
                        if r == 0 and not use and k <= ROT_AT[0]:
                            continue
                        if k == KEY_AT[r]:
                            head_key(p, r)
                        if k == ROT_AT[r]:
                            head_rotated(p, r, after or r)
                        if r < 3 and k == LAT_AT[r]:
                            head_query(p, r, after or r)

                for k in range(10):
                    u = 8 * p - 8 + k
                    if make and k in (0, 1):
                        make_query(k)
                    if use and k >= 2:
                        unit_turn(u - 2, k - 2)
                    if use and k < 8:
                        if k == 0:
                            if after < 2:
                                pe.wait_ge(lat_r, 2)
                            pe.wait_ge(lu_ok, 4 * p - 1)
                        if k == 5:
                            pe.wait_ge(lu_ok, 4 * p)
                        unit_scores(u, k, k or after > 1)
                    if use and k == LAST_AT:
                        head_query(p - 1, 3, True)
                    if make and 1 < k < 9:
                        make_query(k)
                    if use and k >= 2:
                        unit_values(p, u - 2, k - 2, k > 2 or after > 1)

            def expert_up(b, u, after):
                U = UNITS * b + u
                if after or u >= 2:
                    pe.wait_ge(eg_ok, U - 1)
                pe.wait_ge(u_lo, U + 1)
                if u == 0:
                    pe.wait_ge(e_lo, b + 1)
                for gu in range(2):
                    for k in range(KT):
                        for m, (w_part, x_part) in enumerate(((U_hi, E_hi), (U_hi, E_lo), (U_lo, E_hi))):
                            ins = mm(EG[u % 2][:, gu, :], w_part[:, u % 2, k, gu, :], x_part[:, k, ds(b * S, S)],
                                     start=(k == 0 and m == 0), stop=(k == KT - 1 and m == 2))
                ins.then_inc(eg_mm, 1)

            pe.wait_ge(as_exp, H1 * B)
            head_key(0, 0)
            head_rotated(0, 0, 0)
            pe.wait_ge(ao_read, B)
            ln_turn(4, B - 1, bank[1], 0, 0)
            pe.wait_ge(ln_ht, 5 * B)
            pair(0, True, False, 0)
            pair(1, True, True, 1)
            with nc.tensor.Fori(2, H2 // 2) as p:
                pair(p, True, True, 2)
            pair(H2 // 2, False, True, 2)
            pe.wait_ge(lc_ok, B * (H2 // 2))
            for t in range(NT):
                if t >= 2:
                    pe.wait_ge(lf_read, t - 1)
                for m in range(H2 // 2):
                    ins = mm(bank[2 + t % 2][:, 0:D], l_cT[:, m, t * P:t * P + P], Mw[:, m, :], start=(m == 0), stop=(m == H2 // 2 - 1))
                ins.then_inc(lf_mm, 1)
                if t >= 3 and t % 2:
                    b = t // 2 - 1
                    ln_turn(5, b, bank[6 + b % 2])
            expert_up(0, 0, False)
            expert_up(0, 1, False)
            ln_turn(5, 3, bank[7])

            def expert_down(b, u, after):
                pe.wait_ge(ea_lo, UNITS * b + u + 1)
                if not after:
                    pe.wait_ge(d_lo, u // 4 + 1)
                if u < E6:
                    if after or u >= 2:
                        pe.wait_ge(ey_ok, E6 * b + u - 1)
                elif u == E6 and after:
                    pe.wait_ge(x_done, b)
                for t in range(TB):
                    dst = EY[u % 2][:, t, :] if u < E6 else ES[t][:, 0:D]
                    for m, (a_part, w_part) in enumerate(((act_hi, down_hi), (act_hi, down_lo), (act_lo, down_hi))):
                        ins = mm(dst, a_part[:, u % 3, t * P:t * P + P], w_part[:, u, :],
                                 start=(m == 0 and u <= E6), stop=(m == 2 and (u < E6 or u == UNITS - 1)))
                ins.then_inc(ed_mm, 1)

            def moe(b, after, made=0):
                for u in range(made, UNITS):
                    expert_up(b, u, after)
                    if u >= 2:
                        expert_down(b, u - 2, after)
                    elif after:
                        expert_down(b - 1, UNITS + u - 2, True)

            pe.wait_ge(ln_ht, 6 * B)
            pe.wait_ge(lf_read, NT)
            for t in range(NT):
                for k in range(KT):
                    ins = mm(EL[:, t, :], HT[:, k, t * P:t * P + P], e_gate[:, k, :], start=(k == 0), stop=(k == KT - 1))
            ins.then_inc(er_mm, 1)
            moe(0, False, 2)
            with nc.tensor.Fori(1, B) as b:
                moe(b, True)
            for u in (UNITS - 2, UNITS - 1):
                expert_down(B - 1, u, True)


def kernel(**inputs):
    import numpy as np
    import concourse.bacc as bacc
    from concourse.bass_utils import run_bass_kernel_spmd

    g = {k: np.asarray(v) for k, v in inputs.items()}
    arrays = lay_out(np, g)
    arrays.update(constants(np))
    nc = bacc.Bacc("TRN2", target_bir_lowering=False, num_devices=1)
    feeds, args = {}, {}
    for name, value in arrays.items():
        value = np.ascontiguousarray(value)
        feeds[f"in_{name}"] = value
        args[name] = nc.dram_tensor(f"in_{name}", value.shape, mybir.dt.from_np(value.dtype), kind="ExternalInput").ap()
    out = nc.dram_tensor("out_x", (B, S, D), F32, kind="ExternalOutput").ap()
    decoder(nc, args, out)
    return run_bass_kernel_spmd(nc, [feeds], core_ids=[0]).results[0]["out_x"]
```
